# Optimizing a Trainium2 kernel written in Bass

```python
import numpy as np
import jax
import jax.numpy as jnp

def _softmax(x, axis=-1):
    return jax.nn.softmax(x, axis=axis)

def _gelu(x):
    return jax.nn.gelu(x, approximate=True)

def _silu(x):
    return jax.nn.silu(x)

def _sigmoid(x):
    return jax.nn.sigmoid(x)

def _layernorm(x, axis=-1, eps=1e-05):
    m = jnp.mean(x, axis=axis, keepdims=True)
    v = jnp.var(x, axis=axis, keepdims=True)
    return (x - m) / jnp.sqrt(v + eps)

def _scatter_add(tgt, idx, src, axis=0):
    return tgt.at[idx].add(src)

def _segment_sum(src, seg, n):
    return jax.ops.segment_sum(src, seg, n)
kernel_name = 'mk_xattn_ffn_d2_seqx_r8_610171'

def setup_inputs(seed: int=0):
    np.random.seed(seed)
    _w = jnp.asarray

    def _rec_inputs():
        import jax
        import jax.numpy as jnp
        _rk = jax.random.key(seed)
        x = -0.0002928 + 1 * jax.random.normal(jax.random.fold_in(_rk, 1), (16, 128, 256), jnp.float32)
        _lenS = 128 - jax.random.randint(jax.random.fold_in(_rk, 7), (16,), 0, max(1, 128 // 4) + 1, jnp.int32)
        _lenS2 = 128 - jax.random.randint(jax.random.fold_in(_rk, 8), (16,), 0, max(1, 128 // 4) + 1, jnp.int32)
        fside_S2_0 = -0.00337071 + 1.01897 * jax.random.normal(jax.random.fold_in(_rk, 11), (128,), jnp.float32)
        _ctx_2048P = jax.random.normal(jax.random.fold_in(_rk, 12), (16, 16, 256), jnp.float32)
        _ctx_2048c = jax.random.dirichlet(jax.random.fold_in(_rk, 512), 0.3 * jnp.ones((16,), jnp.float32), (16, 128))
        _ctx_2048t = jnp.einsum('bsk,bkd->bsd', _ctx_2048c, _ctx_2048P)
        _ctx_2048t = _ctx_2048t * jax.lax.rsqrt(jnp.mean(jnp.square(_ctx_2048t)) + 1e-12) * 0.953939
        ctx_2048 = 0.000675642 + 1.00031 * (_ctx_2048t + 0.3 * jax.random.normal(jax.random.fold_in(_rk, 612), (16, 128, 256), jnp.float32))
        return (x, fside_S2_0, ctx_2048)
    x, fside_S2_0, ctx_2048 = _rec_inputs()

    def _L0_xattn_setup():
        import jax, jax.numpy as jnp
        import numpy as np
        key = jax.random.key(seed)
        ks = jax.random.split(key, 5)
        B, D, L, NH = (2, 128, 256, 8)
        H = D // NH
        return {'v': jax.random.normal(ks[0], (B, D, L), jnp.float32), 'k': jax.random.normal(ks[1], (H, L), jnp.float32) * 0.1, 'bias': jax.random.normal(ks[2], (D,), jnp.float32), 'x1': jax.random.normal(ks[3], (B, D, L), jnp.float32), 'x2': jax.random.normal(ks[4], (B, D, L), jnp.float32), 'num_heads': NH}
    _L0_xattn_all = _L0_xattn_setup()
    _L0_xattn_in = {k: v for k, v in _L0_xattn_all.items() if k in ('k',)}
    del _L0_xattn_all

    def _L0_ffn_setup():
        import jax, jax.numpy as jnp
        import numpy as np
        H = 256
        I = 176
        E = 16
        K = 2
        SI = I * 2

        def _swiglu(gu, inter):
            g, u = (gu[..., :inter], gu[..., inter:])
            return jax.nn.silu(g) * u
        key = jax.random.key(seed)
        ks = jax.random.split(key, 6)
        s = 0.02
        hidden_states = jax.random.normal(ks[0], (1, 128, H), dtype=jnp.float32)
        gate_w = jax.random.normal(ks[1], (E, H), dtype=jnp.float32) * s
        w_gate_up = jax.random.normal(ks[2], (E, H, 2 * I), dtype=jnp.float32) * s
        w_down = jax.random.normal(ks[3], (E, I, H), dtype=jnp.float32) * s
        shared_gate_up = jax.random.normal(ks[4], (H, 2 * SI), dtype=jnp.float32) * s
        shared_down = jax.random.normal(ks[5], (SI, H), dtype=jnp.float32) * s
        return {'hidden_states': hidden_states, 'gate_w': gate_w, 'w_gate_up': w_gate_up, 'w_down': w_down, 'shared_gate_up': shared_gate_up, 'shared_down': shared_down}
    _L0_ffn_all = _L0_ffn_setup()
    _L0_ffn_in = {k: v for k, v in _L0_ffn_all.items() if k in ('gate_w', 'w_gate_up', 'w_down', 'shared_gate_up', 'shared_down')}
    del _L0_ffn_all

    def _L1_xattn_setup():
        import jax, jax.numpy as jnp
        import numpy as np
        key = jax.random.key(seed)
        k1, k2, k3, k4, k5 = jax.random.split(key, 5)
        B, D_MODEL, L = (2, 128, 256)
        HEAD_DIM = 8
        H = D_MODEL // HEAD_DIM
        return {'k': jax.random.normal(k1, (B, D_MODEL, L), dtype=jnp.float32), 'v': jax.random.normal(k2, (B, D_MODEL, L), dtype=jnp.float32), 'q': jax.random.normal(k3, (B, D_MODEL, L), dtype=jnp.float32), 'ssm_kernel': jax.random.normal(k4, (H, L), dtype=jnp.float32), 'D': jax.random.normal(k5, (H,), dtype=jnp.float32), 'head_dim': HEAD_DIM}
    _L1_xattn_all = _L1_xattn_setup()
    _L1_xattn_in = {k: v for k, v in _L1_xattn_all.items() if k in ('ssm_kernel', 'D')}
    del _L1_xattn_all

    def _L1_ffn_setup():
        import jax, jax.numpy as jnp
        import numpy as np
        EPS = 1e-05
        ROPE_BASE = 150000.0
        NHEADS = 32
        KVHEADS = 8
        HEAD_DIM = 64
        TOP_K = 4

        def _rms(x, w):
            return x * jax.lax.rsqrt(jnp.mean(x * x, -1, keepdims=True) + EPS) * w

        def _rope(q, k):
            S, hd = (q.shape[1], q.shape[-1])
            half = hd // 2
            inv = 1.0 / ROPE_BASE ** (jnp.arange(half, dtype=jnp.float32) / half)
            ang = jnp.arange(S, dtype=jnp.float32)[:, None] * inv
            cos = jnp.concatenate([jnp.cos(ang), jnp.cos(ang)], -1)[None, :, None, :]
            sin = jnp.concatenate([jnp.sin(ang), jnp.sin(ang)], -1)[None, :, None, :]

            def rot(t):
                t1, t2 = (t[..., :half], t[..., half:])
                return jnp.concatenate([-t2, t1], -1)
            return (q * cos + rot(q) * sin, k * cos + rot(k) * sin)
        key = jax.random.key(seed)
        ks = jax.random.split(key, 12)
        B, S, D, H, E = (1, 128, 256, 256, 16)
        s = 0.02
        return {'x': jax.random.normal(ks[0], (B, S, D), jnp.float32), 'ln_w': jnp.ones((D,), jnp.float32), 'ff_ln_w': jnp.ones((D,), jnp.float32), 'wq': jax.random.normal(ks[1], (D, NHEADS * HEAD_DIM), jnp.float32) * s, 'wk': jax.random.normal(ks[2], (D, KVHEADS * HEAD_DIM), jnp.float32) * s, 'wv': jax.random.normal(ks[3], (D, KVHEADS * HEAD_DIM), jnp.float32) * s, 'wo': jax.random.normal(ks[4], (NHEADS * HEAD_DIM, D), jnp.float32) * s, 'wg': jax.random.normal(ks[5], (D, E), jnp.float32) * s, 'w1': jax.random.normal(ks[6], (E, D, H), jnp.float32) * s, 'w3': jax.random.normal(ks[7], (E, D, H), jnp.float32) * s, 'w2': jax.random.normal(ks[8], (E, H, D), jnp.float32) * s}
    _L1_ffn_all = _L1_ffn_setup()
    _L1_ffn_in = {k: v for k, v in _L1_ffn_all.items() if k in ('ln_w', 'ff_ln_w', 'wq', 'wk', 'wv', 'wo', 'wg', 'w1', 'w3', 'w2')}
    del _L1_ffn_all
    return {'x': x, 'fside_S2_0': fside_S2_0, 'ctx_2048': ctx_2048, 'L0_xattn_k': _L0_xattn_in['k'], 'L0_ffn_gate_w': _L0_ffn_in['gate_w'], 'L0_ffn_w_gate_up': _L0_ffn_in['w_gate_up'], 'L0_ffn_w_down': _L0_ffn_in['w_down'], 'L0_ffn_shared_gate_up': _L0_ffn_in['shared_gate_up'], 'L0_ffn_shared_down': _L0_ffn_in['shared_down'], 'L1_xattn_ssm_kernel': _L1_xattn_in['ssm_kernel'], 'L1_xattn_D': _L1_xattn_in['D'], 'L1_ffn_ln_w': _L1_ffn_in['ln_w'], 'L1_ffn_ff_ln_w': _L1_ffn_in['ff_ln_w'], 'L1_ffn_wq': _L1_ffn_in['wq'], 'L1_ffn_wk': _L1_ffn_in['wk'], 'L1_ffn_wv': _L1_ffn_in['wv'], 'L1_ffn_wo': _L1_ffn_in['wo'], 'L1_ffn_wg': _L1_ffn_in['wg'], 'L1_ffn_w1': _L1_ffn_in['w1'], 'L1_ffn_w3': _L1_ffn_in['w3'], 'L1_ffn_w2': _L1_ffn_in['w2']}

def reference(x, fside_S2_0, ctx_2048, L0_xattn_k, L0_ffn_gate_w, L0_ffn_w_gate_up, L0_ffn_w_down, L0_ffn_shared_gate_up, L0_ffn_shared_down, L1_xattn_ssm_kernel, L1_xattn_D, L1_ffn_ln_w, L1_ffn_ff_ln_w, L1_ffn_wq, L1_ffn_wk, L1_ffn_wv, L1_ffn_wo, L1_ffn_wg, L1_ffn_w1, L1_ffn_w3, L1_ffn_w2):
    import jax
    import jax.numpy as jnp

    def _L0_xattn_ref(v, k, bias, x1, x2, num_heads):
        import jax, jax.numpy as jnp
        import numpy as np
        B, D, L = v.shape
        H = D // num_heads
        fft_size = 2 * L
        vr = v.reshape(B, H, num_heads, L)
        x1r = x1.reshape(B, H, num_heads, L)
        x2r = x2.reshape(B, H, num_heads, L)
        kv = vr[:, :, :, None, :] * x2r[:, :, None, :, :]
        k_f = jnp.fft.rfft(k.astype(jnp.float32), n=fft_size)
        y = jnp.fft.irfft(jnp.fft.rfft(kv, n=fft_size) * k_f[None, :, None, None, :], n=fft_size)[..., :L]
        skip = bias.astype(jnp.float32).reshape(H, num_heads)[None, :, :, None, None]
        y = y + kv * skip
        out = jnp.einsum('bhijl,bhil->bhjl', y, x1r)
        return out.reshape(B, D, L)

    def _L0_ffn_ref(hidden_states, gate_w, w_gate_up, w_down, shared_gate_up, shared_down):
        import jax, jax.numpy as jnp
        import numpy as np
        H = 256
        I = 176
        E = 16
        K = 2
        SI = I * 2

        def _swiglu(gu, inter):
            g, u = (gu[..., :inter], gu[..., inter:])
            return jax.nn.silu(g) * u
        orig_shape = hidden_states.shape
        x = hidden_states.reshape(-1, H)
        logits = jnp.einsum('th,eh->te', x, gate_w)
        scores = jax.nn.softmax(logits, axis=-1)
        topk_w, topk_idx = jax.lax.top_k(scores, K)
        combine = jnp.sum(jax.nn.one_hot(topk_idx, E, dtype=x.dtype) * topk_w[..., None], axis=1)
        gu = jnp.einsum('th,ehj->etj', x, w_gate_up)
        h = _swiglu(gu, I)
        y = jnp.einsum('eti,eih,te->th', h, w_down, combine)
        gu_s = x @ shared_gate_up
        y = y + _swiglu(gu_s, SI) @ shared_down
        return y.reshape(orig_shape)

    def _L1_xattn_ref(k, v, q, ssm_kernel, D, head_dim):
        import jax, jax.numpy as jnp
        import numpy as np
        B, HD, L = k.shape
        H = HD // head_dim
        fft_size = 2 * L
        k_ = k.reshape(B, H, head_dim, L)
        v_ = v.reshape(B, H, head_dim, L)
        q_ = q.reshape(B, H, head_dim, L)
        kv = jnp.einsum('bhil,bhjl->bijhl', k_, v_)
        kv_f = jnp.fft.rfft(kv, n=fft_size)
        kernel_f = jnp.fft.rfft(ssm_kernel, n=fft_size)
        y = jnp.fft.irfft(kv_f * kernel_f, n=fft_size)[..., :L]
        out = y + kv * D[None, None, None, :, None]
        out = jnp.einsum('bijhl,bhil->bjhl', out, q_)
        out = jnp.transpose(out, (0, 2, 1, 3)).reshape(B, H * head_dim, L)
        return out.astype(k.dtype)

    def _L1_ffn_ref(x, ln_w, ff_ln_w, wq, wk, wv, wo, wg, w1, w3, w2):
        import jax, jax.numpy as jnp
        import numpy as np
        EPS = 1e-05
        ROPE_BASE = 150000.0
        NHEADS = 32
        KVHEADS = 8
        HEAD_DIM = 64
        TOP_K = 4

        def _rms(x, w):
            return x * jax.lax.rsqrt(jnp.mean(x * x, -1, keepdims=True) + EPS) * w

        def _rope(q, k):
            S, hd = (q.shape[1], q.shape[-1])
            half = hd // 2
            inv = 1.0 / ROPE_BASE ** (jnp.arange(half, dtype=jnp.float32) / half)
            ang = jnp.arange(S, dtype=jnp.float32)[:, None] * inv
            cos = jnp.concatenate([jnp.cos(ang), jnp.cos(ang)], -1)[None, :, None, :]
            sin = jnp.concatenate([jnp.sin(ang), jnp.sin(ang)], -1)[None, :, None, :]

            def rot(t):
                t1, t2 = (t[..., :half], t[..., half:])
                return jnp.concatenate([-t2, t1], -1)
            return (q * cos + rot(q) * sin, k * cos + rot(k) * sin)
        B, S, D = x.shape
        h = _rms(x, ln_w)
        q = (h @ wq).reshape(B, S, NHEADS, HEAD_DIM)
        k = (h @ wk).reshape(B, S, KVHEADS, HEAD_DIM)
        v = (h @ wv).reshape(B, S, KVHEADS, HEAD_DIM)
        q, k = _rope(q, k)
        g = NHEADS // KVHEADS
        k = jnp.repeat(k, g, axis=2)
        v = jnp.repeat(v, g, axis=2)
        scores = jnp.einsum('bqhd,bkhd->bhqk', q, k) / np.float32(np.sqrt(HEAD_DIM))
        causal = jnp.tril(jnp.ones((S, S), bool))
        scores = jnp.where(causal[None, None], scores, jnp.float32(-1e+30))
        attn = jax.nn.softmax(scores, -1)
        o = jnp.einsum('bhqk,bkhd->bqhd', attn, v).reshape(B, S, NHEADS * HEAD_DIM)
        x = x + o @ wo
        h = _rms(x, ff_ln_w)
        logits = h @ wg
        topv, topi = jax.lax.top_k(logits, TOP_K)
        gate = jax.nn.softmax(topv, -1)
        bidx = jnp.arange(B)[:, None, None]
        sidx = jnp.arange(S)[None, :, None]
        weights = jnp.zeros_like(logits).at[bidx, sidx, topi].set(gate)
        a = jax.nn.silu(jnp.einsum('bsd,edh->bseh', h, w1)) * jnp.einsum('bsd,edh->bseh', h, w3)
        y = jnp.einsum('bseh,ehd->bsed', a, w2)
        moe = jnp.einsum('bsed,bse->bsd', y, weights)
        return x + moe
    x = x + _L0_xattn_ref(_layernorm(x, axis=-1), L0_xattn_k, fside_S2_0, ctx_2048, ctx_2048, 8)
    x = x + _L0_ffn_ref(_layernorm(x, axis=-1), L0_ffn_gate_w, L0_ffn_w_gate_up, L0_ffn_w_down, L0_ffn_shared_gate_up, L0_ffn_shared_down)
    x = x + _L1_xattn_ref(ctx_2048, ctx_2048, _layernorm(x, axis=-1), L1_xattn_ssm_kernel, L1_xattn_D, 8)
    x = x + _L1_ffn_ref(_layernorm(x, axis=-1), L1_ffn_ln_w, L1_ffn_ff_ln_w, L1_ffn_wq, L1_ffn_wk, L1_ffn_wv, L1_ffn_wo, L1_ffn_wg, L1_ffn_w1, L1_ffn_w3, L1_ffn_w2)
    return x

_drawn_inputs = setup_inputs


def setup_inputs(seed=0):
    import zlib

    import numpy as np

    out = dict(_drawn_inputs(seed))
    spreads = {'L1_ffn_ln_w': (1.0, 0.6), 'L1_ffn_ff_ln_w': (1.0, 0.6)}
    factors = {'L0_ffn_gate_w': 8.0,
     'L0_ffn_w_gate_up': 8.0,
     'L0_ffn_w_down': 8.0,
     'L0_ffn_shared_gate_up': 8.0,
     'L0_ffn_shared_down': 8.0,
     'L1_ffn_wq': 8.0,
     'L1_ffn_wk': 8.0,
     'L1_ffn_wv': 8.0,
     'L1_ffn_wo': 8.0,
     'L1_ffn_wg': 8.0,
     'L1_ffn_w1': 8.0,
     'L1_ffn_w3': 8.0,
     'L1_ffn_w2': 8.0}
    for name, (base, spread) in spreads.items():
        noise = np.random.default_rng([zlib.crc32(name.encode()), seed]).standard_normal(out[name].shape)
        drawn = base * np.exp(spread * noise) if base else spread * noise
        out[name] = jnp.asarray(drawn.astype(out[name].dtype))
    for name, factor in factors.items():
        out[name] = (out[name] * factor).astype(out[name].dtype)
    return out
```

```python
from contextlib import ExitStack

import numpy as np

import concourse.bass as bass
from concourse import mybir

F32 = mybir.dt.float32
I32 = mybir.dt.int32
U32 = mybir.dt.uint32
ALU = mybir.AluOpType
ACT = mybir.ActivationFunctionType
AX = mybir.AxisListType

P = 128
NB = 16
D = 256
EPS = 1e-5

MH = 16
MD = 8

E = 16
TOPK = [2, 4]
INTER = [176, 256]
KROWS = [88, 128]
SI = 352
SCH = [128, 128, 96]

QH, KH, HD = 32, 8, 64
QCH = 6

EROWS = NB * P + P
DUMMY = E * EROWS
XROWS = DUMMY + P
XCOLS = D + E + 1
NTOK = NB * P
TILES = [NTOK * k // P + E for k in TOPK]
TMAX = max(TILES) + 4


def ds(start, size):
    return bass.ds(start, size)


def program(nc, x, ctx, conv_k, skip, gate_t, gu, dn, sgu, sdn, dvec, lnw, fflnw,
            wq, wk, wv, wo, wg, w1, w3, w2, cos, sin, out, stage=4):
    es = ExitStack()
    with es:
        def sb(name, shape, dt=F32):
            return es.enter_context(nc.sbuf_tensor(name, shape, dt))

        def sem(name):
            return es.enter_context(nc.semaphore(name))

        PS = es.enter_context(nc.psum_tensor("PS", [P, 8, 512], F32))

        X = sb("X", [P, NB, D])
        WREG = sb("WREG", [P, 24576])
        WOR = sb("WOR", [P, 16 * D])
        SCR = sb("SCR", [P, 17600])
        ident = sb("ident", [P, P])
        tri = sb("tri", [P, P])
        ones = sb("ones", [P, P])
        group = sb("group", [P, P])
        iota_e = sb("iota_e", [P, E])
        row_e = sb("row_e", [P, E])
        le_e = sb("le_e", [P, E, E])
        token_id = sb("token_id", [P, NB], I32)
        zrow = sb("zrow", [P, XCOLS])
        skip_s = sb("skip_s", [P, 2])
        wg_s = sb("wg_s", [P, 2, E])
        st6 = sb("st6", [P, NB, 6])
        lnv = sb("lnv", [P, 8, NB])
        s2, dd, MEAN, M2, VAR, VE, RSTD, RMS = (lnv[:, q, :] for q in range(8))
        s12 = sb("s12", [P, NB, 2])
        mhalf = sb("mhalf", [P, NB])
        rms = sb("rms", [P, 3])
        mcum = sb("mcum", [P, 5, E])
        tab = sb("tab", [1, 2 * TMAX + 1 + E], I32)
        cnt_s = sb("cnt_s", [P, 6, E])
        n_pair = sb("n_pair", [1, 1], I32)
        cnt_i = sb("cnt_i", [P, 2 * E], I32)

        def carve(region, at, *dims, parts=P):
            n = int(np.prod(dims))
            v = region[0:parts, at:at + n]
            if len(dims) == 2:
                v = v.rearrange("p (a b) -> p a b", a=dims[0])
            elif len(dims) == 3:
                v = v.rearrange("p (a b c) -> p a b c", a=dims[0], b=dims[1])
            elif len(dims) == 4:
                v = v.rearrange("p (a b c d) -> p a b c d", a=dims[0], b=dims[1], c=dims[2])
            return v

        GU = carve(WREG, 0, 2, E, 2 * INTER[0])
        DN = carve(WREG, 11264, 2, E, D, parts=88)
        SGU = carve(WREG, 19456, 2, 2 * SI)
        SDN = carve(WREG, 20864, 3, D)
        GT0 = carve(WREG, 21632, 2, E)
        W13 = carve(WREG, 0, 2, E, 2 * INTER[1])
        W2 = carve(WREG, 16384, 2, E, D)
        WQ = carve(WREG, 16384, 2, QH * HD)
        WK = carve(WREG, 20480, 2, KH * HD)
        WV = carve(WREG, 21504, 2, KH * HD)

        WO = carve(WOR, 0, 16, D)
        cT = carve(SCR, 0, 2, NB, P)
        vT = carve(SCR, 4096, 2, NB, P)
        dT = carve(SCR, 8192, 2, NB, P)
        U = carve(SCR, 8192, NB, D)
        CALL = carve(SCR, 12288, NB, D)
        kv = [[carve(SCR, 12288 + 2048 * u + 1024 * blk, 1024) for blk in range(2)] for u in range(2)]
        zb = [carve(WOR, 1024 * blk, 1024) for blk in range(2)]
        TZ = [carve(WOR, 2048 + 256 * u, D) for u in range(2)]
        Vb = [carve(SCR, 16384 + 256 * u, D) for u in range(2)]
        Cb = [carve(SCR, 16896 + 256 * u, D) for u in range(2)]
        gtmp = [carve(WOR, 2560 + 512 * u, 2, D) for u in range(2)]

        o = 4096
        HR0 = carve(SCR, o, 4, XCOLS); o += 4 * XCOLS
        hTg = carve(SCR, o, 2, 4 * P); o += 8 * P
        sgT = carve(SCR, o, 3, 4 * P); o += 12 * P
        aTg = carve(SCR, o, 3, 4 * P); o += 12 * P
        assert o <= 10240
        R_AT = [10240, 17240]

        def route_bufs(at, nb, k):
            r = {}
            for name, dims in (("LG", (nb, E)), ("TV", (nb, 8)), ("EX", (nb, E)), ("TIF", (nb, k)),
                               ("OH", (nb, k, E)), ("M", (nb, E)), ("EM", (nb, E)), ("DEN", (nb,)),
                               ("RD", (nb,)), ("RK", (nb, E)), ("PR", (nb, k, E)), ("PF", (nb, k))):
                n = int(np.prod(dims))
                r[name] = carve(SCR, at, *dims)
                at += n
            return r
        RB = [route_bufs(R_AT[0], 4, 2), route_bufs(R_AT[1], 1, 4)]
        TI = [sb("TI0", [P, 4, 8], U32), sb("TI1", [P, 1, 8], U32)]
        POS = [sb("POS0", [P, 4, 2], I32), sb("POS1", [P, 1, 4], I32)]

        o = 11200
        xt = [carve(SCR, o + 280 * u, XCOLS) for u in range(2)]; o += 560
        xTt = [carve(SCR, o + 256 * u, 2, P) for u in range(2)]; o += 512
        sg = [carve(SCR, o + 256 * u, 256) for u in range(2)]; o += 512
        am = [carve(SCR, o + 256 * u, 256) for u in range(2)]; o += 512
        aTt = carve(SCR, o, 2, P); o += 256
        yt = [carve(SCR, o + 256 * u, D) for u in range(2)]; o += 512
        meta = [carve(SCR, o + 20 * u, E + 1) for u in range(2)]; o += 40
        tcmp = carve(SCR, o, TMAX, E, parts=1); o += TMAX * E
        ttau = carve(SCR, o, TMAX, parts=1); o += TMAX
        ter = carve(SCR, o, 2, TMAX, parts=1); o += 2 * TMAX
        lep = carve(SCR, o, E, E); o += E * E
        assert o <= 16384

        o = 0
        cos_s = carve(SCR, o, HD); o += HD
        sin_s = carve(SCR, o, HD); o += HD
        lnw_s = carve(SCR, o, D); o += D
        fflnw_s = carve(SCR, o, D); o += D
        maskneg = carve(SCR, o, P); o += P
        XD = carve(SCR, o, 4, D); o += 4 * D
        junk = carve(SCR, o, D); o += D
        Hd = carve(SCR, o, D); o += D
        hT = carve(SCR, o, 2, P); o += 2 * P
        Qr = carve(SCR, o, QH * HD); o += QH * HD
        KA = carve(SCR, o, KH * HD); o += KH * HD
        Bt = [carve(SCR, o + 512 * u, 512) for u in range(2)]; o += 1024
        Kd = carve(SCR, o, KH, 2, HD); o += 2 * KH * HD
        qT = carve(SCR, o, 16, P); o += 16 * P
        kTd = carve(SCR, o, KH, P); o += KH * P
        Vs = carve(SCR, o, KH * HD); o += KH * HD
        SM = [[carve(SCR, o + 1024 * i + 512 * par, 4, P) for par in range(2)] for i in range(2)]
        o += 2048
        PT = [carve(SCR, o + 512 * par, 4, P) for par in range(2)]; o += 1024
        On = carve(SCR, o, 512); o += 512
        OT = carve(SCR, o, 16, P); o += 16 * P
        mx = [carve(SCR, o + 8 * i, 2, 4) for i in range(2)]; o += 16
        nbias = [carve(SCR, o + 8 * i, 2, 4) for i in range(2)]; o += 16
        rs = [carve(SCR, o + 8 * i, 2, 4) for i in range(2)]; o += 16
        rinv = [carve(SCR, o + 8 * i, 2, 4) for i in range(2)]; o += 16
        X2 = carve(SCR, o, D); o += D
        h2T = carve(SCR, o, 2, P); o += 2 * P
        HR1 = carve(SCR, o, 1, XCOLS); o += XCOLS
        assert o <= R_AT[1]

        HR = [HR0, HR1]

        kpad = nc.dram_tensor("kpad", [2 * MH, P + D], F32, kind="Internal")
        toe = [nc.dram_tensor(f"toeplitz{n}", [MH, P, D], F32, kind="Internal") for n in range(2)]
        xs = [nc.dram_tensor(f"rows_by_expert{n}", [XROWS, XCOLS], F32, kind="Internal") for n in range(2)]
        acc = [nc.dram_tensor(f"stream{n}", [NTOK + P, D], F32, kind="Internal") for n in range(2)]

        consts = sem("consts_made")
        x_in, misc_in, w0_in = sem("x_in"), sem("misc_in"), sem("w0_in")
        kp_in = sem("kernels_padded")
        toe_out = [sem(f"toeplitz{n}_out") for n in range(2)]
        wd_in, wr_in, w2_in = sem("w13_in"), sem("attention_weights_in"), sem("w2_in")
        wo_in = sem("wo_in")
        d_in = sem("attention_tables_in")
        call_in = sem("ctx_rows_in")
        c_in = [sem(f"ctx_tile{u}_in") for u in range(2)]
        t_in = [sem(f"toeplitz{u}_in") for u in range(2)]
        dve_seq = sem("dve_seq")
        dve_settled, pool_settled = sem("dve_settled"), sem("pool_settled")
        st_done, ve_ready, rstd_ready = sem("stats_done"), sem("variance_ready"), sem("rstd_ready")
        rq_ready, rr_ready = sem("square_ready"), sem("rms_ready")
        v_ready, u_ready = sem("v_ready"), sem("u_ready")
        vt_full, vt_taken = sem("vt_full"), sem("vt_taken")
        g_full, g_taken, g_res = sem("g_full"), sem("g_taken"), sem("g_res")
        kv_ready, y_full, z_ready, dl_ready = sem("kv_ready"), sem("y_full"), sem("z_ready"), sem("delta_ready")
        dt_full, x_done = sem("dt_full"), sem("x_done")
        h_ready = [sem(f"h_ready{n}") for n in range(2)]
        ht_full = [sem(f"ht_full{n}") for n in range(2)]
        ht_taken = [sem(f"ht_taken{n}") for n in range(2)]
        lg_full = [sem(f"logits_full{n}") for n in range(2)]
        lg_taken = [sem(f"logits_taken{n}") for n in range(2)]
        m_ready = [sem(f"picks_ready{n}") for n in range(2)]
        rk_full = [sem(f"rank_full{n}") for n in range(2)]
        rk_taken = [sem(f"rank_taken{n}") for n in range(2)]
        ex_in = [sem(f"gate_shifted{n}") for n in range(2)]
        ex_out = [sem(f"gate_exp{n}") for n in range(2)]
        row_ready = [sem(f"row_ready{n}") for n in range(2)]
        pos_ready = [sem(f"pos_ready{n}") for n in range(2)]
        scattered = [sem(f"scattered{n}") for n in range(2)]
        cnt_full = [sem(f"count_full{n}") for n in range(2)]
        tab_ready = [sem(f"tables_ready{n}") for n in range(2)]
        tau_made = [sem(f"tau_made{n}") for n in range(2)]
        pad_in = [sem(f"padding_in{n}") for n in range(2)]
        acc_in = [sem(f"stream_out{n}") for n in range(2)]
        up_full, sg_ready, at_ready, dn_full, dn_taken = (
            sem("shared_up_full"), sem("shared_silu"), sem("shared_act"), sem("shared_down_full"),
            sem("shared_down_taken"))
        names = ("ok", "t1_full", "xt_ready", "up_full", "silu", "meta", "act", "t2_full", "at", "down_full", "y")
        ML = [{k: sem(f"moe{n}_{k}") for k in names} for n in range(2)]
        xin = [[sem(f"moe{n}_rows{u}_in") for u in range(2)] for n in range(2)]
        added = [sem(f"moe{n}_added") for n in range(2)]
        moe_done = [sem(f"moe{n}_done") for n in range(2)]
        x_back = sem("x_back")
        hT_full, hT_sb = sem("hT_full"), sem("hT_sb")
        proj_full, rope_taken, v_taken, rp_ready = sem("proj_full"), sem("rope_taken"), sem("v_taken"), sem("roped")
        qt_full, qka_sb, qkd_sb = sem("qt_full"), sem("qk_act_sb"), sem("qk_dve_sb")
        s_full, sm_taken, nb_ready, ex_ready = sem("s_full"), sem("s_masked"), sem("nbias_ready"), sem("exp_ready")
        mx_ready, ri_ready = sem("max_ready"), sem("rinv_ready")
        pt_full, pt0_taken, pt1_taken = sem("pt_full"), sem("pt0_taken"), sem("pt1_taken")
        pv_full, o_taken, ot_full, ot_taken = sem("pv_full"), sem("o_taken"), sem("ot_full"), sem("ot_taken")
        wo_full, wo_taken = sem("wo_full"), sem("wo_taken")
        f_res, row_feat = sem("xd_added"), sem("row_features_ready")
        out_done = sem("out_done")

        def need(eng, s, v):
            if isinstance(v, int) and v <= 0:
                return
            eng.wait_ge(s, v)

        def settle(eng, s):
            eng.sem_inc(s, 1)

        class Chain:

            def __init__(self, eng, s):
                self.eng, self.s, self.base, self.i, self.per, self.k = eng, s, 0, None, 0, 0

            def value(self):
                return self.base + self.k if self.i is None else self.i * self.per + (self.base + self.k)

            def link(self, ins):
                self.k += 1
                ins.then_inc(self.s, 1)
                self.eng.wait_ge(self.s, self.value())

            def enter(self, i, start, per):
                self.base = self.base + self.k - start * per
                self.i, self.per, self.k = i, per, 0

            def leave(self, end):
                assert self.k == self.per, ("per is", self.k)
                self.base, self.i, self.k = self.base + end * self.per, None, 0

        block = es.enter_context(nc.Block())

        @block.sync
        def _(sp):
            def load_w0():
                sp.dma_start(GT0, gate_t.rearrange("(k p) e -> p k e", p=P)).then_inc(w0_in, 16)
                sp.dma_start(SGU, sgu.rearrange("(k p) j -> p k j", p=P)).then_inc(w0_in, 16)
                sp.dma_start(SDN[:, 0:2, :], sdn[0:2 * P, :].rearrange("(k p) j -> p k j", p=P)).then_inc(w0_in, 16)
                sp.dma_start(SDN[0:96, 2, :], sdn[2 * P:SI, :]).then_inc(w0_in, 16)
                for k in range(2):
                    sp.dma_start(GU[:, k], gu[:, k * P:(k + 1) * P, :].rearrange("e p j -> p e j")).then_inc(w0_in, 16)
                    sp.dma_start(DN[:, k], dn[:, k * 88:(k + 1) * 88, :].rearrange("e p j -> p e j")).then_inc(w0_in, 16)

            def load_w1():
                sp.wait_ge(moe_done[0], 1)
                for k in range(2):
                    r = slice(k * P, (k + 1) * P)
                    sp.dma_start(WQ[:, k], wq[r, :]).then_inc(wr_in, 16)
                    sp.dma_start(WK[:, k], wk[r, :]).then_inc(wr_in, 16)
                    sp.dma_start(WV[:, k], wv[r, :]).then_inc(wr_in, 16)
                for k in range(2):
                    r = slice(k * P, (k + 1) * P)
                    sp.dma_start(W13[:, k, :, 0:D], w1[:, r, :].rearrange("e p j -> p e j")).then_inc(wd_in, 16)
                    sp.dma_start(W13[:, k, :, D:2 * D], w3[:, r, :].rearrange("e p j -> p e j")).then_inc(wd_in, 16)

            def mix(n):
                if n:
                    sp.wait_ge(z_ready, 4 + 32)
                    sp.wait_ge(moe_done[0], 1)
                sp.dma_start(CALL, ctx.rearrange("b p l -> p b l")).then_inc(call_in, 16)
                if n == 0:
                    with sp.Fori(0, NB // 2) as i:
                        for u in range(2):
                            b = i * 2 + u
                            sp.wait_ge(vt_full, b + 1)
                            sp.dma_start(Cb[u], ctx[ds(b, 1)].rearrange("b p l -> p (b l)")).then_inc(c_in[u], 16)
                sp.wait_ge(toe_out[n], 16)
                with sp.Fori(0, MH // 2) as i:
                    for u in range(2):
                        h = i * 2 + u
                        sp.wait_ge(y_full, h * 2 + (32 * n + 2))
                        sp.dma_start(TZ[u], toe[n][ds(h, 1)].rearrange("a p l -> p (a l)")).then_inc(t_in[u], 16)

            def stream_out(n):
                if n == 0:
                    sp.wait_ge(dn_taken, 8)
                else:
                    sp.wait_ge(wo_taken, NB)
                sp.dma_start(acc[n][0:NTOK, :].rearrange("(b p) l -> p b l", p=P), X[:]).then_inc(acc_in[n], 16)
                sp.dma_start(acc[n][NTOK:NTOK + P, :], zrow[:, 0:D]).then_inc(acc_in[n], 16)

            def moe(n):
                m = ML[n]
                per = NB * TOPK[n] * 16
                sp.wait_ge(scattered[n], per)
                sp.dma_start(xs[n][DUMMY:DUMMY + P, :], zrow[:]).then_inc(pad_in[n], 16)
                sp.wait_ge(tab_ready[n], 1)
                with sp.Fori(0, E) as e:
                    r = sp.value_load(tab[0:1, ds(e + (2 * TMAX + 1), 1)], min_val=0, max_val=DUMMY)
                    sp.dma_start(xs[n][ds(r, P), :], zrow[:]).then_inc(pad_in[n], 16)
                sp.wait_ge(pad_in[n], 16 * (E + 1))

                def load(t, u):
                    r = sp.value_load(tab[0:1, ds(t + TMAX, 1)], min_val=0, max_val=DUMMY)
                    sp.dma_start(xt[u], xs[n][ds(r, P), :]).then_inc(xin[n][u], 16)

                load(0, 0)
                load(1, 1)
                pairs = sp.value_load(tab[0:1, 2 * TMAX:2 * TMAX + 1], min_val=1, max_val=TILES[n] // 2 + 1)
                with sp.Fori(0, pairs) as i:
                    for u in range(2):
                        t = i * 2 + u
                        sp.wait_ge(m["t1_full"], t + 1)
                        sp.wait_ge(m["meta"], t + 1)
                        load(t + 2, u)

            sp.dma_start(X[:], x.rearrange("b p l -> p b l")).then_inc(x_in, 16)
            sp.dma_start(skip_s[:, 0:1], skip.rearrange("(p a) -> p a", a=1)).then_inc(misc_in, 16)
            dv = dvec.rearrange("(p a) -> p a", a=1)
            dsrc = bass.AP(tensor=dv.tensor, offset=dv.offset, ap=[[1, MH], [0, MD], [1, 1]])
            sp.dma_start(skip_s[:, 1:2], dsrc).then_inc(misc_in, 16)
            sp.dma_start(wg_s[:], wg.rearrange("(k p) e -> p k e", p=P)).then_inc(misc_in, 16)
            sp.wait_ge(consts, 1)
            sp.dma_start(kpad[:, 0:P], zrow[0:2 * MH, 0:P]).then_inc(kp_in, 16)
            sp.dma_start(kpad[:, P:P + D], conv_k).then_inc(kp_in, 16)
            sp.wait_ge(kp_in, 32)
            for n in range(2):
                k0 = kpad[n * MH:n * MH + 1, P:P + 1]
                src = bass.AP(tensor=k0.tensor, offset=k0.offset, ap=[[P + D, MH], [-1, P], [1, D]])
                sp.dma_start(toe[n][:, :, :], src).then_inc(toe_out[n], 16)
            load_w0()
            mix(0)
            if stage >= 2:
                stream_out(0)
                moe(0)
                sp.wait_ge(moe_done[0], 1)
                sp.dma_start(X[:], acc[0][0:NTOK, :].rearrange("(b p) l -> p b l", p=P)).then_inc(x_back, 16)
            if stage >= 3:
                load_w1()
                mix(1)
            if stage >= 4:
                sp.wait_ge(x_done, 16)
                sp.dma_start(WO, wo.rearrange("(t p) n -> p t n", p=P)).then_inc(wo_in, 16)
                sp.dma_start(cos_s, cos).then_inc(d_in, 16)
                sp.dma_start(sin_s, sin).then_inc(d_in, 16)
                sp.dma_start(lnw_s, lnw.partition_broadcast(P)).then_inc(d_in, 16)
                sp.dma_start(fflnw_s, fflnw.partition_broadcast(P)).then_inc(d_in, 16)
                sp.wait_ge(proj_full, QCH * NB)
                for k in range(2):
                    sp.dma_start(W2[:, k], w2[:, k * P:(k + 1) * P, :].rearrange("e p j -> p e j")).then_inc(w2_in, 16)
                stream_out(1)
                moe(1)
                sp.wait_ge(moe_done[1], 1)
                sp.dma_start(out.rearrange("b p l -> (b p) l"), acc[1][0:NTOK, :]).then_inc(out_done, 16)
            else:
                if stage == 1:
                    sp.wait_ge(x_done, 8)
                elif stage == 2:
                    sp.wait_ge(x_back, 16)
                else:
                    sp.wait_ge(x_done, 16)
                sp.dma_start(out.rearrange("b p l -> p b l"), X[:]).then_inc(out_done, 16)
            sp.wait_ge(out_done, 16)
            sp.wait_ge(w0_in, 16 * 8)
            sp.wait_ge(toe_out[1], 16)
            if stage >= 2:
                sp.wait_ge(acc_in[0], 32)
            if stage >= 4:
                sp.wait_ge(acc_in[1], 32)

        @block.gpsimd
        def _(pool):
            g = nc.gpsimd
            made = [0]

            def mk(ins):
                made[0] += 1
                ins.then_inc(consts, 1)
                pool.wait_ge(consts, made[0])

            mk(g.memset(zrow[:], 0.0))
            mk(g.memset(ones[:], 1.0))
            mk(g.memset(ident[:], 0.0))
            mk(g.affine_select(out=ident[:], in_=ident[:], compare_op=ALU.not_equal, fill=1.0, base=0,
                               pattern=[[-1, P]], channel_multiplier=1))
            mk(g.affine_select(out=tri[:], in_=ones[:], compare_op=ALU.is_gt, fill=0.0, base=0,
                               pattern=[[1, P]], channel_multiplier=-1))
            mk(g.affine_select(out=group[:], in_=ones[:], compare_op=ALU.is_ge, fill=0.0, base=0,
                               pattern=[[-MD, MH], [0, MD]], channel_multiplier=1))
            mk(g.affine_select(out=group[:], in_=group[:], compare_op=ALU.is_ge, fill=0.0, base=MD - 1,
                               pattern=[[MD, MH], [0, MD]], channel_multiplier=-1))
            mk(g.iota(iota_e[:], pattern=[[1, E]], base=0, channel_multiplier=0,
                      allow_small_or_imprecise_dtypes=True))
            mk(g.iota(row_e[:], pattern=[[EROWS, E]], base=0, channel_multiplier=0,
                      allow_small_or_imprecise_dtypes=True))
            mk(g.memset(le_e[:], 1.0))
            mk(g.affine_select(out=le_e[:], in_=le_e[:], compare_op=ALU.is_ge, fill=0.0, base=0,
                               pattern=[[1, E], [-1, E]], channel_multiplier=0))
            mk(g.iota(token_id[:], pattern=[[P, NB]], base=0, channel_multiplier=1))
            pool.wait_ge(kp_in, 32)
            mk(g.iota(zrow[:, D + E:XCOLS].bitcast(I32), pattern=[[0, 1]], base=NTOK, channel_multiplier=1))
            mk(g.memset(mhalf[:], -0.5))
            assert made[0] == 14

            def root(rnd, dst):
                pool.wait_ge(ve_ready, rnd + 1)
                g.tensor_tensor(dst, VE, mhalf[:], ALU.pow).then_inc(rstd_ready, 1)

            def root1(b):
                pool.wait_ge(rq_ready, b + 1)
                g.tensor_tensor(rms[:, 2:3], rms[:, 1:2], mhalf[:, 0:1], ALU.pow).then_inc(rr_ready, 1)

            def mix(n):
                pre = vT if n == 0 else cT
                pool.wait_ge(vt_taken, 2 + NB * (n + 1))
                pool.wait_ge(g_taken, 2 + 8 * (n + 1))
                with pool.Fori(0, MH // 2) as i:
                    for u in range(2):
                        h = i * 2 + u
                        pool.wait_ge(y_full, h * 2 + (32 * n + 2))
                        for blk in range(2):
                            a = pre[:, blk, :, ds(h * MD, MD)].unsqueeze(3).to_broadcast([P, NB, MD, MD])
                            c = cT[:, blk, :, ds(h * MD, MD)].unsqueeze(2).to_broadcast([P, NB, MD, MD])
                            g.tensor_tensor(kv[u][blk].rearrange("p (b i j) -> p b i j", b=NB, i=MD), a, c,
                                            ALU.mult).then_inc(kv_ready, 1)

            def scatter(n, rounds, j_count, done_per_round):
                pool.wait_ge(pos_ready[n], rounds + 1)
                pool.wait_ge(row_ready[n], rounds + 1)
                settle(pool, pool_settled)
                for j in range(j_count):
                    for k in range(TOPK[n]):
                        g.indirect_dma_start(
                            out=xs[n][:, :], out_offset=bass.IndirectOffsetOnAxis(ap=POS[n][:, j, k:k + 1], axis=0),
                            in_=HR[n][:, j, :], in_offset=None).then_inc(scattered[n], 16)

            def moe(n):
                m = ML[n]
                pool.sem_inc(m["ok"], 2)
                pool.wait_ge(acc_in[n], 32)
                pool.wait_ge(tab_ready[n], 1)
                pairs = pool.value_load(tab[0:1, 2 * TMAX:2 * TMAX + 1], min_val=1, max_val=TILES[n] // 2 + 1)
                with pool.Fori(0, pairs) as i:
                    for u in range(2):
                        t = i * 2 + u
                        pool.wait_ge(m["y"], t + 1)
                        settle(pool, pool_settled)
                        settle(pool, pool_settled)
                        g.indirect_dma_start(
                            out=acc[n][:, :], out_offset=bass.IndirectOffsetOnAxis(
                                ap=meta[u][:, E:E + 1].bitcast(I32), axis=0),
                            in_=yt[u], in_offset=None, compute_op=ALU.add).then_inc(added[n], 16)
                        pool.wait_ge(added[n], t * 16 + 16)
                        pool.sem_inc(m["ok"], 1)
                pool.wait_ge(m["act"], pairs * 2 + 1)
                pool.wait_ge(m["xt_ready"], pairs * 2 + 2)
                pool.sem_inc(moe_done[n], 1)

            def tau(n):
                g.iota(ttau, pattern=[[P, TMAX]], base=0, channel_multiplier=0,
                       allow_small_or_imprecise_dtypes=True).then_inc(tau_made[n], 1)

            def rope(b, c):
                pool.wait_ge(rope_taken, b * 5 + (c + 1))
                need(pool, qt_full, b * 6)
                if c < 4:
                    q = Qr[:, c * 512:(c + 1) * 512]
                    g.tensor_tensor(q, q, Bt[c % 2], ALU.add).then_inc(rp_ready, 1)
                else:
                    def twice(v):
                        return v.rearrange("p (g d) -> p g d", g=KH).unsqueeze(2).to_broadcast([P, KH, 2, HD])
                    g.tensor_tensor(Kd, twice(KA), twice(Bt[0]), ALU.add).then_inc(rp_ready, 1)

            root(0, RSTD)
            mix(0)
            if stage >= 2:
                root(1, RSTD)
                pool.wait_ge(x_done, 8)
                tau(0)
                with pool.Fori(0, 4) as gi:
                    scatter(0, gi, 4, None)
                pool.wait_ge(scattered[0], NB * TOPK[0] * 16)
                moe(0)
            if stage >= 3:
                root(2, RSTD)
                mix(1)
            if stage >= 4:
                pool.wait_ge(x_done, 16)
                g.memset(maskneg, 0.0).then_inc(consts, 1)
                pool.wait_ge(consts, 15)
                g.affine_select(out=maskneg, in_=maskneg, compare_op=ALU.is_ge, fill=-1e30, base=0,
                                pattern=[[-1, P]], channel_multiplier=1).then_inc(consts, 1)
                root(3, RSTD)
                root(4, RMS)
                for c in range(5):
                    rope(0, c)

                def body(b, first=False, last=False):
                    if not first:
                        root1(b - 1)
                    if not last:
                        rope(b + 1, 0)
                        rope(b + 1, 1)
                        rope(b + 1, 2)
                    if not first:
                        scatter(1, b - 1, 1, None)
                    if not last:
                        rope(b + 1, 3)
                        rope(b + 1, 4)
                body(0, first=True)
                with pool.Fori(1, NB - 1) as b:
                    body(b)
                body(NB - 1, last=True)
                root1(NB - 1)
                scatter(1, NB - 1, 1, None)
                pool.wait_ge(wo_taken, NB)
                tau(1)
                moe(1)

        @block.scalar
        def _(act):
            a = nc.scalar
            act.sem_inc(vt_taken, 2)

            def mix(n):
                with act.Fori(0, NB // 2) as i:
                    for u in range(2):
                        b = i * 2 + u
                        act.wait_ge(vt_full, b + (NB * n + 3))
                        src = PS[:, u, :].rearrange("p (c k s) -> p c k s", c=2, k=2)
                        if n == 0:
                            a.copy(cT[:, :, ds(b, 1), :].rearrange("p k b s -> p k (b s)"), src[:, 1])
                        a.copy(vT[:, :, ds(b, 1), :].rearrange("p k b s -> p k (b s)"), src[:, 0])\
                            .then_inc(vt_taken, 1)

            def gate_exp(n, r):
                act.wait_ge(ex_in[n], r + 1)
                a.activation(RB[n]["EX"], RB[n]["EX"], ACT.Exp).then_inc(ex_out[n], 1)

            def ffn0():
                with act.Fori(0, 4) as gi:
                    for j in range(4):
                        if j == 0:
                            act.wait_ge(up_full, gi * 3)
                        act.wait_ge(ht_full[0], gi * 4 + (j + 1))
                        a.copy(hTg[:, :, j * P:(j + 1) * P],
                               PS[:, 6 + j % 2, 0:D].rearrange("p (k s) -> p k s", k=2)).then_inc(ht_taken[0], 1)
                    gate_exp(0, gi)
                    for c in range(3):
                        act.wait_ge(up_full, gi * 3 + (c + 1))
                        act.wait_ge(at_ready, gi * 3 + (c + 1))
                        r = SCH[c]
                        a.activation(sgT[0:r, c, :], PS[0:r, 2 * c, :], ACT.Silu).then_inc(sg_ready, 1)

            def moe(n):
                m = ML[n]
                inter = INTER[n]

                def x_t(t, u, first):
                    act.wait_ge(m["t1_full"], t + 1)
                    if not first:
                        act.wait_ge(m["up_full"], t - 1)
                    a.copy(xTt[u], PS[:, u, 0:D].rearrange("p (k s) -> p k s", k=2)).then_inc(m["xt_ready"], 1)

                def silu(t, u):
                    act.wait_ge(m["up_full"], t + 1)
                    need(act, m["act"], t - 1)
                    a.activation(sg[u][:, 0:inter], PS[:, 2 + u, 0:inter], ACT.Silu).then_inc(m["silu"], 1)

                act.wait_ge(tab_ready[n], 1)
                x_t(0, 0, True)
                silu(0, 0)
                x_t(1, 1, True)
                pairs = act.value_load(tab[0:1, 2 * TMAX:2 * TMAX + 1], min_val=1, max_val=TILES[n] // 2 + 1)
                with act.Fori(0, pairs) as i:
                    for u in range(2):
                        t = i * 2 + u
                        silu(t + 1, 1 - u)
                        x_t(t + 2, u, False)
                        act.wait_ge(m["down_full"], t + 1)
                        act.wait_ge(m["ok"], t + 1)
                        a.copy(yt[u], PS[:, 6 + u, 0:D]).then_inc(m["y"], 1)

            def h_t(b):
                act.wait_ge(hT_full, b + 1)
                need(act, proj_full, b * 6)
                a.copy(hT, PS[:, 7, 0:D].rearrange("p (k s) -> p k s", k=2)).then_inc(hT_sb, 1)

            def exps(b, i):
                act.wait_ge(nb_ready, b * 4 + (i + 1))
                need(act, ri_ready, b * 4 + (i - 1))
                for r in range(8):
                    par, q = r % 2, r // 2
                    s = SM[i % 2][par][:, q, :]
                    ins = a.activation(s, s, ACT.Exp, bias=nbias[i % 2][:, par, q:q + 1], scale=HD ** -0.5,
                                       accum_out=rs[i % 2][:, par, q:q + 1])
                ins.then_inc(ex_ready, 1)

            def pt0(b, i):
                act.wait_ge(pt_full, b * 8 + (2 * i + 1))
                need(act, pv_full, b * 4 + i)
                a.copy(PT[0], PS[:, 4, :].rearrange("p (r q) -> p r q", r=4)).then_inc(pt0_taken, 1)

            def o_t(b, i):
                act.wait_ge(ot_full, b * 4 + (i + 1))
                need(act, wo_full, b)
                a.copy(OT[:, 4 * i:4 * i + 4, :], PS[:, 7, :].rearrange("p (r q) -> p r q", r=4)).then_inc(ot_taken, 1)

            def v_sb(b):
                act.wait_ge(proj_full, b * 6 + 6)
                need(act, pv_full, b * 4)
                a.copy(Vs, PS[:, 3, :]).then_inc(v_taken, 1)

            def qk_sb(b, s):
                act.wait_ge(qt_full, b * 6 + (s + 1))
                need(act, s_full, b * 8)
                src = PS[:, [0, 1, 4, 5, 0, 1][s], :].rearrange("p (r q) -> p r q", r=4)
                dst = qT[:, 4 * s:4 * s + 4, :] if s < 4 else kTd[:, 4 * (s - 4):4 * (s - 3), :]
                a.copy(dst, src).then_inc(qka_sb, 1)

            def h2_t(b):
                act.wait_ge(ht_full[1], b + 1)
                need(act, lg_full[1], b)
                a.copy(h2T, PS[:, 7, 0:D].rearrange("p (k s) -> p k s", k=2)).then_inc(ht_taken[1], 1)

            mix(0)
            if stage >= 2:
                act.wait_ge(x_done, 8)
                ffn0()
                moe(0)
            if stage >= 3:
                act.wait_ge(moe_done[0], 1)
                mix(1)
            if stage >= 4:
                act.wait_ge(x_done, 16)
                h_t(0)
                v_sb(0)
                for s in (0, 2, 4):
                    qk_sb(0, s)

                def body(b, first=False, last=False):
                    if not last:
                        h_t(b + 1)
                    exps(b, 0)
                    if not first:
                        h2_t(b - 1)
                    exps(b, 1)
                    if not first:
                        gate_exp(1, b - 1)
                    pt0(b, 0)
                    exps(b, 2)
                    o_t(b, 0)
                    pt0(b, 1)
                    exps(b, 3)
                    o_t(b, 1)
                    pt0(b, 2)
                    o_t(b, 2)
                    pt0(b, 3)
                    if not last:
                        v_sb(b + 1)
                        for s in (0, 2, 4):
                            qk_sb(b + 1, s)
                    o_t(b, 3)
                body(0, first=True)
                with act.Fori(1, NB - 1) as b:
                    body(b)
                body(NB - 1, last=True)
                h2_t(NB - 1)
                gate_exp(1, NB - 1)
                moe(1)

        @block.tensor
        def _(pe):
            mm, tr = nc.tensor.matmul, nc.tensor.transpose
            pe.sem_inc(vt_full, 2)
            pe.sem_inc(y_full, 4)
            pe.wait_ge(consts, 14)

            def mix(n):
                with pe.Fori(0, NB // 2) as i:
                    for u in range(2):
                        b = i * 2 + u
                        pe.wait_ge(v_ready, b + (NB * n + 1))
                        pe.wait_ge(vt_taken, b + (NB * n + 1))
                        if n == 0:
                            pe.wait_ge(c_in[u], i * 16 + 16)
                            for k in range(2):
                                tr(PS[:, u, D + k * P:D + (k + 1) * P], Cb[u][:, k * P:(k + 1) * P], ident[:])
                        for k in range(2):
                            ins = tr(PS[:, u, k * P:(k + 1) * P], Vb[u][:, k * P:(k + 1) * P], ident[:])
                        ins.then_inc(vt_full, 1)
                with pe.Fori(0, 4) as i:
                    for u in range(2):
                        p = i * 2 + u
                        pe.wait_ge(u_ready, p * 2 + (NB * n + 2))
                        pe.wait_ge(g_taken, p + (8 * n + 1))
                        mm(PS[:, 2 + u, :], group[:], U[:, ds(p * 2, 2), :].rearrange("p b l -> p (b l)"),
                           start=True, stop=True).then_inc(g_full, 1)
                pe.wait_ge(vt_taken, 2 + NB * (n + 1))
                pe.wait_ge(g_taken, 2 + 8 * (n + 1))
                with pe.Fori(0, MH // 2) as i:
                    for u in range(2):
                        h = i * 2 + u
                        pe.wait_ge(t_in[u], i * 16 + (MH // 2 * 16 * n + 16))
                        for blk in range(2):
                            pe.wait_ge(kv_ready, h * 2 + (32 * n + blk + 1))
                            pe.wait_ge(z_ready, h * 2 + (32 * n + blk + 1))
                            for half in range(2):
                                bank = PS[:, 4 * u + 2 * blk + half, :]
                                c = slice(512 * half, 512 * half + 512)
                                if blk:
                                    mm(bank, TZ[u][:, P:D], kv[u][0][:, c], start=True, stop=False)
                                ins = mm(bank, TZ[u][:, 0:P], kv[u][blk][:, c], start=(blk == 0), stop=True)
                            ins.then_inc(y_full, 1)
                pe.wait_ge(z_ready, 4 + 32 * (n + 1))
                pe.wait_ge(dl_ready, 2 + 32 * (n + 1))
                for p in range(8):
                    for q in range(4):
                        ins = tr(PS[:, p, q * P:(q + 1) * P], dT[:, q % 2, 2 * p + q // 2, :], ident[:])
                    ins.then_inc(dt_full, 1)

            def rank(n, nb, bank, cols):
                mm(bank[:, 0:cols], tri[:], RB[n]["M"].rearrange("p b e -> p (b e)"), start=True, stop=False)
                mm(bank[:, 0:cols], ones[:], mcum[:, 0:nb, :].rearrange("p b e -> p (b e)"),
                   start=False, stop=True).then_inc(rk_full[n], 1)

            def ffn0():
                pe.wait_ge(w0_in, 16 * 8)
                with pe.Fori(0, 4) as gi:
                    for j in range(4):
                        pe.wait_ge(h_ready[0], gi * 4 + (j + 1))
                        if j == 0:
                            pe.wait_ge(dn_taken, gi * 2)
                            pe.wait_ge(rk_taken[0], gi)
                        if j >= 2:
                            pe.wait_ge(ht_taken[0], gi * 4 + (j - 1))
                        for k in range(2):
                            ins = tr(PS[:, 6 + j % 2, k * P:(k + 1) * P], HR0[:, j, k * P:(k + 1) * P], ident[:])
                        ins.then_inc(ht_full[0], 1)
                    pe.wait_ge(at_ready, gi * 3 + 3)
                    for j in range(4):
                        pe.wait_ge(ht_taken[0], gi * 4 + (j + 1))
                        for k in range(2):
                            ins = mm(PS[:, 5, j * E:(j + 1) * E], hTg[:, k, j * P:(j + 1) * P], GT0[:, k, :],
                                     start=(k == 0), stop=(k == 1))
                    ins.then_inc(lg_full[0], 1)
                    for c in range(3):
                        pe.wait_ge(at_ready, gi * 3 + (c + 1))
                        if c == 1:
                            pe.wait_ge(m_ready[0], gi + 1)
                            rank(0, 4, PS[:, 6, :], 64)
                        if c == 2:
                            pe.wait_ge(lg_taken[0], gi + 1)
                        r = SCH[c]
                        for half in range(2):
                            for k in range(2):
                                c0 = half * SI + c * P
                                ins = mm(PS[0:r, 2 * c + half, :], SGU[:, k, c0:c0 + r], hTg[:, k, :],
                                         start=(k == 0), stop=(k == 1))
                        ins.then_inc(up_full, 1)
                    pe.wait_ge(at_ready, gi * 3 + 6)
                    for j in range(4):
                        if j == 2:
                            pe.wait_ge(rk_taken[0], gi + 1)
                        for c in range(3):
                            r = SCH[c]
                            ins = mm(PS[:, 7 - j // 2, (j % 2) * D:(j % 2 + 1) * D], aTg[0:r, c, j * P:(j + 1) * P],
                                     SDN[0:r, c, :], start=(c == 0), stop=(c == 2))
                        if j % 2:
                            ins.then_inc(dn_full, 1)
                pe.wait_ge(dn_taken, 8)
                count(0)

            def count(n):
                mm(PS[:, 5, 0:E], ones[:], mcum[:, 0, :], start=True, stop=True).then_inc(cnt_full[n], 1)

            def moe(n):
                m = ML[n]
                inter, kr = INTER[n], KROWS[n]
                up = GU if n == 0 else W13
                down = DN if n == 0 else W2

                def expert(t):
                    return pe.value_load(tab[0:1, ds(t, 1)], min_val=0, max_val=E - 1)

                def t1(t, i, u, first):
                    pe.wait_ge(xin[n][u], i * 16 + 16)
                    if not first:
                        pe.wait_ge(m["xt_ready"], t - 1)
                    for k in range(2):
                        ins = tr(PS[:, u, k * P:(k + 1) * P], xt[u][:, k * P:(k + 1) * P], ident[:])
                    ins.then_inc(m["t1_full"], 1)

                def ups(t, u):
                    e = expert(t)
                    pe.wait_ge(m["xt_ready"], t + 1)
                    need(pe, m["act"], t - 1)
                    for k in range(2):
                        ins = mm(PS[:, 2 + u, 0:2 * inter], xTt[u][:, k, :],
                                 up[:, k, ds(e, 1), :].rearrange("p e j -> p (e j)"), start=(k == 0), stop=(k == 1))
                    ins.then_inc(m["up_full"], 1)

                pe.wait_ge(tab_ready[n], 1)
                if n:
                    pe.wait_ge(wd_in, 64)
                t1(0, 0, 0, True)
                ups(0, 0)
                t1(1, 0, 1, True)
                if n:
                    pe.wait_ge(w2_in, 32)
                pairs = pe.value_load(tab[0:1, 2 * TMAX:2 * TMAX + 1], min_val=1, max_val=TILES[n] // 2 + 1)
                with pe.Fori(0, pairs) as i:
                    for u in range(2):
                        t = i * 2 + u
                        ups(t + 1, 1 - u)
                        pe.wait_ge(m["act"], t + 1)
                        pe.wait_ge(m["at"], t)
                        for k in range(2):
                            ins = tr(PS[0:kr, 4 + u, k * P:(k + 1) * P], am[u][:, k * kr:(k + 1) * kr], ident[:])
                        ins.then_inc(m["t2_full"], 1)
                        t1(t + 2, i + 1, u, False)
                        e = expert(t)
                        pe.wait_ge(m["at"], t + 2)
                        pe.wait_ge(m["ok"], t + 1)
                        for k in range(2):
                            ins = mm(PS[:, 6 + u, 0:D], aTt[0:kr, k, :],
                                     down[:, k, ds(e, 1), :].rearrange("p e j -> p (e j)"),
                                     start=(k == 0), stop=(k == 1))
                        ins.then_inc(m["down_full"], 1)

            def h_t(b, waits):
                pe.wait_ge(h_ready[1], b + 1)
                for s, v in waits:
                    need(pe, s, v)
                for k in range(2):
                    ins = tr(PS[:, 7, k * P:(k + 1) * P], Hd[:, k * P:(k + 1) * P], ident[:])
                ins.then_inc(hT_full, 1)

            def proj(b, c, head=False):
                pe.wait_ge(hT_sb, b + 1)
                if c == 0:
                    need(pe, wo_taken, b - 1)
                elif c == 1:
                    need(pe, v_taken, b)
                else:
                    pe.wait_ge(rope_taken, b * 5 + (c - 1))
                w = WQ[:, :, c * 512:(c + 1) * 512] if c < 4 else (WK if c == 4 else WV)
                for k in range(2):
                    ins = mm(PS[:, 2 + c % 2, :], hT[:, k, :], w[:, k, :], start=(k == 0), stop=(k == 1))
                ins.then_inc(proj_full, 1)

            def q_t(b):
                for s in range(6):
                    pe.wait_ge(rp_ready, b * 5 + (min(s, 4) + 1))
                    if s < 2:
                        need(pe, sm_taken, b * 8)
                    elif s == 2:
                        need(pe, pt0_taken, b * 4)
                    elif s == 3:
                        need(pe, pt1_taken, b * 4)
                    elif s == 4:
                        pe.wait_ge(qka_sb, b * 3 + 1)
                    else:
                        pe.wait_ge(qkd_sb, b * 3 + 1)
                    for q in range(4):
                        if s < 4:
                            src = Qr[:, (4 * s + q) * P:(4 * s + q + 1) * P]
                        else:
                            src = Kd[:, 4 * (s - 4) + q].rearrange("p a d -> p (a d)")
                        ins = tr(PS[:, [0, 1, 4, 5, 0, 1][s], q * P:(q + 1) * P], src, ident[:])
                    ins.then_inc(qt_full, 1)

            def score(b, i):
                if i == 0:
                    pe.wait_ge(qka_sb, b * 3 + 3)
                    pe.wait_ge(qkd_sb, b * 3 + 3)
                else:
                    pe.wait_ge(sm_taken, b * 8 + 2 * i)
                for r in range(8):
                    h = 8 * i + r
                    par, q = r % 2, r // 2
                    rows = slice(par * HD, par * HD + HD)
                    ins = mm(PS[:, par, q * P:(q + 1) * P], qT[rows, h // 2, :], kTd[rows, h // 4, :],
                             start=True, stop=True)
                    if r >= 6:
                        ins.then_inc(s_full, 1)

            def p_t(b, i):
                pe.wait_ge(ex_ready, b * 4 + (i + 1))
                if i:
                    pe.wait_ge(pt0_taken, b * 4 + i)
                    pe.wait_ge(pt1_taken, b * 4 + i)
                for par in range(2):
                    for q in range(4):
                        ins = tr(PS[:, 4 + par, q * P:(q + 1) * P], SM[i % 2][par][:, q, :], ident[:])
                    ins.then_inc(pt_full, 1)

            def pv(b, i):
                pe.wait_ge(pt0_taken, b * 4 + (i + 1))
                pe.wait_ge(pt1_taken, b * 4 + (i + 1))
                if i == 0:
                    pe.wait_ge(v_taken, b + 1)
                need(pe, o_taken, b * 4 + i)
                for r in range(8):
                    g = (8 * i + r) // 4
                    ins = mm(PS[:, 6, r * HD:(r + 1) * HD], PT[r % 2][:, r // 2, :], Vs[:, g * HD:(g + 1) * HD],
                             start=True, stop=True)
                ins.then_inc(pv_full, 1)

            def o_t(b, i, waits=()):
                pe.wait_ge(o_taken, b * 4 + (i + 1))
                for s, v in waits:
                    need(pe, s, v)
                if i:
                    pe.wait_ge(ot_taken, b * 4 + i)
                for q in range(4):
                    ins = tr(PS[:, 7, q * P:(q + 1) * P], On[:, q * P:(q + 1) * P], ident[:])
                ins.then_inc(ot_full, 1)

            def w_o(b, last):
                pe.wait_ge(ot_taken, b * 4 + 4)
                if not last:
                    pe.wait_ge(rope_taken, b * 5 + 10)
                for t in range(16):
                    ins = mm(PS[:, 2, 0:D], OT[:, t, :], WO[:, t, :], start=(t == 0), stop=(t == 15))
                ins.then_inc(wo_full, 1)

            def h2_t(b, waits):
                pe.wait_ge(row_feat, b + 1)
                for s, v in waits:
                    need(pe, s, v)
                for k in range(2):
                    ins = tr(PS[:, 7, k * P:(k + 1) * P], HR1[:, 0, k * P:(k + 1) * P], ident[:])
                ins.then_inc(ht_full[1], 1)

            def logits(b):
                pe.wait_ge(ht_taken[1], b + 1)
                for k in range(2):
                    ins = mm(PS[:, 7, 0:E], h2T[:, k, :], wg_s[:, k, :], start=(k == 0), stop=(k == 1))
                ins.then_inc(lg_full[1], 1)

            def rank1(b):
                pe.wait_ge(lg_taken[1], b + 1)
                pe.wait_ge(m_ready[1], b + 1)
                rank(1, 1, PS[:, 7, :], E)

            mix(0)
            if stage >= 2:
                pe.wait_ge(x_done, 8)
                ffn0()
                moe(0)
            if stage >= 3:
                pe.wait_ge(moe_done[0], 1)
                mix(1)
            if stage >= 4:
                pe.wait_ge(x_done, 16)
                pe.wait_ge(wr_in, 96)
                pe.wait_ge(wo_in, 16)
                pe.wait_ge(misc_in, 48)
                h_t(0, ())
                for c in range(QCH):
                    proj(0, c)
                q_t(0)

                def body(b, first=False, last=False):
                    score(b, 0)
                    if not last:
                        h_t(b + 1, [(ot_taken, b * 4)])
                    if not first:
                        h2_t(b - 1, [(hT_sb, b + 2)] if not last else [(ot_taken, b * 4)])
                    if not last:
                        proj(b + 1, 0)
                    score(b, 1)
                    if not first:
                        logits(b - 1)
                    if not last:
                        proj(b + 1, 1)
                    p_t(b, 0)
                    pv(b, 0)
                    score(b, 2)
                    if not first:
                        rank1(b - 1)
                    if not last:
                        proj(b + 1, 2)
                    o_t(b, 0, [(hT_sb, 2)] if first else [(rk_taken[1], b)])
                    p_t(b, 1)
                    pv(b, 1)
                    score(b, 3)
                    if not last:
                        proj(b + 1, 3)
                    o_t(b, 1)
                    p_t(b, 2)
                    pv(b, 2)
                    if not last:
                        proj(b + 1, 4)
                    o_t(b, 2)
                    p_t(b, 3)
                    pv(b, 3)
                    if not last:
                        proj(b + 1, 5)
                        q_t(b + 1)
                    o_t(b, 3)
                    w_o(b, last)
                body(0, first=True)
                with pe.Fori(1, NB - 1) as b:
                    body(b)
                body(NB - 1, last=True)
                h2_t(NB - 1, [(ot_taken, 4 * NB)])
                logits(NB - 1)
                rank1(NB - 1)
                pe.wait_ge(rk_taken[1], NB)
                pe.wait_ge(pt1_taken, 4 * NB)
                count(1)
                pe.wait_ge(wo_taken, NB)
                moe(1)

        @block.vector
        def _(dve):
            v = nc.vector
            ch = Chain(dve, dve_seq)
            dve.sem_inc(g_taken, 2)
            dve.sem_inc(z_ready, 4)
            dve.sem_inc(dl_ready, 2)
            dve.sem_inc(at_ready, 3)
            dve.wait_ge(consts, 14)
            dve.wait_ge(x_in, 16)
            dve.wait_ge(misc_in, 48)

            def ln_stats(rnd):
                with dve.Fori(0, NB) as b:
                    v.bn_stats(st6[:, ds(b, 1), :].rearrange("p b f -> p (b f)"),
                               X[:, ds(b, 1), :].rearrange("p b l -> p (b l)")).then_inc(st_done, 1)
                dve.wait_ge(st_done, NB * (rnd + 1))
                ch.link(v.tensor_tensor(s12[:], st6[:, :, 1:3], st6[:, :, 4:6], ALU.add))
                ch.link(v.tensor_tensor(dd, st6[:, :, 1], st6[:, :, 4], ALU.subtract))
                ch.link(v.tensor_scalar(MEAN, s12[:, :, 0], 0.5, None, ALU.mult))
                ch.link(v.tensor_tensor(dd, dd, dd, ALU.mult))
                ch.link(v.tensor_scalar(M2, s12[:, :, 1], 1.0 / D, None, ALU.mult))
                ch.link(v.scalar_tensor_tensor(out=VAR, in0=dd, scalar=0.25, in1=M2, op0=ALU.mult, op1=ALU.add))
                v.tensor_scalar(VE, VAR, EPS, None, ALU.add).then_inc(ve_ready, 1)
                dve.wait_ge(rstd_ready, rnd + 1)

            def mix(n):
                post = cT if n == 0 else vT
                dve.wait_ge(call_in, 16 * (n + 1))
                ln_stats(2 * n)
                with dve.Fori(0, NB // 2) as i:
                    for u in range(2):
                        b = i * 2 + u
                        xb = X[:, ds(b, 1), :].rearrange("p b l -> p (b l)")
                        dve.wait_ge(vt_full, b + (NB * n + 1))
                        v.tensor_scalar(Vb[u], xb, MEAN[:, ds(b, 1)], RSTD[:, ds(b, 1)], ALU.subtract, ALU.mult)\
                            .then_inc(v_ready, 1)
                        dve.wait_ge(v_ready, b + (NB * n + 1))
                        v.scalar_tensor_tensor(out=U[:, ds(b, 1), :].rearrange("p b l -> p (b l)"), in0=Vb[u],
                                               scalar=skip_s[:, n:n + 1],
                                               in1=CALL[:, ds(b, 1), :].rearrange("p b l -> p (b l)"),
                                               op0=ALU.mult, op1=ALU.mult).then_inc(u_ready, 1)
                with dve.Fori(0, 4) as i:
                    for u in range(2):
                        p = i * 2 + u
                        dve.wait_ge(g_full, p + (8 * n + 1))
                        need_prev = 8 * n
                        dve.wait_ge(g_res, p + need_prev)
                        v.tensor_tensor(gtmp[u], PS[:, 2 + u, :].rearrange("p (b l) -> p b l", b=2),
                                        CALL[:, ds(p * 2, 2), :], ALU.mult).then_inc(g_taken, 1)
                        dve.wait_ge(g_taken, p + (8 * n + 3))
                        xp = X[:, ds(p * 2, 2), :]
                        v.tensor_tensor(xp, xp, gtmp[u], ALU.add).then_inc(g_res, 1)
                dve.wait_ge(vt_taken, 2 + NB * (n + 1))
                dve.wait_ge(g_full, 8 * (n + 1))
                dve.wait_ge(g_res, 8 * (n + 1))
                with dve.Fori(0, MH // 2) as i:
                    for u in range(2):
                        h = i * 2 + u
                        for blk in range(2):
                            dve.wait_ge(y_full, h * 2 + (32 * n + blk + 5))
                            dve.wait_ge(dl_ready, h * 2 + (32 * n + blk + 1))
                            a = post[:, blk, :, ds(h * MD, MD)].unsqueeze(3).to_broadcast([P, NB, MD, MD])
                            y = PS[:, 4 * u + 2 * blk:4 * u + 2 * blk + 2, :].rearrange(
                                "p k (b i j) -> p (k b) i j", i=MD, j=MD)
                            v.tensor_tensor(zb[blk].rearrange("p (b i j) -> p b i j", i=MD, j=MD), y, a, ALU.mult)\
                                .then_inc(z_ready, 1)
                        for blk in range(2):
                            dve.wait_ge(z_ready, h * 2 + (32 * n + blk + 5))
                            v.tensor_reduce(dT[:, blk, :, ds(h * MD, MD)],
                                            zb[blk].rearrange("p (b i j) -> p b j i", i=MD, j=MD),
                                            AX.X, ALU.add).then_inc(dl_ready, 1)
                for p in range(8):
                    dve.wait_ge(dt_full, 8 * n + p + 1)
                    xp = X[:, 2 * p:2 * p + 2, :].rearrange("p b l -> p (b l)")
                    v.tensor_tensor(xp, xp, PS[:, p, :], ALU.add).then_inc(x_done, 1)

            def picks(n, nb, logits, r):
                R, k = RB[n], TOPK[n]
                logits.then_inc(lg_taken[n], 1)
                dve.wait_ge(lg_taken[n], r + 1)
                for j in range(nb):
                    settle(dve, dve_settled)
                    ch.link(v.max(R["TV"][:, j, :], R["LG"][:, j, :]))
                    settle(dve, dve_settled)
                    ch.link(v.max_index(TI[n][:, j, :], R["TV"][:, j, :], R["LG"][:, j, :]))
                v.tensor_tensor(R["EX"], R["LG"], R["TV"][:, :, 0:1].to_broadcast([P, nb, E]),
                                ALU.subtract).then_inc(ex_in[n], 1)
                ch.link(v.tensor_copy(R["TIF"], TI[n][:, :, 0:k]))
                ch.link(v.tensor_tensor(
                    R["OH"], iota_e[:].unsqueeze(1).unsqueeze(1).to_broadcast([P, nb, k, E]),
                    R["TIF"].unsqueeze(3).to_broadcast([P, nb, k, E]), ALU.is_equal))
                ch.link(v.tensor_reduce(R["M"], R["OH"].rearrange("p b k e -> p b e k"), AX.X, ALU.add))
                for j in range(nb):
                    ins = v.tensor_tensor(mcum[:, j + 1, :], mcum[:, j, :], R["M"][:, j, :], ALU.add)
                    if j < nb - 1:
                        ch.link(ins)
                ins.then_inc(m_ready[n], 1)

            def places(n, nb, bank, r):
                R, k = RB[n], TOPK[n]
                dve.wait_ge(ex_out[n], r + 1)
                ch.link(v.tensor_tensor(R["EM"], R["EX"], R["M"], ALU.mult))
                ch.link(v.tensor_reduce(R["DEN"], R["EX"] if n == 0 else R["EM"], AX.X, ALU.add))
                ch.link(v.reciprocal(R["RD"], R["DEN"]))
                v.tensor_tensor(HR[n][:, :, D:D + E], R["EM"], R["RD"].unsqueeze(2).to_broadcast([P, nb, E]),
                                ALU.mult).then_inc(row_ready[n], 1)
                dve.wait_ge(rk_full[n], r + 1)
                ch.link(v.tensor_tensor(R["RK"], bank.rearrange("p (b e) -> p b e", e=E),
                                        row_e[:].unsqueeze(1).to_broadcast([P, nb, E]), ALU.add))
                v.tensor_copy(mcum[:, 0, :], mcum[:, nb, :]).then_inc(rk_taken[n], 1)
                ch.link(v.tensor_tensor(R["PR"], R["OH"], R["RK"].unsqueeze(2).to_broadcast([P, nb, k, E]),
                                        ALU.mult))
                ch.link(v.tensor_reduce(R["PF"], R["PR"], AX.X, ALU.add))
                v.tensor_copy(POS[n][:], R["PF"]).then_inc(pos_ready[n], 1)

            def ffn0():
                ch.link(v.memset(mcum[:, 0, :], 0.0))
                ln_stats(1)
                with dve.Fori(0, 4) as gi:
                    ch.enter(gi, 0, 20)
                    dve.wait_ge(scattered[0], gi * (16 * 8))
                    for j in range(4):
                        b = gi * 4 + j
                        xb = X[:, ds(b, 1), :].rearrange("p b l -> p (b l)")
                        v.tensor_copy(HR0[:, j, D + E:XCOLS].bitcast(I32), token_id[:, ds(b, 1)])
                        v.tensor_scalar(HR0[:, j, 0:D], xb, MEAN[:, ds(b, 1)], RSTD[:, ds(b, 1)], ALU.subtract, ALU.mult)\
                            .then_inc(h_ready[0], 1)
                    dve.wait_ge(lg_full[0], gi + 1)
                    lg = v.tensor_copy(RB[0]["LG"], PS[:, 5, 0:64].rearrange("p (b e) -> p b e", e=E))
                    picks(0, 4, lg, gi)
                    for c in range(3):
                        dve.wait_ge(up_full, gi * 3 + (c + 1))
                        dve.wait_ge(sg_ready, gi * 3 + (c + 1))
                        dve.wait_ge(dn_full, gi * 2)
                        r = SCH[c]
                        v.tensor_tensor(aTg[0:r, c, :], sgT[0:r, c, :], PS[0:r, 2 * c + 1, :], ALU.mult)\
                            .then_inc(at_ready, 1)
                    places(0, 4, PS[:, 6, 0:64], gi)
                    for q in range(2):
                        dve.wait_ge(dn_full, gi * 2 + (q + 1))
                        xp = X[:, ds(gi * 4 + 2 * q, 2), :].rearrange("p b l -> p (b l)")
                        v.tensor_tensor(xp, xp, PS[:, 7 - q, :], ALU.add).then_inc(dn_taken, 1)
                ch.leave(4)

            def tables(n):
                dve.wait_ge(cnt_full[n], 1)
                dve.wait_ge(tau_made[n], 1)
                cnt, rem, pad, end, dg, ec = (cnt_s[:, q, :] for q in range(6))
                ch.link(v.tensor_copy(cnt, PS[:, 5, 0:E]))
                ch.link(v.tensor_scalar(cnt_i[:, 0:E], cnt, float(P - 1), None, ALU.add))
                ch.link(v.tensor_scalar(cnt_i[:, E:2 * E], cnt_i[:, 0:E], 7, 7, ALU.arith_shift_right,
                                        ALU.logical_shift_left))
                ch.link(v.tensor_copy(pad, cnt_i[:, E:2 * E]))
                ch.link(v.tensor_tensor(lep, le_e[:], pad.unsqueeze(1).to_broadcast([P, E, E]), ALU.mult))
                ch.link(v.tensor_reduce(end, lep, AX.X, ALU.add))
                ch.link(v.tensor_scalar(dg, pad, -1.0, float(EROWS), ALU.mult, ALU.add))
                ch.link(v.tensor_tensor(ec, cnt, row_e[:], ALU.add))
                ch.link(v.tensor_copy(tab[0:1, 2 * TMAX + 1:2 * TMAX + 1 + E], ec[0:1, :]))
                ch.link(v.tensor_tensor(tcmp, ttau.unsqueeze(2).to_broadcast([1, TMAX, E]),
                                        end[0:1, :].unsqueeze(1).to_broadcast([1, TMAX, E]), ALU.is_ge))
                ch.link(v.tensor_reduce(ter[:, 0, :], tcmp[:, :, 0:E - 1], AX.X, ALU.add))
                ch.link(v.tensor_tensor(tcmp, tcmp, dg[0:1, :].unsqueeze(1).to_broadcast([1, TMAX, E]), ALU.mult))
                ch.link(v.tensor_reduce(ter[:, 1, :], tcmp, AX.X, ALU.add))
                ch.link(v.tensor_tensor(ter[:, 1, :], ter[:, 1, :], ttau, ALU.add))
                ch.link(v.tensor_scalar(ter[:, 1, :], ter[:, 1, :], float(DUMMY), None, ALU.min))
                ch.link(v.tensor_copy(tab[0:1, 0:2 * TMAX], ter.rearrange("p a t -> p (a t)")))
                ch.link(v.tensor_scalar(n_pair[:], end[0:1, E - 1:E], float(P), None, ALU.add))
                v.tensor_scalar(tab[0:1, 2 * TMAX:2 * TMAX + 1], n_pair[:], 8, None, ALU.arith_shift_right)\
                    .then_inc(tab_ready[n], 1)

            def moe(n):
                m = ML[n]
                inter, kr = INTER[n], KROWS[n]

                def act_of(t, i, u):
                    e = dve.value_load(tab[0:1, ds(t, 1)], min_val=0, max_val=E - 1)
                    dve.wait_ge(xin[n][u], i * 16 + 16)
                    if isinstance(t, int):
                        pass
                    else:
                        dve.wait_ge(m["ok"], t + 1)
                    v.tensor_copy(meta[u], xt[u][:, D:XCOLS]).then_inc(m["meta"], 1)
                    dve.wait_ge(m["meta"], t + 1)
                    dve.wait_ge(m["silu"], t + 1)
                    need(dve, m["t2_full"], t - 1)
                    v.scalar_tensor_tensor(out=am[u][:, 0:inter], in0=sg[u][:, 0:inter],
                                           scalar=meta[u][:, ds(e, 1)], in1=PS[:, 2 + u, inter:2 * inter],
                                           op0=ALU.mult, op1=ALU.mult).then_inc(m["act"], 1)

                dve.sem_inc(m["at"], 1)
                dve.wait_ge(tab_ready[n], 1)
                act_of(0, 0, 0)
                pairs = dve.value_load(tab[0:1, 2 * TMAX:2 * TMAX + 1], min_val=1, max_val=TILES[n] // 2 + 1)
                with dve.Fori(0, pairs) as i:
                    for u in range(2):
                        t = i * 2 + u
                        dve.wait_ge(m["t2_full"], t + 1)
                        dve.wait_ge(m["down_full"], t)
                        v.tensor_copy(aTt[0:kr], PS[0:kr, 4 + u, 0:D].rearrange("p (k s) -> p k s", k=2))\
                            .then_inc(m["at"], 1)
                        act_of(t + 1, i + u, 1 - u)

            def front(b):
                xb = X[:, ds(b, 1), :].rearrange("p b l -> p (b l)")
                xd = XD[:, ds(b % 4, 1), :].rearrange("p b l -> p (b l)")
                ch.link(v.tensor_scalar(xd, xb, MEAN[:, ds(b, 1)], RSTD[:, ds(b, 1)], ALU.subtract, ALU.mult))
                need(dve, hT_full, b)
                v.scalar_tensor_tensor(out=Hd, in0=xd, scalar=RMS[:, ds(b, 1)], in1=lnw_s, op0=ALU.mult, op1=ALU.mult)\
                    .then_inc(h_ready[1], 1)
                v.tensor_tensor(xb, xb, xd, ALU.add).then_inc(f_res, 1)

            def rope(b, c):
                dve.wait_ge(proj_full, b * 6 + (c + 1))
                need(dve, qt_full, b * 6)
                need(dve, rp_ready, b * 5 + (c - 1))
                ps = PS[:, 2 + c % 2, :].rearrange("p (h a d) -> p h a d", h=8, a=2)
                dst = (Qr[:, c * 512:(c + 1) * 512] if c < 4 else KA).rearrange("p (h d) -> p h d", h=8)
                bt = Bt[c % 2].rearrange("p (h a d) -> p h a d", h=8, a=2)
                H2 = HD // 2
                v.tensor_tensor(dst, PS[:, 2 + c % 2, :].rearrange("p (h d) -> p h d", h=8),
                                cos_s.unsqueeze(1).to_broadcast([P, 8, HD]), ALU.mult)
                v.tensor_tensor(bt[:, :, 0, :], ps[:, :, 1, :],
                                sin_s[:, 0:H2].unsqueeze(1).to_broadcast([P, 8, H2]), ALU.mult)
                v.tensor_tensor(bt[:, :, 1, :], ps[:, :, 0, :],
                                sin_s[:, H2:HD].unsqueeze(1).to_broadcast([P, 8, H2]), ALU.mult)\
                    .then_inc(rope_taken, 1)

            def qk_sb(b, s):
                dve.wait_ge(qt_full, b * 6 + (s + 1))
                need(dve, s_full, b * 8)
                src = PS[:, [0, 1, 4, 5, 0, 1][s], :].rearrange("p (r q) -> p r q", r=4)
                dst = qT[:, 4 * s:4 * s + 4, :] if s < 4 else kTd[:, 4 * (s - 4):4 * (s - 3), :]
                v.tensor_copy(dst, src).then_inc(qkd_sb, 1)

            def masked(b, i):
                need(dve, pt_full, b * 8 + (2 * i - 2))
                for par in range(2):
                    dve.wait_ge(s_full, b * 8 + (2 * i + par + 1))
                    v.tensor_tensor(SM[i % 2][par], PS[:, par, :].rearrange("p (r q) -> p r q", r=4),
                                    maskneg.unsqueeze(1).to_broadcast([P, 4, P]), ALU.add).then_inc(sm_taken, 1)
                for par in range(2):
                    dve.wait_ge(sm_taken, b * 8 + (2 * i + par + 1))
                    v.tensor_reduce(mx[i % 2][:, par, :], SM[i % 2][par], AX.X, ALU.max).then_inc(mx_ready, 1)
                dve.wait_ge(mx_ready, b * 8 + (2 * i + 2))
                v.tensor_scalar(nbias[i % 2], mx[i % 2], -(HD ** -0.5), None, ALU.mult).then_inc(nb_ready, 1)

            def pt1(b, i):
                dve.wait_ge(pt_full, b * 8 + (2 * i + 2))
                need(dve, pv_full, b * 4 + i)
                v.tensor_copy(PT[1], PS[:, 5, :].rearrange("p (r q) -> p r q", r=4)).then_inc(pt1_taken, 1)
                dve.wait_ge(ex_ready, b * 4 + (i + 1))
                v.reciprocal(rinv[i % 2], rs[i % 2]).then_inc(ri_ready, 1)

            def o_norm(b, i):
                dve.wait_ge(pv_full, b * 4 + (i + 1))
                dve.wait_ge(ri_ready, b * 4 + (i + 1))
                need(dve, ot_full, b * 4 + i)
                o4 = PS[:, 6, :].rearrange("p (q a d) -> p q a d", q=4, a=2)
                d4 = On.rearrange("p (q a d) -> p q a d", q=4, a=2)
                r4 = rinv[i % 2].rearrange("p a q -> p q a").unsqueeze(3).to_broadcast([P, 4, 2, HD])
                v.tensor_tensor(d4, o4, r4, ALU.mult).then_inc(o_taken, 1)

            def post(b):
                dve.wait_ge(wo_full, b + 1)
                dve.wait_ge(f_res, b + 1)
                xb = X[:, ds(b, 1), :].rearrange("p b l -> p (b l)")
                xd = XD[:, ds(b % 4, 1), :].rearrange("p b l -> p (b l)")
                v.tensor_tensor(xb, xb, PS[:, 2, 0:D], ALU.add)
                v.tensor_tensor(X2, xd, PS[:, 2, 0:D], ALU.add).then_inc(wo_taken, 1)
                dve.wait_ge(wo_taken, b + 1)
                ch.link(v.tensor_tensor_reduce(junk, X2, X2, 1.0 / D, 0.0, ALU.mult, ALU.add, rms[:, 0:1]))
                v.tensor_scalar(rms[:, 1:2], rms[:, 0:1], EPS, None, ALU.add).then_inc(rq_ready, 1)
                dve.wait_ge(rr_ready, b + 1)
                need(dve, scattered[1], b * 64)
                v.tensor_copy(HR1[:, 0, D + E:XCOLS].bitcast(I32), token_id[:, ds(b, 1)])
                v.scalar_tensor_tensor(out=HR1[:, 0, 0:D], in0=X2, scalar=rms[:, 2:3], in1=fflnw_s,
                                       op0=ALU.mult, op1=ALU.mult).then_inc(row_feat, 1)

            def picks1(b):
                dve.wait_ge(lg_full[1], b + 1)
                lg = v.tensor_copy(RB[1]["LG"], PS[:, 7, 0:E].unsqueeze(1))
                picks(1, 1, lg, b)

            mix(0)
            if stage >= 2:
                ffn0()
                tables(0)
                moe(0)
            if stage >= 3:
                dve.wait_ge(x_back, 16)
                mix(1)
            if stage >= 4:
                ch.link(v.memset(mcum[:, 0, :], 0.0))
                dve.wait_ge(d_in, 64)
                dve.wait_ge(consts, 16)
                ln_stats(3)
                ch.link(v.tensor_tensor(dd, RSTD, RSTD, ALU.mult))
                ch.link(v.tensor_tensor(dd, dd, VAR, ALU.mult))
                v.tensor_scalar(VE, dd, EPS, None, ALU.add).then_inc(ve_ready, 1)
                dve.wait_ge(rstd_ready, 5)
                front(0)
                front(1)
                for c in range(5):
                    rope(0, c)
                for s in (1, 3, 5):
                    qk_sb(0, s)

                def body(b, first=False, last=False, two=True):
                    masked(b, 0)
                    if not first:
                        post(b - 1)
                    if not last:
                        rope(b + 1, 0)
                    masked(b, 1)
                    if not first:
                        picks1(b - 1)
                    if not last:
                        rope(b + 1, 1)
                    pt1(b, 0)
                    o_norm(b, 0)
                    masked(b, 2)
                    if not last:
                        rope(b + 1, 2)
                    if not first:
                        places(1, 1, PS[:, 7, 0:E], b - 1)
                    pt1(b, 1)
                    o_norm(b, 1)
                    masked(b, 3)
                    if not last:
                        rope(b + 1, 3)
                    pt1(b, 2)
                    o_norm(b, 2)
                    if not last:
                        rope(b + 1, 4)
                    pt1(b, 3)
                    o_norm(b, 3)
                    if two:
                        front(b + 2)
                    if not last:
                        for s in (1, 3, 5):
                            qk_sb(b + 1, s)
                body(0, first=True)
                with dve.Fori(1, NB - 2) as b:
                    ch.enter(b, 1, 13)
                    body(b)
                ch.leave(NB - 2)
                body(NB - 2, two=False)
                body(NB - 1, last=True, two=False)
                post(NB - 1)
                picks1(NB - 1)
                places(1, 1, PS[:, 7, 0:E], NB - 1)
                tables(1)
                moe(1)


_NAMES = ["x", "ctx", "conv_k", "skip", "gate_t", "gu", "dn", "sgu", "sdn", "dvec", "lnw", "fflnw",
          "wq", "wk", "wv", "wo", "wg", "w1", "w3", "w2", "cos", "sin"]


def rope_tables():
    half = HD // 2
    inv = (np.float32(1.0) / np.float32(150000.0) ** (np.arange(half, dtype=np.float32) / np.float32(half)))
    ang = np.arange(P, dtype=np.float32)[:, None] * inv.astype(np.float32)
    c, s = np.cos(ang).astype(np.float32), np.sin(ang).astype(np.float32)
    return np.concatenate([c, c], -1), np.concatenate([-s, s], -1)


def kernel(x, fside_S2_0, ctx_2048, L0_xattn_k, L0_ffn_gate_w, L0_ffn_w_gate_up, L0_ffn_w_down,
           L0_ffn_shared_gate_up, L0_ffn_shared_down, L1_xattn_ssm_kernel, L1_xattn_D, L1_ffn_ln_w,
           L1_ffn_ff_ln_w, L1_ffn_wq, L1_ffn_wk, L1_ffn_wv, L1_ffn_wo, L1_ffn_wg, L1_ffn_w1, L1_ffn_w3,
           L1_ffn_w2, _stage=4):
    import concourse.bacc as bacc
    from concourse.bass_utils import run_bass_kernel_spmd

    cos, sin = rope_tables()
    host = [x, ctx_2048, np.concatenate([np.asarray(L0_xattn_k), np.asarray(L1_xattn_ssm_kernel)]), fside_S2_0,
            np.asarray(L0_ffn_gate_w).T, L0_ffn_w_gate_up, L0_ffn_w_down, L0_ffn_shared_gate_up,
            L0_ffn_shared_down, L1_xattn_D, L1_ffn_ln_w, L1_ffn_ff_ln_w, L1_ffn_wq, L1_ffn_wk, L1_ffn_wv,
            L1_ffn_wo, L1_ffn_wg, L1_ffn_w1, L1_ffn_w3, L1_ffn_w2, cos, sin]
    nc = bacc.Bacc("TRN2", target_bir_lowering=False, num_devices=1)
    arrays, args = {}, []
    for name, a in zip(_NAMES, host):
        a = np.ascontiguousarray(a)
        arrays[f"in_{name}"] = a
        args.append(nc.dram_tensor(f"in_{name}", a.shape, mybir.dt.from_np(a.dtype), kind="ExternalInput").ap())
    out = nc.dram_tensor("out_0", (NB, P, D), F32, kind="ExternalOutput").ap()
    program(nc, *args, out, stage=_stage)
    r = run_bass_kernel_spmd(nc, [arrays], core_ids=[0])
    return r.results[0]["out_0"]
```

```python
from contextlib import ExitStack

import numpy as np

import concourse.bass as bass
from concourse import mybir

F32 = mybir.dt.float32
I32 = mybir.dt.int32
U32 = mybir.dt.uint32
ALU = mybir.AluOpType
ACT = mybir.ActivationFunctionType
AX = mybir.AxisListType

P = 128
NB = 16
D = 256
EPS = 1e-5

MH = 16
MD = 8

E = 16
TOPK = [2, 4]
INTER = [176, 256]
KROWS = [88, 128]
SI = 352
SCH = [128, 128, 96]

QH, KH, HD = 32, 8, 64
QCH = 6

EROWS = NB * P + P
DUMMY = E * EROWS
XROWS = DUMMY + P
XCOLS = D + E + 1
NTOK = NB * P
TILES = [NTOK * k // P + E for k in TOPK]
TMAX = max(TILES) + 4


def ds(start, size):
    return bass.ds(start, size)


def program(nc, x, ctx, conv_k, skip, gate_t, gu, dn, sgu, sdn, dvec, lnw, fflnw,
            wq, wk, wv, wo, wg, w1, w3, w2, cos, sin, out, stage=4):
    es = ExitStack()
    with es:
        def sb(name, shape, dt=F32):
            return es.enter_context(nc.sbuf_tensor(name, shape, dt))

        def sem(name):
            return es.enter_context(nc.semaphore(name))

        PS = es.enter_context(nc.psum_tensor("PS", [P, 8, 512], F32))

        X = sb("X", [P, NB, D])
        WREG = sb("WREG", [P, 24576])
        WOR = sb("WOR", [P, 16 * D])
        SCR = sb("SCR", [P, 17600])
        ident = sb("ident", [P, P])
        tri = sb("tri", [P, P])
        ones = sb("ones", [P, P])
        group = sb("group", [P, P])
        iota_e = sb("iota_e", [P, E])
        row_e = sb("row_e", [P, E])
        le_e = sb("le_e", [P, E, E])
        token_id = sb("token_id", [P, NB], I32)
        zrow = sb("zrow", [P, XCOLS])
        skip_s = sb("skip_s", [P, 2])
        wg_s = sb("wg_s", [P, 2, E])
        st6 = sb("st6", [P, NB, 6])
        lnv = sb("lnv", [P, 8, NB])
        s2, dd, MEAN, M2, VAR, VE, RSTD, RMS = (lnv[:, q, :] for q in range(8))
        s12 = sb("s12", [P, NB, 2])
        X2 = sb("X2", [P, D])
        mhalf = sb("mhalf", [P, NB])
        rms = sb("rms", [P, 3])
        mcum = sb("mcum", [P, 5, E])
        tab = sb("tab", [1, 2 * TMAX + 1 + E], I32)
        cnt_s = sb("cnt_s", [P, 6, E])
        n_pair = sb("n_pair", [1, 1], I32)
        cnt_i = sb("cnt_i", [P, 2 * E], I32)

        def carve(region, at, *dims, parts=P):
            n = int(np.prod(dims))
            v = region[0:parts, at:at + n]
            if len(dims) == 2:
                v = v.rearrange("p (a b) -> p a b", a=dims[0])
            elif len(dims) == 3:
                v = v.rearrange("p (a b c) -> p a b c", a=dims[0], b=dims[1])
            elif len(dims) == 4:
                v = v.rearrange("p (a b c d) -> p a b c d", a=dims[0], b=dims[1], c=dims[2])
            return v

        GU = carve(WREG, 0, 2, E, 2 * INTER[0])
        DN = carve(WREG, 11264, 2, E, D, parts=88)
        SGU = carve(WREG, 19456, 2, 2 * SI)
        SDN = carve(WREG, 20864, 3, D)
        GT0 = carve(WREG, 21632, 2, E)
        W13 = carve(WREG, 0, 2, E, 2 * INTER[1])
        W2 = carve(WREG, 16384, 2, E, D)
        WQ = carve(WREG, 16384, 2, QH * HD)
        WK = carve(WREG, 20480, 2, KH * HD)
        WV = carve(WREG, 21504, 2, KH * HD)

        WO = carve(WOR, 0, 16, D)
        cT = carve(SCR, 0, 2, NB, P)
        vT = carve(SCR, 4096, 2, NB, P)
        dT = carve(SCR, 8192, 2, NB, P)
        U = carve(SCR, 8192, NB, D)
        CALL = carve(SCR, 12288, NB, D)
        kv = [[carve(SCR, 12288 + 2048 * u + 1024 * blk, 1024) for blk in range(2)] for u in range(2)]
        zb = [carve(WOR, 1024 * blk, 1024) for blk in range(2)]
        TZ = [carve(WOR, 2048 + 256 * u, D) for u in range(2)]
        Vb = [carve(SCR, 16384 + 256 * u, D) for u in range(2)]
        Cb = [carve(SCR, 16896 + 256 * u, D) for u in range(2)]
        gtmp = [carve(WOR, 2560 + 512 * u, 2, D) for u in range(2)]

        o = 4096
        HR0 = carve(SCR, o, 4, XCOLS); o += 4 * XCOLS
        hTg = carve(SCR, o, 2, 4 * P); o += 8 * P
        sgT = carve(SCR, o, 3, 4 * P); o += 12 * P
        aTg = carve(SCR, o, 3, 4 * P); o += 12 * P
        assert o <= 10240
        R_AT = [10240, 17240]

        def route_bufs(at, nb, k):
            r = {}
            for name, dims in (("LG", (nb, E)), ("TV", (nb, 8)), ("EX", (nb, E)), ("TIF", (nb, k)),
                               ("OH", (nb, k, E)), ("M", (nb, E)), ("EM", (nb, E)), ("DEN", (nb,)),
                               ("RD", (nb,)), ("RK", (nb, E)), ("RS", (nb, E)), ("PR", (nb, k, E)), ("PF", (nb, k))):
                n = int(np.prod(dims))
                r[name] = carve(SCR, at, *dims)
                at += n
            return r
        RB = [route_bufs(R_AT[0], 4, 2), route_bufs(R_AT[1], 1, 4)]
        TI = [sb("TI0", [P, 4, 8], U32), sb("TI1", [P, 1, 8], U32)]
        POS = [sb("POS0", [P, 4, 2], I32), sb("POS1", [P, 1, 4], I32)]

        o = 11200
        xt = [carve(SCR, o + 280 * u, XCOLS) for u in range(2)]; o += 560
        xTt = [carve(SCR, o + 256 * u, 2, P) for u in range(2)]; o += 512
        sg = [carve(SCR, o + 256 * u, 256) for u in range(2)]; o += 512
        am = [carve(SCR, o + 256 * u, 256) for u in range(2)]; o += 512
        aTt = carve(SCR, o, 2, P); o += 256
        yt = [carve(SCR, o + 256 * u, D) for u in range(2)]; o += 512
        meta = [carve(SCR, o + 20 * u, E + 1) for u in range(2)]; o += 40
        tcmp = carve(SCR, o, TMAX, E, parts=1); o += TMAX * E
        ttau = carve(SCR, o, TMAX, parts=1); o += TMAX
        ter = carve(SCR, o, 2, TMAX, parts=1); o += 2 * TMAX
        lep = carve(SCR, o, E, E); o += E * E
        assert o <= 16384

        o = 0
        cos_s = carve(SCR, o, HD); o += HD
        sin_s = carve(SCR, o, HD); o += HD
        lnw_s = carve(SCR, o, D); o += D
        fflnw_s = carve(SCR, o, D); o += D
        maskneg = carve(SCR, o, P); o += P
        XD = carve(SCR, o, 4, D); o += 4 * D
        Hd = carve(SCR, o, D); o += D
        hT = carve(SCR, o, 2, P); o += 2 * P
        Qr = carve(SCR, o, QH * HD); o += QH * HD
        KA = carve(SCR, o, KH * HD); o += KH * HD
        Bt = [carve(SCR, o + 512 * u, 512) for u in range(2)]; o += 1024
        Kd = carve(SCR, o, KH, 2, HD); o += 2 * KH * HD
        qT = carve(SCR, o, 16, P); o += 16 * P
        kTd = carve(SCR, o, KH, P); o += KH * P
        Vs = carve(SCR, o, 2, KH * HD); o += 2 * KH * HD
        SM = [[carve(SCR, o + 1024 * i + 512 * par, 4, P) for par in range(2)] for i in range(2)]
        o += 2048
        PT = [carve(SCR, o + 512 * par, 4, P) for par in range(2)]; o += 1024
        On = carve(SCR, o, 512); o += 512
        OT = carve(SCR, o, 16, P); o += 16 * P
        mx = [carve(SCR, o + 8 * i, 2, 4) for i in range(2)]; o += 16
        nbias = [carve(SCR, o + 8 * i, 2, 4) for i in range(2)]; o += 16
        rs = [carve(SCR, o + 8 * i, 2, 4) for i in range(2)]; o += 16
        rinv = [carve(SCR, o + 8 * i, 2, 4) for i in range(2)]; o += 16
        h2T = carve(SCR, o, 2, P); o += 2 * P
        HR1 = carve(SCR, o, 1, XCOLS); o += XCOLS
        assert o <= R_AT[1]

        HR = [HR0, HR1]

        kpad = nc.dram_tensor("kpad", [2 * MH, P + D], F32, kind="Internal")
        toe = [nc.dram_tensor(f"toeplitz{n}", [MH, P, D], F32, kind="Internal") for n in range(2)]
        xs = [nc.dram_tensor(f"rows_by_expert{n}", [XROWS, XCOLS], F32, kind="Internal") for n in range(2)]
        acc = [nc.dram_tensor(f"stream{n}", [NTOK + P, D], F32, kind="Internal") for n in range(2)]

        consts = sem("consts_made")
        x_in, misc_in, w0_in = sem("x_in"), sem("misc_in"), sem("w0_in")
        kp_in = sem("kernels_padded")
        toe_out = [sem(f"toeplitz{n}_out") for n in range(2)]
        wd_in, wr_in, w2_in = sem("w13_in"), sem("attention_weights_in"), sem("w2_in")
        wo_in = sem("wo_in")
        d_in = sem("attention_tables_in")
        call_in = sem("ctx_rows_in")
        c_in = [sem(f"ctx_tile{u}_in") for u in range(2)]
        t_in = [sem(f"toeplitz{u}_in") for u in range(2)]
        dve_seq = sem("dve_seq")
        dve_settled, pool_settled = sem("dve_settled"), sem("pool_settled")
        st_done, ve_ready, rstd_ready = sem("stats_done"), sem("variance_ready"), sem("rstd_ready")
        rq_ready, rr_ready = sem("square_ready"), sem("rms_ready")
        v_ready, u_ready = sem("v_ready"), sem("u_ready")
        vt_full, vt_taken = sem("vt_full"), sem("vt_taken")
        g_full, g_taken, g_res = sem("g_full"), sem("g_taken"), sem("g_res")
        kv_ready, y_full, z_ready, dl_ready = sem("kv_ready"), sem("y_full"), sem("z_ready"), sem("delta_ready")
        dt_full, x_done = sem("dt_full"), sem("x_done")
        h_ready = [sem(f"h_ready{n}") for n in range(2)]
        ht_full = sem("ht_full")
        ht_taken = sem("ht_taken")
        lg_full = sem("logits_full")
        lg_taken = sem("logits_taken")
        m_ready = [sem(f"picks_ready{n}") for n in range(2)]
        rk_full = sem("rank_full")
        rk_taken = [sem(f"rank_taken{n}") for n in range(2)]
        ex_in = [sem(f"gate_shifted{n}") for n in range(2)]
        ex_out = [sem(f"gate_exp{n}") for n in range(2)]
        row_ready = [sem(f"row_ready{n}") for n in range(2)]
        pos_ready = [sem(f"pos_ready{n}") for n in range(2)]
        scattered = [sem(f"scattered{n}") for n in range(2)]
        cnt_full = [sem(f"count_full{n}") for n in range(2)]
        tab_ready = [sem(f"tables_ready{n}") for n in range(2)]
        tau_made = [sem(f"tau_made{n}") for n in range(2)]
        pad_in = [sem(f"padding_in{n}") for n in range(2)]
        acc_in = [sem(f"stream_out{n}") for n in range(2)]
        up_full, sg_ready, at_ready, dn_full, dn_taken = (
            sem("shared_up_full"), sem("shared_silu"), sem("shared_act"), sem("shared_down_full"),
            sem("shared_down_taken"))
        names = ("ok", "t1_full", "xt_ready", "up_full", "silu", "meta", "act", "t2_full", "at", "down_full", "y")
        ML = [{k: sem(f"moe{n}_{k}") for k in names} for n in range(2)]
        xin = [[sem(f"moe{n}_rows{u}_in") for u in range(2)] for n in range(2)]
        added = [sem(f"moe{n}_added") for n in range(2)]
        moe_done = [sem(f"moe{n}_done") for n in range(2)]
        x_back = sem("x_back")
        side_full, side_taken = sem("side_bank_full"), sem("side_bank_taken")
        proj_full, rope_taken, v_taken, rp_ready = sem("proj_full"), sem("rope_taken"), sem("v_taken"), sem("roped")
        ta_full, ta_taken = sem("turned_full_for_act"), sem("turned_taken_by_act")
        td_full, td_taken = sem("turned_full_for_dve"), sem("turned_taken_by_dve")
        s_full, sm_taken, nb_ready, ex_ready = sem("s_full"), sem("s_masked"), sem("nbias_ready"), sem("exp_ready")
        ri_ready = sem("rinv_ready")
        pv_full, o_taken = sem("pv_full"), sem("o_taken")
        wo_full, wo_taken = sem("wo_full"), sem("wo_taken")
        f_res, row_feat = sem("xd_added"), sem("row_features_ready")
        out_done = sem("out_done")

        def need(eng, s, v):
            if isinstance(v, int) and v <= 0:
                return
            eng.wait_ge(s, v)

        def settle(eng, s):
            eng.sem_inc(s, 1)

        class Chain:

            def __init__(self, eng, s):
                self.eng, self.s, self.base, self.i, self.per, self.k = eng, s, 0, None, 0, 0

            def value(self):
                return self.base + self.k if self.i is None else self.i * self.per + (self.base + self.k)

            def link(self, ins):
                self.k += 1
                ins.then_inc(self.s, 1)
                self.eng.wait_ge(self.s, self.value())

            def enter(self, i, start, per):
                self.base = self.base + self.k - start * per
                self.i, self.per, self.k = i, per, 0

            def leave(self, end):
                assert self.k == self.per, ("per is", self.k)
                self.base, self.i, self.k = self.base + end * self.per, None, 0

        def there(b):
            return not isinstance(b, int) or 0 <= b < NB

        def tally(offsets):
            def through(b, k):
                return sum(1 for s in range(-1, b + 1) for q, o in enumerate(offsets)
                           if 0 <= s + o < NB and (s < b or q < k))

            def value(b, k, shift=0):
                if isinstance(b, int):
                    return through(b + shift, k)
                return b * len(offsets) + (through(2 + shift, k) - 2 * len(offsets))
            return value
        turned = tally((-1, 0, 0, 1, 0, 1, 0, 1))
        side = tally((1, -1, -2, -1, -2, 0, 0, -1))

        def steps(eng, body, chain=None, per=0):
            for b in (-1, 0, 1):
                body(b)
            with eng.Fori(2, NB - 2) as b:
                if chain:
                    chain.enter(b, 2, per)
                body(b)
            if chain:
                chain.leave(NB - 2)
            for b in (NB - 2, NB - 1, NB, NB + 1):
                body(b)

        block = es.enter_context(nc.Block())

        @block.sync
        def _(sp):
            def load_w0():
                sp.dma_start(GT0, gate_t.rearrange("(k p) e -> p k e", p=P)).then_inc(w0_in, 16)
                sp.dma_start(SGU, sgu.rearrange("(k p) j -> p k j", p=P)).then_inc(w0_in, 16)
                sp.dma_start(SDN[:, 0:2, :], sdn[0:2 * P, :].rearrange("(k p) j -> p k j", p=P)).then_inc(w0_in, 16)
                sp.dma_start(SDN[0:96, 2, :], sdn[2 * P:SI, :]).then_inc(w0_in, 16)
                for k in range(2):
                    sp.dma_start(GU[:, k], gu[:, k * P:(k + 1) * P, :].rearrange("e p j -> p e j")).then_inc(w0_in, 16)
                    sp.dma_start(DN[:, k], dn[:, k * 88:(k + 1) * 88, :].rearrange("e p j -> p e j")).then_inc(w0_in, 16)

            def load_w1():
                sp.wait_ge(moe_done[0], 1)
                for k in range(2):
                    r = slice(k * P, (k + 1) * P)
                    sp.dma_start(WQ[:, k], wq[r, :]).then_inc(wr_in, 16)
                    sp.dma_start(WK[:, k], wk[r, :]).then_inc(wr_in, 16)
                    sp.dma_start(WV[:, k], wv[r, :]).then_inc(wr_in, 16)
                for k in range(2):
                    r = slice(k * P, (k + 1) * P)
                    sp.dma_start(W13[:, k, :, 0:D], w1[:, r, :].rearrange("e p j -> p e j")).then_inc(wd_in, 16)
                    sp.dma_start(W13[:, k, :, D:2 * D], w3[:, r, :].rearrange("e p j -> p e j")).then_inc(wd_in, 16)

            def mix(n):
                if n:
                    sp.wait_ge(z_ready, 4 + 32)
                    sp.wait_ge(moe_done[0], 1)
                sp.dma_start(CALL, ctx.rearrange("b p l -> p b l")).then_inc(call_in, 16)
                if n == 0:
                    with sp.Fori(0, NB // 2) as i:
                        for u in range(2):
                            b = i * 2 + u
                            sp.wait_ge(vt_full, b + 1)
                            sp.dma_start(Cb[u], ctx[ds(b, 1)].rearrange("b p l -> p (b l)")).then_inc(c_in[u], 16)
                sp.wait_ge(toe_out[n], 16)
                with sp.Fori(0, MH // 2) as i:
                    for u in range(2):
                        h = i * 2 + u
                        sp.wait_ge(y_full, h * 2 + (32 * n + 2))
                        sp.dma_start(TZ[u], toe[n][ds(h, 1)].rearrange("a p l -> p (a l)")).then_inc(t_in[u], 16)

            def stream_out(n):
                if n == 0:
                    sp.wait_ge(dn_taken, 8)
                else:
                    sp.wait_ge(wo_taken, NB)
                sp.dma_start(acc[n][0:NTOK, :].rearrange("(b p) l -> p b l", p=P), X[:]).then_inc(acc_in[n], 16)
                sp.dma_start(acc[n][NTOK:NTOK + P, :], zrow[:, 0:D]).then_inc(acc_in[n], 16)

            def moe(n):
                m = ML[n]
                per = NB * TOPK[n] * 16
                sp.wait_ge(scattered[n], per)
                sp.dma_start(xs[n][DUMMY:DUMMY + P, :], zrow[:]).then_inc(pad_in[n], 16)
                sp.wait_ge(tab_ready[n], 1)
                with sp.Fori(0, E) as e:
                    r = sp.value_load(tab[0:1, ds(e + (2 * TMAX + 1), 1)], min_val=0, max_val=DUMMY)
                    sp.dma_start(xs[n][ds(r, P), :], zrow[:]).then_inc(pad_in[n], 16)
                sp.wait_ge(pad_in[n], 16 * (E + 1))

                def load(t, u):
                    r = sp.value_load(tab[0:1, ds(t + TMAX, 1)], min_val=0, max_val=DUMMY)
                    sp.dma_start(xt[u], xs[n][ds(r, P), :]).then_inc(xin[n][u], 16)

                load(0, 0)
                load(1, 1)
                pairs = sp.value_load(tab[0:1, 2 * TMAX:2 * TMAX + 1], min_val=1, max_val=TILES[n] // 2 + 1)
                with sp.Fori(0, pairs) as i:
                    for u in range(2):
                        t = i * 2 + u
                        sp.wait_ge(m["t1_full"], t + 1)
                        sp.wait_ge(m["meta"], t + 1)
                        load(t + 2, u)

            sp.dma_start(X[:], x.rearrange("b p l -> p b l")).then_inc(x_in, 16)
            sp.dma_start(skip_s[:, 0:1], skip.rearrange("(p a) -> p a", a=1)).then_inc(misc_in, 16)
            dv = dvec.rearrange("(p a) -> p a", a=1)
            dsrc = bass.AP(tensor=dv.tensor, offset=dv.offset, ap=[[1, MH], [0, MD], [1, 1]])
            sp.dma_start(skip_s[:, 1:2], dsrc).then_inc(misc_in, 16)
            sp.dma_start(wg_s[:], wg.rearrange("(k p) e -> p k e", p=P)).then_inc(misc_in, 16)
            sp.wait_ge(consts, 1)
            sp.dma_start(kpad[:, 0:P], zrow[0:2 * MH, 0:P]).then_inc(kp_in, 16)
            sp.dma_start(kpad[:, P:P + D], conv_k).then_inc(kp_in, 16)
            sp.wait_ge(kp_in, 32)
            for n in range(2):
                k0 = kpad[n * MH:n * MH + 1, P:P + 1]
                src = bass.AP(tensor=k0.tensor, offset=k0.offset, ap=[[P + D, MH], [-1, P], [1, D]])
                sp.dma_start(toe[n][:, :, :], src).then_inc(toe_out[n], 16)
            load_w0()
            mix(0)
            if stage >= 2:
                stream_out(0)
                moe(0)
                sp.wait_ge(moe_done[0], 1)
                sp.dma_start(X[:], acc[0][0:NTOK, :].rearrange("(b p) l -> p b l", p=P)).then_inc(x_back, 16)
            if stage >= 3:
                load_w1()
                mix(1)
            if stage >= 4:
                sp.wait_ge(x_done, 16)
                sp.dma_start(WO, wo.rearrange("(t p) n -> p t n", p=P)).then_inc(wo_in, 16)
                sp.dma_start(cos_s, cos).then_inc(d_in, 16)
                sp.dma_start(sin_s, sin).then_inc(d_in, 16)
                sp.dma_start(lnw_s, lnw.partition_broadcast(P)).then_inc(d_in, 16)
                sp.dma_start(fflnw_s, fflnw.partition_broadcast(P)).then_inc(d_in, 16)
                sp.wait_ge(proj_full, QCH * NB)
                for k in range(2):
                    sp.dma_start(W2[:, k], w2[:, k * P:(k + 1) * P, :].rearrange("e p j -> p e j")).then_inc(w2_in, 16)
                stream_out(1)
                moe(1)
                sp.wait_ge(moe_done[1], 1)
                sp.dma_start(out.rearrange("b p l -> (b p) l"), acc[1][0:NTOK, :]).then_inc(out_done, 16)
            else:
                if stage == 1:
                    sp.wait_ge(x_done, 8)
                elif stage == 2:
                    sp.wait_ge(x_back, 16)
                else:
                    sp.wait_ge(x_done, 16)
                sp.dma_start(out.rearrange("b p l -> p b l"), X[:]).then_inc(out_done, 16)
            sp.wait_ge(out_done, 16)
            sp.wait_ge(w0_in, 16 * 8)
            sp.wait_ge(toe_out[1], 16)
            if stage >= 2:
                sp.wait_ge(acc_in[0], 32)
            if stage >= 4:
                sp.wait_ge(acc_in[1], 32)

        @block.gpsimd
        def _(pool):
            g = nc.gpsimd
            made = [0]

            def mk(ins):
                made[0] += 1
                ins.then_inc(consts, 1)
                pool.wait_ge(consts, made[0])

            mk(g.memset(zrow[:], 0.0))
            mk(g.memset(ones[:], 1.0))
            mk(g.memset(ident[:], 0.0))
            mk(g.affine_select(out=ident[:], in_=ident[:], compare_op=ALU.not_equal, fill=1.0, base=0,
                               pattern=[[-1, P]], channel_multiplier=1))
            mk(g.affine_select(out=tri[:], in_=ones[:], compare_op=ALU.is_gt, fill=0.0, base=0,
                               pattern=[[1, P]], channel_multiplier=-1))
            mk(g.affine_select(out=group[:], in_=ones[:], compare_op=ALU.is_ge, fill=0.0, base=0,
                               pattern=[[-MD, MH], [0, MD]], channel_multiplier=1))
            mk(g.affine_select(out=group[:], in_=group[:], compare_op=ALU.is_ge, fill=0.0, base=MD - 1,
                               pattern=[[MD, MH], [0, MD]], channel_multiplier=-1))
            mk(g.iota(iota_e[:], pattern=[[1, E]], base=0, channel_multiplier=0,
                      allow_small_or_imprecise_dtypes=True))
            mk(g.iota(row_e[:], pattern=[[EROWS, E]], base=0, channel_multiplier=0,
                      allow_small_or_imprecise_dtypes=True))
            mk(g.memset(le_e[:], 1.0))
            mk(g.affine_select(out=le_e[:], in_=le_e[:], compare_op=ALU.is_ge, fill=0.0, base=0,
                               pattern=[[1, E], [-1, E]], channel_multiplier=0))
            mk(g.iota(token_id[:], pattern=[[P, NB]], base=0, channel_multiplier=1))
            pool.wait_ge(kp_in, 32)
            mk(g.iota(zrow[:, D + E:XCOLS].bitcast(I32), pattern=[[0, 1]], base=NTOK, channel_multiplier=1))
            mk(g.memset(mhalf[:], -0.5))
            assert made[0] == 14

            def root(rnd, dst):
                pool.wait_ge(ve_ready, rnd + 1)
                g.tensor_tensor(dst, VE, mhalf[:], ALU.pow).then_inc(rstd_ready, 1)

            def root1(b):
                pool.wait_ge(rq_ready, b + 1)
                g.tensor_tensor(rms[:, 2:3], rms[:, 1:2], mhalf[:, 0:1], ALU.pow).then_inc(rr_ready, 1)

            def mix(n):
                pre = vT if n == 0 else cT
                pool.wait_ge(vt_taken, 2 + NB * (n + 1))
                pool.wait_ge(g_taken, 2 + 8 * (n + 1))
                with pool.Fori(0, MH // 2) as i:
                    for u in range(2):
                        h = i * 2 + u
                        pool.wait_ge(y_full, h * 2 + (32 * n + 2))
                        for blk in range(2):
                            a = pre[:, blk, :, ds(h * MD, MD)].unsqueeze(3).to_broadcast([P, NB, MD, MD])
                            c = cT[:, blk, :, ds(h * MD, MD)].unsqueeze(2).to_broadcast([P, NB, MD, MD])
                            g.tensor_tensor(kv[u][blk].rearrange("p (b i j) -> p b i j", b=NB, i=MD), a, c,
                                            ALU.mult).then_inc(kv_ready, 1)

            def scatter(n, rounds, j_count):
                pool.wait_ge(pos_ready[n], rounds + 1)
                pool.wait_ge(row_ready[n], rounds + 1)
                settle(pool, pool_settled)
                for j in range(j_count):
                    for k in range(TOPK[n]):
                        g.indirect_dma_start(
                            out=xs[n][:, :], out_offset=bass.IndirectOffsetOnAxis(ap=POS[n][:, j, k:k + 1], axis=0),
                            in_=HR[n][:, j, :], in_offset=None).then_inc(scattered[n], 16)

            def moe(n):
                m = ML[n]
                pool.sem_inc(m["ok"], 2)
                pool.wait_ge(acc_in[n], 32)
                pool.wait_ge(tab_ready[n], 1)
                pairs = pool.value_load(tab[0:1, 2 * TMAX:2 * TMAX + 1], min_val=1, max_val=TILES[n] // 2 + 1)
                with pool.Fori(0, pairs) as i:
                    for u in range(2):
                        t = i * 2 + u
                        pool.wait_ge(m["y"], t + 1)
                        settle(pool, pool_settled)
                        settle(pool, pool_settled)
                        g.indirect_dma_start(
                            out=acc[n][:, :], out_offset=bass.IndirectOffsetOnAxis(
                                ap=meta[u][:, E:E + 1].bitcast(I32), axis=0),
                            in_=yt[u], in_offset=None, compute_op=ALU.add).then_inc(added[n], 16)
                        pool.wait_ge(added[n], t * 16 + 16)
                        pool.sem_inc(m["ok"], 1)
                pool.wait_ge(m["act"], pairs * 2 + 1)
                pool.wait_ge(m["xt_ready"], pairs * 2 + 2)
                pool.sem_inc(moe_done[n], 1)

            def tau(n):
                g.iota(ttau, pattern=[[P, TMAX]], base=0, channel_multiplier=0,
                       allow_small_or_imprecise_dtypes=True).then_inc(tau_made[n], 1)

            def rope(p, n):
                if n == 0:
                    need(pool, td_full, turned(p, 2, -1))
                pool.wait_ge(rope_taken, p * 5 + (n + 1))
                if n:
                    q = Qr[:, (n - 1) * 512:n * 512]
                    g.tensor_tensor(q, q, Bt[n % 2], ALU.add).then_inc(rp_ready, 1)
                else:
                    def twice(v):
                        return v.rearrange("p (g d) -> p g d", g=KH).unsqueeze(2).to_broadcast([P, KH, 2, HD])
                    g.tensor_tensor(Kd, twice(KA), twice(Bt[0]), ALU.add).then_inc(rp_ready, 1)

            root(0, RSTD)
            mix(0)
            if stage >= 2:
                root(1, RSTD)
                pool.wait_ge(x_done, 8)
                tau(0)
                with pool.Fori(0, 4) as gi:
                    scatter(0, gi, 4)
                pool.wait_ge(scattered[0], NB * TOPK[0] * 16)
                moe(0)
            if stage >= 3:
                root(2, RSTD)
                mix(1)
            if stage >= 4:
                pool.wait_ge(x_done, 16)
                g.memset(maskneg, 0.0).then_inc(consts, 1)
                pool.wait_ge(consts, 15)
                g.affine_select(out=maskneg, in_=maskneg, compare_op=ALU.is_ge, fill=-1e30, base=0,
                                pattern=[[-1, P]], channel_multiplier=1).then_inc(consts, 1)
                root(3, RSTD)
                root(4, RMS)

                def body(b):
                    if there(b + 1):
                        rope(b + 1, 0)
                        rope(b + 1, 1)
                        rope(b + 1, 2)
                    if there(b - 2):
                        scatter(1, b - 2, 1)
                    if there(b + 1):
                        rope(b + 1, 3)
                    if there(b - 1):
                        root1(b - 1)
                    if there(b + 1):
                        rope(b + 1, 4)
                steps(pool, body)
                pool.wait_ge(wo_taken, NB)
                tau(1)
                moe(1)

        @block.scalar
        def _(act):
            a = nc.scalar
            act.sem_inc(vt_taken, 2)

            def mix(n):
                with act.Fori(0, NB // 2) as i:
                    for u in range(2):
                        b = i * 2 + u
                        act.wait_ge(vt_full, b + (NB * n + 3))
                        src = PS[:, u, :].rearrange("p (c k s) -> p c k s", c=2, k=2)
                        if n == 0:
                            a.copy(cT[:, :, ds(b, 1), :].rearrange("p k b s -> p k (b s)"), src[:, 1])
                        a.copy(vT[:, :, ds(b, 1), :].rearrange("p k b s -> p k (b s)"), src[:, 0])\
                            .then_inc(vt_taken, 1)

            def gate_exp(n, r):
                act.wait_ge(ex_in[n], r + 1)
                a.activation(RB[n]["EX"], RB[n]["EX"], ACT.Exp).then_inc(ex_out[n], 1)

            def ffn0():
                with act.Fori(0, 4) as gi:
                    for j in range(4):
                        if j == 0:
                            act.wait_ge(up_full, gi * 3)
                        act.wait_ge(ht_full, gi * 4 + (j + 1))
                        a.copy(hTg[:, :, j * P:(j + 1) * P],
                               PS[:, 6 + j % 2, 0:D].rearrange("p (k s) -> p k s", k=2)).then_inc(ht_taken, 1)
                    gate_exp(0, gi)
                    for c in range(3):
                        act.wait_ge(up_full, gi * 3 + (c + 1))
                        act.wait_ge(at_ready, gi * 3 + (c + 1))
                        r = SCH[c]
                        a.activation(sgT[0:r, c, :], PS[0:r, 2 * c, :], ACT.Silu).then_inc(sg_ready, 1)

            def moe(n):
                m = ML[n]
                inter = INTER[n]

                def x_t(t, u, first):
                    act.wait_ge(m["t1_full"], t + 1)
                    if not first:
                        act.wait_ge(m["up_full"], t - 1)
                    a.copy(xTt[u], PS[:, u, 0:D].rearrange("p (k s) -> p k s", k=2)).then_inc(m["xt_ready"], 1)

                def silu(t, u):
                    act.wait_ge(m["up_full"], t + 1)
                    need(act, m["act"], t - 1)
                    a.activation(sg[u][:, 0:inter], PS[:, 2 + u, 0:inter], ACT.Silu).then_inc(m["silu"], 1)

                act.wait_ge(tab_ready[n], 1)
                x_t(0, 0, True)
                silu(0, 0)
                x_t(1, 1, True)
                pairs = act.value_load(tab[0:1, 2 * TMAX:2 * TMAX + 1], min_val=1, max_val=TILES[n] // 2 + 1)
                with act.Fori(0, pairs) as i:
                    for u in range(2):
                        t = i * 2 + u
                        silu(t + 1, 1 - u)
                        x_t(t + 2, u, False)
                        act.wait_ge(m["down_full"], t + 1)
                        act.wait_ge(m["ok"], t + 1)
                        a.copy(yt[u], PS[:, 6 + u, 0:D]).then_inc(m["y"], 1)

            def side_copy(b, k, dst, cols, waits=()):
                act.wait_ge(side_full, side(b, k))
                for s, v in waits:
                    need(act, s, v)
                a.copy(dst, PS[:, 7, 0:cols]).then_inc(side_taken, 1)

            def exps(b, i):
                act.wait_ge(nb_ready, b * 4 + (i + 1))
                for r in range(8):
                    par, q = r % 2, r // 2
                    s = SM[i % 2][par][:, q, :]
                    ins = a.activation(s, s, ACT.Exp, bias=nbias[i % 2][:, par, q:q + 1], scale=HD ** -0.5,
                                       accum_out=rs[i % 2][:, par, q:q + 1])
                ins.then_inc(ex_ready, 1)

            def p_t(b, i):
                act.wait_ge(ta_full, turned(b, 2 * i + 1))
                a.copy(PT[0], PS[:, 4, :].rearrange("p (r q) -> p r q", r=4)).then_inc(ta_taken, 1)

            def q_t(b, i):
                c = (i - 1) % 4
                act.wait_ge(ta_full, turned(b, 2 * i + 2))
                a.copy(qT[:, 4 * c:4 * c + 4, :], PS[:, 4, :].rearrange("p (r q) -> p r q", r=4)).then_inc(ta_taken, 1)

            def v_sb(p):
                act.wait_ge(proj_full, p * 6 + 5)
                a.copy(Vs[:, ds(p % 2, 1), :].rearrange("p a d -> p (a d)"), PS[:, 3, :]).then_inc(v_taken, 1)

            def outs(c):
                return OT[:, 4 * c:4 * c + 4, :].rearrange("p r q -> p (r q)")

            mix(0)
            if stage >= 2:
                act.wait_ge(x_done, 8)
                ffn0()
                moe(0)
            if stage >= 3:
                act.wait_ge(moe_done[0], 1)
                mix(1)
            if stage >= 4:
                act.wait_ge(x_done, 16)

                def body(b):
                    for i in range(4):
                        prev = b if i else b - 1
                        coming = b + 1 if i else b
                        if i == 0:
                            if there(b + 1):
                                side_copy(b, 1, hT.rearrange("p k s -> p (k s)"), D)
                            if there(b - 1):
                                side_copy(b, 2, outs(2), 512)
                        if i == 1 and there(b - 1):
                            side_copy(b, 4, outs(3), 512)
                        if i >= 2 and there(b):
                            side_copy(b, 4 + i, outs(i - 2), 512)
                        if i == 1 and there(b - 2):
                            gate_exp(1, b - 2)
                        if i == 3 and there(b + 1):
                            v_sb(b + 1)
                        if there(prev):
                            p_t(b, i)
                        if i == 0 and there(b - 2):
                            side_copy(b, 3, RB[1]["LG"].rearrange("p b e -> p (b e)"), E,
                                      [(m_ready[1], b - 2)])
                        if i == 1 and there(b - 2):
                            side_copy(b, 5, RB[1]["RS"].rearrange("p b e -> p (b e)"), E)
                        if there(b):
                            exps(b, i)
                        if i == 3 and there(b - 1):
                            side_copy(b, 8, h2T.rearrange("p k s -> p (k s)"), D)
                        if there(coming):
                            q_t(b, i)
                steps(act, body)
                moe(1)

        @block.tensor
        def _(pe):
            mm, tr = nc.tensor.matmul, nc.tensor.transpose
            pe.sem_inc(vt_full, 2)
            pe.sem_inc(y_full, 4)
            pe.wait_ge(consts, 14)

            def mix(n):
                with pe.Fori(0, NB // 2) as i:
                    for u in range(2):
                        b = i * 2 + u
                        pe.wait_ge(v_ready, b + (NB * n + 1))
                        pe.wait_ge(vt_taken, b + (NB * n + 1))
                        if n == 0:
                            pe.wait_ge(c_in[u], i * 16 + 16)
                            for k in range(2):
                                tr(PS[:, u, D + k * P:D + (k + 1) * P], Cb[u][:, k * P:(k + 1) * P], ident[:])
                        for k in range(2):
                            ins = tr(PS[:, u, k * P:(k + 1) * P], Vb[u][:, k * P:(k + 1) * P], ident[:])
                        ins.then_inc(vt_full, 1)
                with pe.Fori(0, 4) as i:
                    for u in range(2):
                        p = i * 2 + u
                        pe.wait_ge(u_ready, p * 2 + (NB * n + 2))
                        pe.wait_ge(g_taken, p + (8 * n + 1))
                        mm(PS[:, 2 + u, :], group[:], U[:, ds(p * 2, 2), :].rearrange("p b l -> p (b l)"),
                           start=True, stop=True).then_inc(g_full, 1)
                pe.wait_ge(vt_taken, 2 + NB * (n + 1))
                pe.wait_ge(g_taken, 2 + 8 * (n + 1))
                with pe.Fori(0, MH // 2) as i:
                    for u in range(2):
                        h = i * 2 + u
                        pe.wait_ge(t_in[u], i * 16 + (MH // 2 * 16 * n + 16))
                        for blk in range(2):
                            pe.wait_ge(kv_ready, h * 2 + (32 * n + blk + 1))
                            pe.wait_ge(z_ready, h * 2 + (32 * n + blk + 1))
                            for half in range(2):
                                bank = PS[:, 4 * u + 2 * blk + half, :]
                                c = slice(512 * half, 512 * half + 512)
                                if blk:
                                    mm(bank, TZ[u][:, P:D], kv[u][0][:, c], start=True, stop=False)
                                ins = mm(bank, TZ[u][:, 0:P], kv[u][blk][:, c], start=(blk == 0), stop=True)
                            ins.then_inc(y_full, 1)
                pe.wait_ge(z_ready, 4 + 32 * (n + 1))
                pe.wait_ge(dl_ready, 2 + 32 * (n + 1))
                for p in range(8):
                    for q in range(4):
                        ins = tr(PS[:, p, q * P:(q + 1) * P], dT[:, q % 2, 2 * p + q // 2, :], ident[:])
                    ins.then_inc(dt_full, 1)

            def rank(n, nb, bank, cols, full):
                mm(bank[:, 0:cols], tri[:], RB[n]["M"].rearrange("p b e -> p (b e)"), start=True, stop=False)
                mm(bank[:, 0:cols], ones[:], mcum[:, 0:nb, :].rearrange("p b e -> p (b e)"),
                   start=False, stop=True).then_inc(full, 1)

            def ffn0():
                pe.wait_ge(w0_in, 16 * 8)
                with pe.Fori(0, 4) as gi:
                    for j in range(4):
                        pe.wait_ge(h_ready[0], gi * 4 + (j + 1))
                        if j == 0:
                            pe.wait_ge(dn_taken, gi * 2)
                            pe.wait_ge(rk_taken[0], gi)
                        if j >= 2:
                            pe.wait_ge(ht_taken, gi * 4 + (j - 1))
                        for k in range(2):
                            ins = tr(PS[:, 6 + j % 2, k * P:(k + 1) * P], HR0[:, j, k * P:(k + 1) * P], ident[:])
                        ins.then_inc(ht_full, 1)
                    pe.wait_ge(at_ready, gi * 3 + 3)
                    for j in range(4):
                        pe.wait_ge(ht_taken, gi * 4 + (j + 1))
                        for k in range(2):
                            ins = mm(PS[:, 5, j * E:(j + 1) * E], hTg[:, k, j * P:(j + 1) * P], GT0[:, k, :],
                                     start=(k == 0), stop=(k == 1))
                    ins.then_inc(lg_full, 1)
                    for c in range(3):
                        pe.wait_ge(at_ready, gi * 3 + (c + 1))
                        if c == 1:
                            pe.wait_ge(m_ready[0], gi + 1)
                            rank(0, 4, PS[:, 6, :], 64, rk_full)
                        if c == 2:
                            pe.wait_ge(lg_taken, gi + 1)
                        r = SCH[c]
                        for half in range(2):
                            for k in range(2):
                                c0 = half * SI + c * P
                                ins = mm(PS[0:r, 2 * c + half, :], SGU[:, k, c0:c0 + r], hTg[:, k, :],
                                         start=(k == 0), stop=(k == 1))
                        ins.then_inc(up_full, 1)
                    pe.wait_ge(at_ready, gi * 3 + 6)
                    for j in range(4):
                        if j == 2:
                            pe.wait_ge(rk_taken[0], gi + 1)
                        for c in range(3):
                            r = SCH[c]
                            ins = mm(PS[:, 7 - j // 2, (j % 2) * D:(j % 2 + 1) * D], aTg[0:r, c, j * P:(j + 1) * P],
                                     SDN[0:r, c, :], start=(c == 0), stop=(c == 2))
                        if j % 2:
                            ins.then_inc(dn_full, 1)
                pe.wait_ge(dn_taken, 8)
                count(0)

            def count(n):
                mm(PS[:, 5, 0:E], ones[:], mcum[:, 0, :], start=True, stop=True).then_inc(cnt_full[n], 1)

            def moe(n):
                m = ML[n]
                inter, kr = INTER[n], KROWS[n]
                up = GU if n == 0 else W13
                down = DN if n == 0 else W2

                def expert(t):
                    return pe.value_load(tab[0:1, ds(t, 1)], min_val=0, max_val=E - 1)

                def t1(t, i, u, first):
                    pe.wait_ge(xin[n][u], i * 16 + 16)
                    if not first:
                        pe.wait_ge(m["xt_ready"], t - 1)
                    for k in range(2):
                        ins = tr(PS[:, u, k * P:(k + 1) * P], xt[u][:, k * P:(k + 1) * P], ident[:])
                    ins.then_inc(m["t1_full"], 1)

                def ups(t, u):
                    e = expert(t)
                    pe.wait_ge(m["xt_ready"], t + 1)
                    need(pe, m["act"], t - 1)
                    for k in range(2):
                        ins = mm(PS[:, 2 + u, 0:2 * inter], xTt[u][:, k, :],
                                 up[:, k, ds(e, 1), :].rearrange("p e j -> p (e j)"), start=(k == 0), stop=(k == 1))
                    ins.then_inc(m["up_full"], 1)

                pe.wait_ge(tab_ready[n], 1)
                if n:
                    pe.wait_ge(wd_in, 64)
                t1(0, 0, 0, True)
                ups(0, 0)
                t1(1, 0, 1, True)
                if n:
                    pe.wait_ge(w2_in, 32)
                pairs = pe.value_load(tab[0:1, 2 * TMAX:2 * TMAX + 1], min_val=1, max_val=TILES[n] // 2 + 1)
                with pe.Fori(0, pairs) as i:
                    for u in range(2):
                        t = i * 2 + u
                        ups(t + 1, 1 - u)
                        pe.wait_ge(m["act"], t + 1)
                        pe.wait_ge(m["at"], t)
                        for k in range(2):
                            ins = tr(PS[0:kr, 4 + u, k * P:(k + 1) * P], am[u][:, k * kr:(k + 1) * kr], ident[:])
                        ins.then_inc(m["t2_full"], 1)
                        t1(t + 2, i + 1, u, False)
                        e = expert(t)
                        pe.wait_ge(m["at"], t + 2)
                        pe.wait_ge(m["ok"], t + 1)
                        for k in range(2):
                            ins = mm(PS[:, 6 + u, 0:D], aTt[0:kr, k, :],
                                     down[:, k, ds(e, 1), :].rearrange("p e j -> p (e j)"),
                                     start=(k == 0), stop=(k == 1))
                        ins.then_inc(m["down_full"], 1)

            def side_turn(b, k, src, s, v, n):
                pe.wait_ge(s, v)
                need(pe, side_taken, side(b, k - 1))
                for q in range(n):
                    ins = tr(PS[:, 7, q * P:(q + 1) * P], src[:, q * P:(q + 1) * P], ident[:])
                ins.then_inc(side_full, 1)

            def proj(p, c):
                if c == 0:
                    need(pe, rope_taken, p * 5)
                elif c == 1:
                    need(pe, v_taken, p)
                elif c == 4:
                    need(pe, wo_taken, p - 1)
                else:
                    pe.wait_ge(rope_taken, p * 5 + (c if c < 4 else 4))
                w = WK if c == 0 else WV if c == 5 else WQ[:, :, (c - 1) * 512:c * 512]
                for k in range(2):
                    ins = mm(PS[:, 2 if c in (0, 4) else 3, :], hT[:, k, :], w[:, k, :], start=(k == 0), stop=(k == 1))
                ins.then_inc(proj_full, 1)

            def q_t(b, i, p):
                c = (i - 1) % 4
                pe.wait_ge(rp_ready, p * 5 + (c + 2))
                need(pe, ta_taken, turned(b, 2 * i + 1))
                need(pe, td_taken, turned(b, 2 * i + 1))
                for q in range(4):
                    ins = tr(PS[:, 4, q * P:(q + 1) * P], Qr[:, (4 * c + q) * P:(4 * c + q + 1) * P], ident[:])
                ins.then_inc(ta_full, 1)
                for q in range(2):
                    ins = tr(PS[:, 5, q * P:(q + 1) * P], Kd[:, 2 * c + q].rearrange("p a d -> p (a d)"), ident[:])
                ins.then_inc(td_full, 1)

            def score(b, i):
                v = turned(b, 2 * i + 4, -1) if i < 3 else turned(b, 2)
                pe.wait_ge(ta_taken, v)
                pe.wait_ge(td_taken, v)
                need(pe, sm_taken, b * 8 + 2 * i)
                for r in range(8):
                    h = 8 * i + r
                    par, q = r % 2, r // 2
                    rows = slice(par * HD, par * HD + HD)
                    ins = mm(PS[:, par, q * P:(q + 1) * P], qT[rows, h // 2, :], kTd[rows, h // 4, :],
                             start=True, stop=True)
                    if r >= 6:
                        ins.then_inc(s_full, 1)

            def p_t(b, i):
                pe.wait_ge(ex_ready, b * 4 + i)
                need(pe, ta_taken, turned(b, 2 * i))
                need(pe, td_taken, turned(b, 2 * i))
                for par in range(2):
                    for q in range(4):
                        ins = tr(PS[:, 4 + par, q * P:(q + 1) * P], SM[(i - 1) % 2][par][:, q, :], ident[:])
                    ins.then_inc(td_full if par else ta_full, 1)

            def pv(b, i, p):
                pe.wait_ge(ta_taken, turned(b, 2 * i + 1))
                pe.wait_ge(td_taken, turned(b, 2 * i + 1))
                if i == 1:
                    pe.wait_ge(v_taken, b + 1)
                need(pe, o_taken, b * 4 + (i - 1))
                for r in range(8):
                    g = (8 * ((i - 1) % 4) + r) // 4
                    ins = mm(PS[:, 6, r * HD:(r + 1) * HD], PT[r % 2][:, r // 2, :],
                             Vs[:, ds(p % 2, 1), g * HD:(g + 1) * HD].rearrange("p a d -> p (a d)"),
                             start=True, stop=True)
                ins.then_inc(pv_full, 1)

            def w_o(b, half):
                if half == 0:
                    pe.wait_ge(rope_taken, b * 5 + 6 if there(b + 1) else NB * 5)
                pe.wait_ge(side_taken, side(b, 4 if half else 2))
                for t in range(8 * half, 8 * half + 8):
                    ins = mm(PS[:, 2, 0:D], OT[:, t, :], WO[:, t, :], start=(t == 0), stop=(t == 15))
                if half:
                    ins.then_inc(wo_full, 1)

            def logits(b):
                need(pe, side_taken, side(b, 2))
                for k in range(2):
                    ins = mm(PS[:, 7, 0:E], h2T[:, k, :], wg_s[:, k, :], start=(k == 0), stop=(k == 1))
                ins.then_inc(side_full, 1)

            def rank1(b):
                pe.wait_ge(m_ready[1], b - 1)
                need(pe, side_taken, side(b, 4))
                rank(1, 1, PS[:, 7, :], E, side_full)

            mix(0)
            if stage >= 2:
                pe.wait_ge(x_done, 8)
                ffn0()
                moe(0)
            if stage >= 3:
                pe.wait_ge(moe_done[0], 1)
                mix(1)
            if stage >= 4:
                pe.wait_ge(x_done, 16)
                pe.wait_ge(wr_in, 96)
                pe.wait_ge(wo_in, 16)
                pe.wait_ge(misc_in, 48)

                def body(b):
                    for i in range(4):
                        prev = b if i else b - 1
                        coming = b + 1 if i else b
                        if i == 0 and there(b + 1):
                            side_turn(b, 1, Hd, h_ready[1], b + 2, 2)
                        if there(b):
                            score(b, i)
                        last = b if i > 1 else b - 1
                        if there(last):
                            side_turn(b, (2, 4, 6, 7)[i], On, o_taken, b * 4 + (i - 1), 4)
                        if i == 0 and there(b + 1):
                            pe.wait_ge(side_taken, side(b, 1))
                            proj(b + 1, 0)
                        if i in (1, 2) and there(b - 1):
                            w_o(b, i - 1)
                        if i == 3 and there(b + 1):
                            proj(b + 1, 5)
                        if there(prev):
                            p_t(b, i)
                        if i == 0 and there(b - 2):
                            logits(b)
                        if i == 1 and there(b - 2):
                            rank1(b)
                        if there(b + 1):
                            proj(b + 1, i + 1)
                        if i == 3 and there(b - 1):
                            side_turn(b, 8, HR1[:, 0, 0:D], row_feat, b, 2)
                        if there(prev):
                            pv(b, i, prev)
                        if there(coming):
                            q_t(b, i, coming)
                steps(pe, body)
                pe.wait_ge(side_taken, side(NB + 1, 8))
                pe.wait_ge(rk_taken[1], NB)
                pe.wait_ge(td_taken, turned(NB + 1, 8))
                count(1)
                pe.wait_ge(wo_taken, NB)
                moe(1)

        @block.vector
        def _(dve):
            v = nc.vector
            ch = Chain(dve, dve_seq)
            dve.sem_inc(g_taken, 2)
            dve.sem_inc(z_ready, 4)
            dve.sem_inc(dl_ready, 2)
            dve.sem_inc(at_ready, 3)
            dve.wait_ge(consts, 14)
            dve.wait_ge(x_in, 16)
            dve.wait_ge(misc_in, 48)

            def ln_stats(rnd):
                with dve.Fori(0, NB) as b:
                    v.bn_stats(st6[:, ds(b, 1), :].rearrange("p b f -> p (b f)"),
                               X[:, ds(b, 1), :].rearrange("p b l -> p (b l)")).then_inc(st_done, 1)
                dve.wait_ge(st_done, NB * (rnd + 1))
                ch.link(v.tensor_tensor(s12[:], st6[:, :, 1:3], st6[:, :, 4:6], ALU.add))
                ch.link(v.tensor_tensor(dd, st6[:, :, 1], st6[:, :, 4], ALU.subtract))
                ch.link(v.tensor_scalar(MEAN, s12[:, :, 0], 0.5, None, ALU.mult))
                ch.link(v.tensor_tensor(dd, dd, dd, ALU.mult))
                ch.link(v.tensor_scalar(M2, s12[:, :, 1], 1.0 / D, None, ALU.mult))
                ch.link(v.scalar_tensor_tensor(out=VAR, in0=dd, scalar=0.25, in1=M2, op0=ALU.mult, op1=ALU.add))
                v.tensor_scalar(VE, VAR, EPS, None, ALU.add).then_inc(ve_ready, 1)
                dve.wait_ge(rstd_ready, rnd + 1)

            def mix(n):
                post = cT if n == 0 else vT
                dve.wait_ge(call_in, 16 * (n + 1))
                ln_stats(2 * n)
                with dve.Fori(0, NB // 2) as i:
                    for u in range(2):
                        b = i * 2 + u
                        xb = X[:, ds(b, 1), :].rearrange("p b l -> p (b l)")
                        dve.wait_ge(vt_full, b + (NB * n + 1))
                        v.tensor_scalar(Vb[u], xb, MEAN[:, ds(b, 1)], RSTD[:, ds(b, 1)], ALU.subtract, ALU.mult)\
                            .then_inc(v_ready, 1)
                        dve.wait_ge(v_ready, b + (NB * n + 1))
                        v.scalar_tensor_tensor(out=U[:, ds(b, 1), :].rearrange("p b l -> p (b l)"), in0=Vb[u],
                                               scalar=skip_s[:, n:n + 1],
                                               in1=CALL[:, ds(b, 1), :].rearrange("p b l -> p (b l)"),
                                               op0=ALU.mult, op1=ALU.mult).then_inc(u_ready, 1)
                with dve.Fori(0, 4) as i:
                    for u in range(2):
                        p = i * 2 + u
                        dve.wait_ge(g_full, p + (8 * n + 1))
                        need_prev = 8 * n
                        dve.wait_ge(g_res, p + need_prev)
                        v.tensor_tensor(gtmp[u], PS[:, 2 + u, :].rearrange("p (b l) -> p b l", b=2),
                                        CALL[:, ds(p * 2, 2), :], ALU.mult).then_inc(g_taken, 1)
                        dve.wait_ge(g_taken, p + (8 * n + 3))
                        xp = X[:, ds(p * 2, 2), :]
                        v.tensor_tensor(xp, xp, gtmp[u], ALU.add).then_inc(g_res, 1)
                dve.wait_ge(vt_taken, 2 + NB * (n + 1))
                dve.wait_ge(g_full, 8 * (n + 1))
                dve.wait_ge(g_res, 8 * (n + 1))
                with dve.Fori(0, MH // 2) as i:
                    for u in range(2):
                        h = i * 2 + u
                        for blk in range(2):
                            dve.wait_ge(y_full, h * 2 + (32 * n + blk + 5))
                            dve.wait_ge(dl_ready, h * 2 + (32 * n + blk + 1))
                            a = post[:, blk, :, ds(h * MD, MD)].unsqueeze(3).to_broadcast([P, NB, MD, MD])
                            y = PS[:, 4 * u + 2 * blk:4 * u + 2 * blk + 2, :].rearrange(
                                "p k (b i j) -> p (k b) i j", i=MD, j=MD)
                            v.tensor_tensor(zb[blk].rearrange("p (b i j) -> p b i j", i=MD, j=MD), y, a, ALU.mult)\
                                .then_inc(z_ready, 1)
                        for blk in range(2):
                            dve.wait_ge(z_ready, h * 2 + (32 * n + blk + 5))
                            v.tensor_reduce(dT[:, blk, :, ds(h * MD, MD)],
                                            zb[blk].rearrange("p (b i j) -> p b j i", i=MD, j=MD),
                                            AX.X, ALU.add).then_inc(dl_ready, 1)
                for p in range(8):
                    dve.wait_ge(dt_full, 8 * n + p + 1)
                    xp = X[:, 2 * p:2 * p + 2, :].rearrange("p b l -> p (b l)")
                    v.tensor_tensor(xp, xp, PS[:, p, :], ALU.add).then_inc(x_done, 1)

            def picks(n, nb, r):
                R, k = RB[n], TOPK[n]
                for j in range(nb):
                    settle(dve, dve_settled)
                    ch.link(v.max(R["TV"][:, j, :], R["LG"][:, j, :]))
                    settle(dve, dve_settled)
                    ch.link(v.max_index(TI[n][:, j, :], R["TV"][:, j, :], R["LG"][:, j, :]))
                v.tensor_tensor(R["EX"], R["LG"], R["TV"][:, :, 0:1].to_broadcast([P, nb, E]),
                                ALU.subtract).then_inc(ex_in[n], 1)
                ch.link(v.tensor_copy(R["TIF"], TI[n][:, :, 0:k]))
                ch.link(v.tensor_tensor(
                    R["OH"], iota_e[:].unsqueeze(1).unsqueeze(1).to_broadcast([P, nb, k, E]),
                    R["TIF"].unsqueeze(3).to_broadcast([P, nb, k, E]), ALU.is_equal))
                ch.link(v.tensor_reduce(R["M"], R["OH"].rearrange("p b k e -> p b e k"), AX.X, ALU.add))
                for j in range(nb):
                    ins = v.tensor_tensor(mcum[:, j + 1, :], mcum[:, j, :], R["M"][:, j, :], ALU.add)
                    if j < nb - 1:
                        ch.link(ins)
                ins.then_inc(m_ready[n], 1)

            def places(n, nb, bank, r):
                R, k = RB[n], TOPK[n]
                dve.wait_ge(ex_out[n], r + 1)
                ch.link(v.tensor_tensor(R["EM"], R["EX"], R["M"], ALU.mult))
                ch.link(v.tensor_reduce(R["DEN"], R["EX"] if n == 0 else R["EM"], AX.X, ALU.add))
                ch.link(v.reciprocal(R["RD"], R["DEN"]))
                v.tensor_tensor(HR[n][:, :, D:D + E], R["EM"], R["RD"].unsqueeze(2).to_broadcast([P, nb, E]),
                                ALU.mult).then_inc(row_ready[n], 1)
                if n == 0:
                    dve.wait_ge(rk_full, r + 1)
                ch.link(v.tensor_tensor(R["RK"], bank.rearrange("p (b e) -> p b e", e=E),
                                        row_e[:].unsqueeze(1).to_broadcast([P, nb, E]), ALU.add))
                v.tensor_copy(mcum[:, 0, :], mcum[:, nb, :]).then_inc(rk_taken[n], 1)
                ch.link(v.tensor_tensor(R["PR"], R["OH"], R["RK"].unsqueeze(2).to_broadcast([P, nb, k, E]),
                                        ALU.mult))
                ch.link(v.tensor_reduce(R["PF"], R["PR"], AX.X, ALU.add))
                v.tensor_copy(POS[n][:], R["PF"]).then_inc(pos_ready[n], 1)

            def ffn0():
                ch.link(v.memset(mcum[:, 0, :], 0.0))
                ln_stats(1)
                with dve.Fori(0, 4) as gi:
                    ch.enter(gi, 0, 20)
                    dve.wait_ge(scattered[0], gi * (16 * 8))
                    for j in range(4):
                        b = gi * 4 + j
                        xb = X[:, ds(b, 1), :].rearrange("p b l -> p (b l)")
                        v.tensor_copy(HR0[:, j, D + E:XCOLS].bitcast(I32), token_id[:, ds(b, 1)])
                        v.tensor_scalar(HR0[:, j, 0:D], xb, MEAN[:, ds(b, 1)], RSTD[:, ds(b, 1)], ALU.subtract, ALU.mult)\
                            .then_inc(h_ready[0], 1)
                    dve.wait_ge(lg_full, gi + 1)
                    v.tensor_copy(RB[0]["LG"], PS[:, 5, 0:64].rearrange("p (b e) -> p b e", e=E)).then_inc(lg_taken, 1)
                    dve.wait_ge(lg_taken, gi + 1)
                    picks(0, 4, gi)
                    for c in range(3):
                        dve.wait_ge(up_full, gi * 3 + (c + 1))
                        dve.wait_ge(sg_ready, gi * 3 + (c + 1))
                        dve.wait_ge(dn_full, gi * 2)
                        r = SCH[c]
                        v.tensor_tensor(aTg[0:r, c, :], sgT[0:r, c, :], PS[0:r, 2 * c + 1, :], ALU.mult)\
                            .then_inc(at_ready, 1)
                    places(0, 4, PS[:, 6, 0:64], gi)
                    for q in range(2):
                        dve.wait_ge(dn_full, gi * 2 + (q + 1))
                        xp = X[:, ds(gi * 4 + 2 * q, 2), :].rearrange("p b l -> p (b l)")
                        v.tensor_tensor(xp, xp, PS[:, 7 - q, :], ALU.add).then_inc(dn_taken, 1)
                ch.leave(4)

            def tables(n):
                dve.wait_ge(cnt_full[n], 1)
                dve.wait_ge(tau_made[n], 1)
                cnt, rem, pad, end, dg, ec = (cnt_s[:, q, :] for q in range(6))
                ch.link(v.tensor_copy(cnt, PS[:, 5, 0:E]))
                ch.link(v.tensor_scalar(cnt_i[:, 0:E], cnt, float(P - 1), None, ALU.add))
                ch.link(v.tensor_scalar(cnt_i[:, E:2 * E], cnt_i[:, 0:E], 7, 7, ALU.arith_shift_right,
                                        ALU.logical_shift_left))
                ch.link(v.tensor_copy(pad, cnt_i[:, E:2 * E]))
                ch.link(v.tensor_tensor(lep, le_e[:], pad.unsqueeze(1).to_broadcast([P, E, E]), ALU.mult))
                ch.link(v.tensor_reduce(end, lep, AX.X, ALU.add))
                ch.link(v.tensor_scalar(dg, pad, -1.0, float(EROWS), ALU.mult, ALU.add))
                ch.link(v.tensor_tensor(ec, cnt, row_e[:], ALU.add))
                ch.link(v.tensor_copy(tab[0:1, 2 * TMAX + 1:2 * TMAX + 1 + E], ec[0:1, :]))
                ch.link(v.tensor_tensor(tcmp, ttau.unsqueeze(2).to_broadcast([1, TMAX, E]),
                                        end[0:1, :].unsqueeze(1).to_broadcast([1, TMAX, E]), ALU.is_ge))
                ch.link(v.tensor_reduce(ter[:, 0, :], tcmp[:, :, 0:E - 1], AX.X, ALU.add))
                ch.link(v.tensor_tensor(tcmp, tcmp, dg[0:1, :].unsqueeze(1).to_broadcast([1, TMAX, E]), ALU.mult))
                ch.link(v.tensor_reduce(ter[:, 1, :], tcmp, AX.X, ALU.add))
                ch.link(v.tensor_tensor(ter[:, 1, :], ter[:, 1, :], ttau, ALU.add))
                ch.link(v.tensor_scalar(ter[:, 1, :], ter[:, 1, :], float(DUMMY), None, ALU.min))
                ch.link(v.tensor_copy(tab[0:1, 0:2 * TMAX], ter.rearrange("p a t -> p (a t)")))
                ch.link(v.tensor_scalar(n_pair[:], end[0:1, E - 1:E], float(P), None, ALU.add))
                v.tensor_scalar(tab[0:1, 2 * TMAX:2 * TMAX + 1], n_pair[:], 8, None, ALU.arith_shift_right)\
                    .then_inc(tab_ready[n], 1)

            def moe(n):
                m = ML[n]
                inter, kr = INTER[n], KROWS[n]

                def act_of(t, i, u):
                    e = dve.value_load(tab[0:1, ds(t, 1)], min_val=0, max_val=E - 1)
                    dve.wait_ge(xin[n][u], i * 16 + 16)
                    if isinstance(t, int):
                        pass
                    else:
                        dve.wait_ge(m["ok"], t + 1)
                    v.tensor_copy(meta[u], xt[u][:, D:XCOLS]).then_inc(m["meta"], 1)
                    dve.wait_ge(m["meta"], t + 1)
                    dve.wait_ge(m["silu"], t + 1)
                    need(dve, m["t2_full"], t - 1)
                    v.scalar_tensor_tensor(out=am[u][:, 0:inter], in0=sg[u][:, 0:inter],
                                           scalar=meta[u][:, ds(e, 1)], in1=PS[:, 2 + u, inter:2 * inter],
                                           op0=ALU.mult, op1=ALU.mult).then_inc(m["act"], 1)

                dve.sem_inc(m["at"], 1)
                dve.wait_ge(tab_ready[n], 1)
                act_of(0, 0, 0)
                pairs = dve.value_load(tab[0:1, 2 * TMAX:2 * TMAX + 1], min_val=1, max_val=TILES[n] // 2 + 1)
                with dve.Fori(0, pairs) as i:
                    for u in range(2):
                        t = i * 2 + u
                        dve.wait_ge(m["t2_full"], t + 1)
                        dve.wait_ge(m["down_full"], t)
                        v.tensor_copy(aTt[0:kr], PS[0:kr, 4 + u, 0:D].rearrange("p (k s) -> p k s", k=2))\
                            .then_inc(m["at"], 1)
                        act_of(t + 1, i + u, 1 - u)

            def front(b, turned_h):
                xb = X[:, ds(b, 1), :].rearrange("p b l -> p (b l)")
                xd = XD[:, ds(b % 4, 1), :].rearrange("p b l -> p (b l)")
                ch.link(v.tensor_scalar(xd, xb, MEAN[:, ds(b, 1)], RSTD[:, ds(b, 1)], ALU.subtract, ALU.mult))
                need(dve, side_full, turned_h)
                v.scalar_tensor_tensor(out=Hd, in0=xd, scalar=RMS[:, ds(b, 1)], in1=lnw_s, op0=ALU.mult, op1=ALU.mult)\
                    .then_inc(h_ready[1], 1)
                v.tensor_tensor(xb, xb, xd, ALU.add).then_inc(f_res, 1)

            def rope(p, n):
                dve.wait_ge(proj_full, p * 6 + (n + 1 if n < 4 else 6))
                need(dve, rp_ready, p * 5 + (n - 1 if n > 1 else 0))
                bank = PS[:, 2 if n in (0, 4) else 3, :]
                ps = bank.rearrange("p (h a d) -> p h a d", h=8, a=2)
                dst = (Qr[:, (n - 1) * 512:n * 512] if n else KA).rearrange("p (h d) -> p h d", h=8)
                bt = Bt[n % 2].rearrange("p (h a d) -> p h a d", h=8, a=2)
                H2 = HD // 2
                v.tensor_tensor(dst, bank.rearrange("p (h d) -> p h d", h=8),
                                cos_s.unsqueeze(1).to_broadcast([P, 8, HD]), ALU.mult)
                v.tensor_tensor(bt[:, :, 0, :], ps[:, :, 1, :],
                                sin_s[:, 0:H2].unsqueeze(1).to_broadcast([P, 8, H2]), ALU.mult)
                v.tensor_tensor(bt[:, :, 1, :], ps[:, :, 0, :],
                                sin_s[:, H2:HD].unsqueeze(1).to_broadcast([P, 8, H2]), ALU.mult)\
                    .then_inc(rope_taken, 1)

            def k_t(b, i):
                c = (i - 1) % 4
                dve.wait_ge(td_full, turned(b, 2 * i + 2))
                v.tensor_copy(kTd[:, 2 * c:2 * c + 2, :], PS[:, 5, 0:2 * P].rearrange("p (r q) -> p r q", r=2))\
                    .then_inc(td_taken, 1)

            def masked(b, i):
                for par in range(2):
                    dve.wait_ge(s_full, b * 8 + (2 * i + par + 1))
                    settle(dve, dve_settled)
                    for q in range(4):
                        ins = v.tensor_tensor_reduce(SM[i % 2][par][:, q, :], PS[:, par, q * P:(q + 1) * P], maskneg,
                                                     1.0, -3e38, ALU.add, ALU.max, mx[i % 2][:, par, q:q + 1])
                    ins.then_inc(sm_taken, 1)
                dve.wait_ge(sm_taken, b * 8 + (2 * i + 2))
                v.tensor_scalar(nbias[i % 2], mx[i % 2], -(HD ** -0.5), None, ALU.mult).then_inc(nb_ready, 1)

            def p_t(b, i):
                dve.wait_ge(td_full, turned(b, 2 * i + 1))
                v.tensor_copy(PT[1], PS[:, 5, :].rearrange("p (r q) -> p r q", r=4)).then_inc(td_taken, 1)
                j = (i - 1) % 2
                dve.wait_ge(ex_ready, b * 4 + i)
                v.reciprocal(rinv[j], rs[j]).then_inc(ri_ready, 1)

            def o_norm(b, i):
                dve.wait_ge(pv_full, b * 4 + i)
                dve.wait_ge(ri_ready, b * 4 + i)
                o4 = PS[:, 6, :].rearrange("p (q a d) -> p q a d", q=4, a=2)
                d4 = On.rearrange("p (q a d) -> p q a d", q=4, a=2)
                r4 = rinv[(i - 1) % 2].rearrange("p a q -> p q a").unsqueeze(3).to_broadcast([P, 4, 2, HD])
                v.tensor_tensor(d4, o4, r4, ALU.mult).then_inc(o_taken, 1)

            def post(b):
                dve.wait_ge(wo_full, b + 1)
                dve.wait_ge(f_res, b + 1)
                xb = X[:, ds(b, 1), :].rearrange("p b l -> p (b l)")
                xd = XD[:, ds(b % 4, 1), :].rearrange("p b l -> p (b l)")
                v.tensor_tensor(xb, xb, PS[:, 2, 0:D], ALU.add)
                v.tensor_tensor(X2[:], xd, PS[:, 2, 0:D], ALU.add).then_inc(wo_taken, 1)
                dve.wait_ge(wo_taken, b + 1)
                need(dve, scattered[1], b * 64)
                settle(dve, dve_settled)
                ch.link(v.tensor_tensor_reduce(HR1[:, 0, 0:D], X2[:], X2[:], 1.0 / D, 0.0, ALU.mult, ALU.add, rms[:, 0:1]))
                v.tensor_scalar(rms[:, 1:2], rms[:, 0:1], EPS, None, ALU.add).then_inc(rq_ready, 1)

            def row(b):
                dve.wait_ge(rr_ready, b + 1)
                v.tensor_copy(HR1[:, 0, D + E:XCOLS].bitcast(I32), token_id[:, ds(b, 1)])
                v.scalar_tensor_tensor(out=HR1[:, 0, 0:D], in0=X2[:], scalar=rms[:, 2:3], in1=fflnw_s,
                                       op0=ALU.mult, op1=ALU.mult).then_inc(row_feat, 1)

            mix(0)
            if stage >= 2:
                ffn0()
                tables(0)
                moe(0)
            if stage >= 3:
                dve.wait_ge(x_back, 16)
                mix(1)
            if stage >= 4:
                ch.link(v.memset(mcum[:, 0, :], 0.0))
                dve.wait_ge(d_in, 64)
                dve.wait_ge(consts, 16)
                ln_stats(3)
                ch.link(v.tensor_tensor(dd, RSTD, RSTD, ALU.mult))
                ch.link(v.tensor_tensor(dd, dd, VAR, ALU.mult))
                v.tensor_scalar(VE, dd, EPS, None, ALU.add).then_inc(ve_ready, 1)
                dve.wait_ge(rstd_ready, 5)
                front(0, 0)

                def body(b):
                    for i in range(4):
                        prev = b if i else b - 1
                        coming = b + 1 if i else b
                        if i == 3 and there(b - 1):
                            post(b - 1)
                        if there(b):
                            masked(b, i)
                        if i == 0 and there(b + 1):
                            rope(b + 1, 0)
                        if i == 3 and there(b - 1):
                            row(b - 1)
                        if there(prev):
                            p_t(b, i)
                        if i == 0 and there(b - 2):
                            dve.wait_ge(side_taken, side(b, 3))
                            picks(1, 1, b - 2)
                        if there(prev):
                            o_norm(b, i)
                        if there(b + 1):
                            rope(b + 1, i + 1)
                        if there(coming):
                            k_t(b, i)
                        if i == 1 and there(b - 2):
                            dve.wait_ge(side_taken, side(b, 5))
                            places(1, 1, RB[1]["RS"].rearrange("p b e -> p (b e)"), b - 2)
                        if i == 2 and there(b + 2):
                            front(b + 2, side(b, 1))
                steps(dve, body, ch, 13)
                tables(1)
                moe(1)


_NAMES = ["x", "ctx", "conv_k", "skip", "gate_t", "gu", "dn", "sgu", "sdn", "dvec", "lnw", "fflnw",
          "wq", "wk", "wv", "wo", "wg", "w1", "w3", "w2", "cos", "sin"]


def rope_tables():
    half = HD // 2
    inv = (np.float32(1.0) / np.float32(150000.0) ** (np.arange(half, dtype=np.float32) / np.float32(half)))
    ang = np.arange(P, dtype=np.float32)[:, None] * inv.astype(np.float32)
    c, s = np.cos(ang).astype(np.float32), np.sin(ang).astype(np.float32)
    return np.concatenate([c, c], -1), np.concatenate([-s, s], -1)


def kernel(x, fside_S2_0, ctx_2048, L0_xattn_k, L0_ffn_gate_w, L0_ffn_w_gate_up, L0_ffn_w_down,
           L0_ffn_shared_gate_up, L0_ffn_shared_down, L1_xattn_ssm_kernel, L1_xattn_D, L1_ffn_ln_w,
           L1_ffn_ff_ln_w, L1_ffn_wq, L1_ffn_wk, L1_ffn_wv, L1_ffn_wo, L1_ffn_wg, L1_ffn_w1, L1_ffn_w3,
           L1_ffn_w2, _stage=4):
    import concourse.bacc as bacc
    from concourse.bass_utils import run_bass_kernel_spmd

    cos, sin = rope_tables()
    host = [x, ctx_2048, np.concatenate([np.asarray(L0_xattn_k), np.asarray(L1_xattn_ssm_kernel)]), fside_S2_0,
            np.asarray(L0_ffn_gate_w).T, L0_ffn_w_gate_up, L0_ffn_w_down, L0_ffn_shared_gate_up,
            L0_ffn_shared_down, L1_xattn_D, L1_ffn_ln_w, L1_ffn_ff_ln_w, L1_ffn_wq, L1_ffn_wk, L1_ffn_wv,
            L1_ffn_wo, L1_ffn_wg, L1_ffn_w1, L1_ffn_w3, L1_ffn_w2, cos, sin]
    nc = bacc.Bacc("TRN2", target_bir_lowering=False, num_devices=1)
    arrays, args = {}, []
    for name, a in zip(_NAMES, host):
        a = np.ascontiguousarray(a)
        arrays[f"in_{name}"] = a
        args.append(nc.dram_tensor(f"in_{name}", a.shape, mybir.dt.from_np(a.dtype), kind="ExternalInput").ap())
    out = nc.dram_tensor("out_0", (NB, P, D), F32, kind="ExternalOutput").ap()
    program(nc, *args, out, stage=_stage)
    r = run_bass_kernel_spmd(nc, [arrays], core_ids=[0])
    return r.results[0]["out_0"]
```

```python
from contextlib import ExitStack

import numpy as np

import concourse.bass as bass
from concourse import mybir

F32 = mybir.dt.float32
I32 = mybir.dt.int32
U32 = mybir.dt.uint32
ALU = mybir.AluOpType
ACT = mybir.ActivationFunctionType
AX = mybir.AxisListType

P = 128
NB = 16
D = 256
EPS = 1e-5

MH = 16
MD = 8

E = 16
TOPK = [2, 4]
INTER = [176, 256]
KROWS = [88, 128]
SI = 352
SCH = [128, 128, 96]

QH, KH, HD = 32, 8, 64
QCH = 6

EROWS = NB * P + P
DUMMY = E * EROWS
XROWS = DUMMY + P
XCOLS = D + E + 1
NTOK = NB * P
TILES = [NTOK * k // P + E for k in TOPK]
TMAX = max(TILES) + 4


def ds(start, size):
    return bass.ds(start, size)


def program(nc, x, ctx, conv_k, skip, gate_t, gu, dn, sgu, sdn, dvec, lnw, fflnw,
            wq, wk, wv, wo, wg, w1, w3, w2, cos, sin, out):
    es = ExitStack()
    with es:
        def sb(name, shape, dt=F32):
            return es.enter_context(nc.sbuf_tensor(name, shape, dt))

        def sem(name):
            return es.enter_context(nc.semaphore(name))

        PS = es.enter_context(nc.psum_tensor("PS", [P, 8, 512], F32))

        X = sb("X", [P, NB, D])
        WREG = sb("WREG", [P, 24576])
        WOR = sb("WOR", [P, 16 * D])
        SCR = sb("SCR", [P, 17600])
        ident = sb("ident", [P, P])
        tri = sb("tri", [P, P])
        ones = sb("ones", [P, P])
        group = sb("group", [P, P])
        group_s = sb("group_s", [P, P])
        iota_e = sb("iota_e", [P, E])
        row_e = sb("row_e", [P, E])
        le_e = sb("le_e", [P, E, E])
        token_id = sb("token_id", [P, NB], I32)
        zrow = sb("zrow", [P, XCOLS])
        skip_s = sb("skip_s", [P, 2])
        wg_s = sb("wg_s", [P, 2, E])
        st6 = sb("st6", [P, NB, 6])
        lnv = sb("lnv", [P, 8, NB])
        VE2, dd, MEAN, M2, VAR, VE, RSTD, RMS = (lnv[:, q, :] for q in range(8))
        s12 = sb("s12", [P, NB, 2])
        squares = sb("squares", [P, D])
        X2 = sb("X2", [P, D])
        mhalf = sb("mhalf", [P, NB])
        rms = sb("rms", [P, 3])
        mcum = sb("mcum", [P, 5, E])
        tab = sb("tab", [1, 5 * TMAX // 2 + 1 + E], I32)
        cnt_s = sb("cnt_s", [P, 4, E])
        tau = sb("tau", [P, 1])
        n_pair = sb("n_pair", [1, 1], I32)
        cnt_i = sb("cnt_i", [P, 2 * E], I32)

        CONSTS = 15
        ENDS = 2 * TMAX + 1
        PACKED = 2 * TMAX + 1 + E

        def padding(eng, n, first, last, done):
            eng.wait_ge(ends_ready[n], 1)
            with eng.Fori(first, last) as i:
                counts = eng.value_load(tab[0:1, ds(i + ENDS, 1)], min_val=0, max_val=4097 * NTOK)
                for u, c in enumerate((counts % 4096, counts // 4096)):
                    eng.dma_start(xs[n][ds(i * (2 * EROWS) + u * EROWS + c, P), :], zrow[:]).then_inc(done, 16)

        def packed(eng, i):
            pk = eng.value_load(tab[0:1, ds(i + PACKED, 1)], min_val=0, max_val=E ** 4 - 1)
            return pk % E, (pk // E) % E, (pk // E ** 2) % E, pk // E ** 3

        def carve(region, at, *dims, parts=P):
            n = int(np.prod(dims))
            v = region[0:parts, at:at + n]
            if len(dims) == 2:
                v = v.rearrange("p (a b) -> p a b", a=dims[0])
            elif len(dims) == 3:
                v = v.rearrange("p (a b c) -> p a b c", a=dims[0], b=dims[1])
            elif len(dims) == 4:
                v = v.rearrange("p (a b c d) -> p a b c d", a=dims[0], b=dims[1], c=dims[2])
            return v

        GU = carve(WREG, 0, 2, E, 2 * INTER[0])
        DN = carve(WREG, 11264, 2, E, D, parts=88)
        SGU = carve(WREG, 19456, 2, 2 * SI)
        SDN = carve(WREG, 20864, 3, D)
        GT0 = carve(WREG, 21632, 2, E)
        W13 = carve(WREG, 0, 2, E, 2 * INTER[1])
        W2 = carve(WREG, 16384, 2, E, D)
        WQ = carve(WREG, 16384, 2, QH * HD)
        WK = carve(WREG, 20480, 2, KH * HD)
        WV = carve(WREG, 21504, 2, KH * HD)

        WO = carve(WOR, 0, 16, D)
        cT = carve(SCR, 0, 2, NB, P)
        vT = carve(SCR, 4096, 2, NB, P)
        dT = carve(SCR, 8192, 2, NB, P)
        U = carve(SCR, 8192, NB, D)
        CALL = carve(SCR, 12288, NB, D)
        kv = [[carve(WREG, 22528 + 1024 * blk, 1024) for blk in range(2)],
              [carve(SCR, 12288 + 1024 * blk, 1024) for blk in range(2)]]
        weighted = [carve(WOR, 1024 * blk, 1024) for blk in range(2)]
        TZ = [carve(WOR, 2048 + 256 * u, D) for u in range(4)]
        Vb = [carve(SCR, 16384 + 256 * u, D) for u in range(4)]
        S1 = [carve(SCR, 4096, NB, D), carve(SCR, 0, NB, D)]
        gtmp = [carve(WOR, 3072 + 512 * u, 2, D) for u in range(2)]

        hTa = carve(SCR, 4096, 2, NB * P)
        HR0 = [carve(SCR, 8192 + 4 * XCOLS * u, 4, XCOLS) for u in range(2)]
        sgT = carve(WOR, 0, 3, 4 * P)
        aTg = carve(WOR, 12 * P, 3, 4 * P)
        R_AT = [16384, 17240]

        def route_bufs(at, nb, k):
            r = {}
            for name, dims in (("LG", (nb, E)), ("TV", (nb, 8)), ("EX", (nb, E)), ("TIF", (nb, k)),
                               ("OH", (nb, k, E)), ("M", (nb, E)), ("EM", (nb, E)), ("DEN", (nb,)),
                               ("RD", (nb,)), ("RK", (nb, E)), ("RS", (nb, E)), ("PR", (nb, k, E)), ("PF", (nb, k))):
                n = int(np.prod(dims))
                r[name] = carve(SCR, at, *dims)
                at += n
            return r
        RB = [route_bufs(R_AT[0], 4, 2), route_bufs(R_AT[1], 1, 4)]
        TI = [sb("TI0", [P, 4, 8], U32), sb("TI1", [P, 1, 8], U32)]
        POS0 = [sb(f"POS0{u}", [P, 4, 2], I32) for u in range(2)]
        POS1 = sb("POS1", [P, 1, 4], I32)

        o = 11200
        xt = [carve(SCR, o + 280 * u, XCOLS) for u in range(2)]; o += 560
        xTt = [carve(SCR, o + 256 * u, 2, P) for u in range(2)]; o += 512
        sg = [carve(SCR, o + 256 * u, 256) for u in range(2)]; o += 512
        am = [carve(SCR, o + 256 * u, 256) for u in range(2)]; o += 512
        aTt = [carve(SCR, o + 256 * u, 2, P) for u in range(2)]; o += 512
        yt = [carve(SCR, o + 256 * u, D) for u in range(2)]; o += 512
        META = 20
        meta = carve(SCR, o, 4 * META); o += 4 * META
        ids = [sb(f"row_tokens{u}", [P, 1], I32) for u in range(2)]
        tcmp = carve(SCR, o, 2, E); o += 2 * E
        ter = carve(SCR, o, 2); o += 2
        pk = carve(SCR, o, TMAX // 2 - 1, parts=1); o += TMAX // 2
        lep = carve(SCR, o, E, E); o += E * E
        assert o <= 16384

        o = 0
        cos_s = carve(SCR, o, HD); o += HD
        sin_s = carve(SCR, o, HD); o += HD
        lnw_s = carve(SCR, o, D); o += D
        fflnw_s = carve(SCR, o, D); o += D
        maskneg = carve(SCR, o, P); o += P
        XD = carve(SCR, o, 4, D); o += 4 * D
        Hd = carve(SCR, o, D); o += D
        hT = carve(SCR, o, 2, P); o += 2 * P
        Qr = carve(SCR, o, QH * HD); o += QH * HD
        KA = carve(SCR, o, KH * HD); o += KH * HD
        Bt = [carve(SCR, o + 512 * u, 512) for u in range(2)]; o += 1024
        Kd = carve(SCR, o, KH, 2, HD); o += 2 * KH * HD
        qT = carve(SCR, o, 16, P); o += 16 * P
        kTd = carve(SCR, o, KH, P); o += KH * P
        Vs = carve(SCR, o, 2, KH * HD); o += 2 * KH * HD
        SM = [[carve(SCR, o + 1024 * i + 512 * par, 4, P) for par in range(2)] for i in range(2)]
        o += 2048
        PT = [carve(SCR, o + 512 * par, 4, P) for par in range(2)]; o += 1024
        On = carve(SCR, o, 512); o += 512
        OT = carve(SCR, o, 16, P); o += 16 * P
        mx = [carve(SCR, o + 8 * i, 2, 4) for i in range(2)]; o += 16
        nbias = [carve(SCR, o + 8 * i, 2, 4) for i in range(2)]; o += 16
        rs = [carve(SCR, o + 8 * i, 2, 4) for i in range(2)]; o += 16
        rinv = [carve(SCR, o + 8 * i, 2, 4) for i in range(2)]; o += 16
        h2T = carve(SCR, o, 2, P); o += 2 * P
        HR1 = carve(SCR, o, 1, XCOLS); o += XCOLS
        assert o <= R_AT[1]

        toe = [nc.dram_tensor(f"toeplitz{n}", [MH, P, D], F32, kind="Internal") for n in range(2)]
        xs = [nc.dram_tensor(f"rows_by_expert{n}", [XROWS, XCOLS], F32, kind="Internal") for n in range(2)]
        acc = [[nc.dram_tensor(f"stream{n}_{u}", [NTOK + P, D], F32, kind="Internal") for u in range(2)]
               for n in range(2)]

        consts = sem("consts_made")
        x_in, misc_in = [sem(f"x{q}_in") for q in range(4)], sem("misc_in")
        toe_out = [sem(f"toeplitz{n}_out") for n in range(2)]
        ws_in, we_in = sem("shared_weights_in"), sem("expert_weights_in")
        wd_in, wr_in, w2_in = sem("w13_in"), sem("attention_weights_in"), sem("w2_in")
        wo_in = sem("wo_in")
        d_in = sem("attention_tables_in")
        call_in = [sem(f"ctx_rows{n}_in") for n in range(2)]
        t_in = [sem(f"toeplitz{u}_in") for u in range(4)]
        dve_seq = sem("dve_seq")
        dve_settled, pool_settled = sem("dve_settled"), sem("pool_settled")
        st_done, ve_ready, rstd_ready = sem("stats_done"), sem("variance_ready"), sem("rstd_ready")
        rq_ready, rr_ready = sem("square_ready"), sem("rms_ready")
        gs_ready = sem("group_scaled")
        v_ready, u_ready = sem("v_ready"), sem("u_ready")
        ct_full, ct_taken = sem("ctx_turned"), sem("ctx_taken")
        vt_full, vt_taken = sem("vt_full"), sem("vt_taken")
        g_full, g_taken, g_res = sem("g_full"), sem("g_taken"), sem("g_res")
        kv_ready, y_full, z_ready, dl_ready = sem("kv_ready"), sem("y_full"), sem("z_ready"), sem("delta_ready")
        dt_full, x_done = sem("dt_full"), sem("x_done")
        h_ready = [sem(f"h_ready{n}") for n in range(2)]
        ht_full = sem("ht_full")
        ht_taken = sem("ht_taken")
        lg_full = sem("logits_full")
        lg_taken = sem("logits_taken")
        m_ready = [sem(f"picks_ready{n}") for n in range(2)]
        rk_full = sem("rank_full")
        rk_taken = [sem(f"rank_taken{n}") for n in range(2)]
        ex_in = [sem(f"gate_shifted{n}") for n in range(2)]
        ex_out = [sem(f"gate_exp{n}") for n in range(2)]
        row_ready = [sem(f"row_ready{n}") for n in range(2)]
        pos_ready = [sem(f"pos_ready{n}") for n in range(2)]
        scattered0 = [sem(f"scattered0_{u}") for u in range(2)]
        scattered1 = sem("scattered1")
        cnt_full = [sem(f"count_full{n}") for n in range(2)]
        tab_ready = [sem(f"tables_ready{n}") for n in range(2)]
        ends_ready = [sem(f"ends_ready{n}") for n in range(2)]
        tile_ready = [sem(f"tile_columns_ready{n}") for n in range(2)]
        tile_full = [sem(f"tile_rows_full{n}") for n in range(2)]
        pad_act, pad_pool = sem("padding_in_by_act"), sem("padding_in_by_pool")
        pad_in = [sem(f"padding_in{n}") for n in range(2)]
        acc_in = [sem(f"stream_out{n}") for n in range(2)]
        up_full, sg_ready, at_ready, dn_full, dn_taken = (
            sem("shared_up_full"), sem("shared_silu"), sem("shared_act"), sem("shared_down_full"),
            sem("shared_down_taken"))
        names = ("ok", "id", "t1_full", "xt_ready", "up_full", "silu", "meta", "act", "t2_full", "at", "down_full", "y")
        ML = [{k: sem(f"moe{n}_{k}") for k in names} for n in range(2)]
        xin = [[sem(f"moe{n}_rows{u}_in") for u in range(2)] for n in range(2)]
        added = [[sem(f"moe{n}_added{u}") for u in range(2)] for n in range(2)]
        summed = sem("streams_summed")
        moe_done = [sem(f"moe{n}_done") for n in range(2)]
        x_back = [sem(f"x{q}_back") for q in range(4)]
        side_full, side_taken = sem("side_bank_full"), sem("side_bank_taken")
        proj_full, rope_taken, v_taken, rp_ready = sem("proj_full"), sem("rope_taken"), sem("v_taken"), sem("roped")
        ta_full, ta_taken = sem("turned_full_for_act"), sem("turned_taken_by_act")
        td_full, td_taken = sem("turned_full_for_dve"), sem("turned_taken_by_dve")
        s_full, sm_taken, nb_ready, ex_ready = sem("s_full"), sem("s_masked"), sem("nbias_ready"), sem("exp_ready")
        ri_ready = sem("rinv_ready")
        pv_full, o_taken = sem("pv_full"), sem("o_taken")
        wo_full, wo_taken = sem("wo_full"), sem("wo_taken")
        f_res, row_feat = sem("xd_added"), sem("row_features_ready")
        out_done = sem("out_done")

        def need(eng, s, v):
            if isinstance(v, int) and v <= 0:
                return
            eng.wait_ge(s, v)

        def settle(eng, s):
            eng.sem_inc(s, 1)

        class Chain:

            def __init__(self, eng, s):
                self.eng, self.s, self.base, self.i, self.per, self.k = eng, s, 0, None, 0, 0

            def value(self):
                return self.base + self.k if self.i is None else self.i * self.per + (self.base + self.k)

            def link(self, ins):
                self.k += 1
                ins.then_inc(self.s, 1)
                self.eng.wait_ge(self.s, self.value())

            def enter(self, i, start, per):
                self.base = self.base + self.k - start * per
                self.i, self.per, self.k = i, per, 0

            def leave(self, end):
                assert self.k == self.per, ("per is", self.k)
                self.base, self.i, self.k = self.base + end * self.per, None, 0

        def there(b):
            return not isinstance(b, int) or 0 <= b < NB

        def tally(offsets):
            def through(b, k):
                return sum(1 for s in range(-1, b + 1) for q, o in enumerate(offsets)
                           if 0 <= s + o < NB and (s < b or q < k))

            def value(b, k, shift=0):
                if isinstance(b, int):
                    return through(b + shift, k)
                return b * len(offsets) + (through(2 + shift, k) - 2 * len(offsets))
            return value
        turned = tally((-1, 0, 0, 1, 0, 1, 0, 1))
        side = tally((1, -1, -2, -1, -2, 0, 0, -1))

        def steps(eng, body, chain=None, per=0):
            for b in (-1, 0, 1):
                body(b)
            with eng.Fori(2, NB - 2) as b:
                if chain:
                    chain.enter(b, 2, per)
                body(b)
            if chain:
                chain.leave(NB - 2)
            for b in (NB - 2, NB - 1, NB, NB + 1):
                body(b)

        block = es.enter_context(nc.Block())

        @block.sync
        def _(sp):
            def toeplitz(n, i, u):
                h = i * 4 + u
                if n or not isinstance(i, int):
                    sp.wait_ge(y_full, h * 2 + (32 * n - 2))
                sp.dma_start(TZ[u], toe[n][ds(h, 1)].rearrange("a p l -> p (a l)")).then_inc(t_in[u], 16)

            def blocks(w, rows=P):
                return w.rearrange("(k p) j -> p k j", p=rows)

            def mix(n):
                sp.wait_ge(toe_out[n], 16)
                for u in range(4):
                    toeplitz(n, 0, u)
                if n == 0:
                    sp.dma_start(GT0, blocks(gate_t)).then_inc(ws_in, 16)
                    sp.dma_start(SGU, blocks(sgu)).then_inc(ws_in, 16)
                    sp.dma_start(SDN[:, 0:2, :], blocks(sdn[0:2 * P, :])).then_inc(ws_in, 16)
                    sp.dma_start(SDN[0:96, 2, :], sdn[2 * P:SI, :]).then_inc(ws_in, 16)
                else:
                    sp.dma_start(WK, blocks(wk)).then_inc(wr_in, 16)
                    sp.dma_start(WQ, blocks(wq)).then_inc(wr_in, 16)
                    sp.dma_start(WV, blocks(wv)).then_inc(wr_in, 16)
                def one_expert(e):
                    def of(w, rows=P):
                        return w[ds(e, 1)].rearrange("a (k p) j -> p k (a j)", p=rows)
                    if n == 0:
                        sp.dma_start(GU[:, :, ds(e, 1)].rearrange("p k a j -> p k (a j)"), of(gu)).then_inc(we_in, 16)
                        sp.dma_start(DN[:, :, ds(e, 1)].rearrange("p k a j -> p k (a j)"), of(dn, KROWS[0]))\
                            .then_inc(we_in, 16)
                    else:
                        sp.dma_start(W13[:, :, ds(e, 1), 0:D].rearrange("p k a j -> p k (a j)"), of(w1))\
                            .then_inc(wd_in, 16)
                        sp.dma_start(W13[:, :, ds(e, 1), D:2 * D].rearrange("p k a j -> p k (a j)"), of(w3))\
                            .then_inc(wd_in, 16)
                for e in range(4):
                    one_expert(e)
                with sp.Fori(1, 4) as i:
                    for u in range(4):
                        toeplitz(n, i, u)
                        one_expert(i * 4 + u)

            def stream_out0(s):
                sp.wait_ge(dn_taken, 2 * s + 2)
                sp.dma_start(acc[0][0][4 * P * s:4 * P * (s + 1), :].rearrange("(b p) l -> p b l", p=P),
                             X[:, 4 * s:4 * s + 4, :]).then_inc(acc_in[0], 16)

            def stream_out1(b):
                sp.wait_ge(wo_taken, b + 1)
                sp.dma_start(acc[1][0][ds(b * P, P), :], X[:, ds(b, 1), :].rearrange("p b l -> p (b l)"))\
                    .then_inc(acc_in[1], 16)

            def moe(n, pad_count, between):
                m = ML[n]
                for s in ([scattered1] if n else scattered0):
                    sp.wait_ge(s, NB * TOPK[n] * 16 // (1 if n else 2))
                sp.wait_ge(pad_in[n], 16 * (pad_count + 1))
                sp.wait_ge(pad_act, 16 * (4 + 6 * n))
                if n:
                    sp.wait_ge(pad_pool, 16 * 4)
                sp.wait_ge(tab_ready[n], 1)

                def load(t, u):
                    r = sp.value_load(tab[0:1, ds(t + TMAX, 1)], min_val=0, max_val=DUMMY)
                    sp.dma_start(xt[u], xs[n][ds(r, P), :]).then_inc(xin[n][u], 16)

                load(0, 0)
                load(1, 1)
                between()
                pairs = sp.value_load(tab[0:1, 2 * TMAX:2 * TMAX + 1], min_val=1, max_val=TILES[n] // 2 + 1)
                sp.wait_ge(m["t1_full"], 1)
                sp.wait_ge(m["meta"], 1)
                load(2, 0)
                with sp.Fori(0, pairs) as i:
                    for u in range(2):
                        t = i * 2 + u
                        sp.wait_ge(m["t1_full"], t + 2)
                        sp.wait_ge(m["meta"], t + 2)
                        load(t + 3, 1 - u)

            for q in range(4):
                sp.dma_start(X[:, 4 * q:4 * q + 4, :], x[4 * q:4 * q + 4].rearrange("b p l -> p b l"))\
                    .then_inc(x_in[q], 16)
            sp.dma_start(skip_s[:, 0:1], skip.rearrange("(p a) -> p a", a=1)).then_inc(misc_in, 16)
            dv = dvec.rearrange("(p a) -> p a", a=1)
            dsrc = bass.AP(tensor=dv.tensor, offset=dv.offset, ap=[[1, MH], [0, MD], [1, 1]])
            sp.dma_start(skip_s[:, 1:2], dsrc).then_inc(misc_in, 16)
            sp.dma_start(CALL, ctx.rearrange("b p l -> p b l")).then_inc(call_in[0], 16)
            sp.dma_start(wg_s[:], wg.rearrange("(k p) e -> p k e", p=P)).then_inc(misc_in, 16)
            for n in range(2):
                k0 = conv_k[n * MH:n * MH + 1, P:P + 1]
                src = bass.AP(tensor=k0.tensor, offset=k0.offset, ap=[[P + D, MH], [-1, P], [1, D]])
                sp.dma_start(toe[n][:, :, :], src).then_inc(toe_out[n], 16)
            mix(0)
            sp.wait_ge(consts, CONSTS)
            for n in range(2):
                sp.dma_start(acc[n][0][NTOK:NTOK + P, :], zrow[:, 0:D]).then_inc(acc_in[n], 16)
                sp.dma_start(acc[n][1][:, :].rearrange("(b p) l -> p b l", p=P),
                             zrow[:, 0:D].unsqueeze(1).to_broadcast([P, NB + 1, D])).then_inc(acc_in[n], 16)
                sp.dma_start(xs[n][DUMMY:DUMMY + P, :], zrow[:]).then_inc(pad_in[n], 16)
            stream_out0(0)
            stream_out0(1)
            padding(sp, 0, 0, 6, pad_in[0])
            moe(0, 12, lambda: (stream_out0(2), stream_out0(3)))
            sp.wait_ge(moe_done[0], 1)
            for q in range(4):
                r = slice(4 * P * q, 4 * P * (q + 1))
                sp.dma_start(X[:, 4 * q:4 * q + 4, :], acc[0][0][r, :].rearrange("(b p) l -> p b l", p=P))\
                    .then_inc(x_back[q], 16)
                sp.dma_start(S1[0][:, 4 * q:4 * q + 4, :], acc[0][1][r, :].rearrange("(b p) l -> p b l", p=P))\
                    .then_inc(x_back[q], 16)
            sp.dma_start(CALL, ctx.rearrange("b p l -> p b l")).then_inc(call_in[1], 16)
            mix(1)
            sp.wait_ge(x_done, 16)
            sp.dma_start(cos_s, cos).then_inc(d_in, 16)
            sp.dma_start(sin_s, sin).then_inc(d_in, 16)
            sp.dma_start(lnw_s, lnw.partition_broadcast(P)).then_inc(d_in, 16)
            sp.dma_start(fflnw_s, fflnw.partition_broadcast(P)).then_inc(d_in, 16)
            sp.dma_start(WO, wo.rearrange("(t p) n -> p t n", p=P)).then_inc(wo_in, 16)
            with sp.Fori(0, NB - 1) as b:
                stream_out1(b)
            sp.wait_ge(proj_full, QCH * NB)
            for k in range(2):
                sp.dma_start(W2[:, k], w2[:, k * P:(k + 1) * P, :].rearrange("e p j -> p e j")).then_inc(w2_in, 16)
            stream_out1(NB - 1)
            padding(sp, 1, 0, 3, pad_in[1])
            moe(1, 6, lambda: None)
            sp.wait_ge(moe_done[1], 1)
            for q in range(4):
                r = slice(4 * P * q, 4 * P * (q + 1))
                sp.dma_start(X[:, 4 * q:4 * q + 4, :], acc[1][0][r, :].rearrange("(b p) l -> p b l", p=P))\
                    .then_inc(x_back[q], 16)
                sp.dma_start(S1[1][:, 4 * q:4 * q + 4, :], acc[1][1][r, :].rearrange("(b p) l -> p b l", p=P))\
                    .then_inc(x_back[q], 16)
            for q in range(4):
                sp.wait_ge(summed, q + 1)
                sp.dma_start(out[4 * q:4 * q + 4].rearrange("b p l -> p b l"), X[:, 4 * q:4 * q + 4, :])\
                    .then_inc(out_done, 16)
            sp.wait_ge(out_done, 64)

        @block.gpsimd
        def _(pool):
            g = nc.gpsimd
            made = [0]

            def mk(ins):
                made[0] += 1
                ins.then_inc(consts, 1)
                pool.wait_ge(consts, made[0])

            mk(g.memset(zrow[:], 0.0))
            mk(g.memset(ones[:], 1.0))
            mk(g.memset(ident[:], 0.0))
            mk(g.affine_select(out=ident[:], in_=ident[:], compare_op=ALU.not_equal, fill=1.0, base=0,
                               pattern=[[-1, P]], channel_multiplier=1))
            mk(g.affine_select(out=tri[:], in_=ones[:], compare_op=ALU.is_gt, fill=0.0, base=0,
                               pattern=[[1, P]], channel_multiplier=-1))
            mk(g.affine_select(out=group[:], in_=ones[:], compare_op=ALU.is_ge, fill=0.0, base=0,
                               pattern=[[-MD, MH], [0, MD]], channel_multiplier=1))
            mk(g.affine_select(out=group[:], in_=group[:], compare_op=ALU.is_ge, fill=0.0, base=MD - 1,
                               pattern=[[MD, MH], [0, MD]], channel_multiplier=-1))
            mk(g.iota(iota_e[:], pattern=[[1, E]], base=0, channel_multiplier=0,
                      allow_small_or_imprecise_dtypes=True))
            mk(g.iota(row_e[:], pattern=[[EROWS, E]], base=0, channel_multiplier=0,
                      allow_small_or_imprecise_dtypes=True))
            mk(g.memset(le_e[:], 1.0))
            mk(g.affine_select(out=le_e[:], in_=le_e[:], compare_op=ALU.is_ge, fill=0.0, base=0,
                               pattern=[[1, E], [-1, E]], channel_multiplier=0))
            mk(g.iota(token_id[:], pattern=[[P, NB]], base=0, channel_multiplier=1))
            mk(g.iota(zrow[:, D + E:XCOLS].bitcast(I32), pattern=[[0, 1]], base=NTOK, channel_multiplier=1))
            mk(g.memset(mhalf[:], -0.5))
            mk(g.iota(tau[:], pattern=[[0, 1]], base=0, channel_multiplier=P, allow_small_or_imprecise_dtypes=True))
            assert made[0] == CONSTS

            def root(rnd):
                for part, (lo, hi) in enumerate(((0, 4), (4, NB))):
                    pool.wait_ge(ve_ready, 2 * rnd + part + 1)
                    g.tensor_tensor(RSTD[:, lo:hi], VE[:, lo:hi], mhalf[:, lo:hi], ALU.pow).then_inc(rstd_ready, 1)
                    if rnd == 3:
                        g.tensor_tensor(RMS[:, lo:hi], VE2[:, lo:hi], mhalf[:, lo:hi], ALU.pow).then_inc(rstd_ready, 1)

            def root1(b):
                pool.wait_ge(rq_ready, b + 1)
                g.tensor_tensor(rms[:, 2:3], rms[:, 1:2], mhalf[:, 0:1], ALU.pow).then_inc(rr_ready, 1)

            pool.sem_inc(u_ready, 4)

            def mix(n):
                pre = vT if n == 0 else cT
                pool.wait_ge(call_in[n], 16)
                with pool.Fori(0, NB // 4) as i:
                    for u in range(4):
                        b = i * 4 + u
                        pool.wait_ge(v_ready, b + (NB * n + 1))
                        g.tensor_tensor(U[:, ds(b, 1), :].rearrange("p b l -> p (b l)"), Vb[u],
                                        CALL[:, ds(b, 1), :].rearrange("p b l -> p (b l)"), ALU.mult)\
                            .then_inc(u_ready, 1)
                pool.wait_ge(vt_taken, 4 + NB * (n + 1))

                def products(h, u):
                    pool.wait_ge(y_full, h * 2 + (32 * n + 2))
                    for blk in range(2):
                        a = pre[:, blk, :, ds(h * MD, MD)].unsqueeze(3).to_broadcast([P, NB, MD, MD])
                        c = cT[:, blk, :, ds(h * MD, MD)].unsqueeze(2).to_broadcast([P, NB, MD, MD])
                        g.tensor_tensor(kv[u][blk].rearrange("p (b i j) -> p b i j", b=NB, i=MD), a, c,
                                        ALU.mult).then_inc(kv_ready, 1)
                products(0, 0)
                pool.wait_ge(g_taken, 2 + 8 * (n + 1))
                products(1, 1)
                with pool.Fori(1, MH // 2) as i:
                    for u in range(2):
                        products(i * 2 + u, u)

            def scatter(n, rounds, j_count, pos, rows, done):
                pool.wait_ge(pos_ready[n], rounds + 1)
                pool.wait_ge(row_ready[n], rounds + 1)
                settle(pool, pool_settled)
                for j in range(j_count):
                    for k in range(TOPK[n]):
                        g.indirect_dma_start(
                            out=xs[n][:, :], out_offset=bass.IndirectOffsetOnAxis(ap=pos[:, j, k:k + 1], axis=0),
                            in_=rows[:, j, :], in_offset=None).then_inc(done, 16)

            def moe(n):
                m = ML[n]
                pool.sem_inc(m["ok"], 2)
                pool.wait_ge(acc_in[n], (16 if n else 4) * 16 + 32)
                pool.wait_ge(tab_ready[n], 1)
                pairs = pool.value_load(tab[0:1, 2 * TMAX:2 * TMAX + 1], min_val=1, max_val=TILES[n] // 2 + 1)
                with pool.Fori(0, pairs) as i:
                    for u in range(2):
                        t = i * 2 + u
                        pool.wait_ge(m["id"], t + 2)
                        pool.wait_ge(m["y"], t + 1)
                        settle(pool, pool_settled)
                        settle(pool, pool_settled)
                        g.indirect_dma_start(
                            out=acc[n][u][:, :], out_offset=bass.IndirectOffsetOnAxis(
                                ap=ids[u][:], axis=0),
                            in_=yt[u], in_offset=None, compute_op=ALU.add).then_inc(added[n][u], 16)
                    for u in range(2):
                        pool.wait_ge(added[n][u], i * 16 + 16)
                        pool.sem_inc(m["ok"], 1)
                for k in ("act", "xt_ready", "meta", "at"):
                    pool.wait_ge(m[k], pairs * 2 + 3)
                pool.sem_inc(moe_done[n], 1)

            def rope(p, n):
                if n == 0:
                    need(pool, td_full, turned(p, 2, -1))
                pool.wait_ge(rope_taken, p * 5 + (n + 1))
                if n:
                    q = Qr[:, (n - 1) * 512:n * 512]
                    g.tensor_tensor(q, q, Bt[n % 2], ALU.add).then_inc(rp_ready, 1)
                else:
                    def twice(v):
                        return v.rearrange("p (g d) -> p g d", g=KH).unsqueeze(2).to_broadcast([P, KH, 2, HD])
                    g.tensor_tensor(Kd, twice(KA), twice(Bt[0]), ALU.add).then_inc(rp_ready, 1)

            root(0)
            mix(0)
            root(1)
            for g4 in range(4):
                scatter(0, g4, 4, POS0[g4 % 2], HR0[g4 % 2], scattered0[g4 % 2])
            moe(0)
            root(2)
            mix(1)
            pool.wait_ge(x_done, 16)
            g.memset(maskneg, 0.0).then_inc(consts, 1)
            pool.wait_ge(consts, CONSTS + 1)
            g.affine_select(out=maskneg, in_=maskneg, compare_op=ALU.is_ge, fill=-1e30, base=0,
                            pattern=[[-1, P]], channel_multiplier=1).then_inc(consts, 1)
            root(3)

            def body(b):
                if there(b + 1):
                    rope(b + 1, 0)
                    rope(b + 1, 1)
                    rope(b + 1, 2)
                if there(b - 2):
                    scatter(1, b - 2, 1, POS1, HR1, scattered1)
                if there(b + 1):
                    rope(b + 1, 3)
                if there(b - 1):
                    root1(b - 1)
                if there(b + 1):
                    rope(b + 1, 4)
            steps(pool, body)
            padding(pool, 1, 6, E // 2, pad_pool)
            moe(1)

        @block.scalar
        def _(act):
            a = nc.scalar
            act.sem_inc(vt_taken, 4)

            def mix(n):
                if n == 0:
                    for p in range(NB // 2):
                        act.wait_ge(ct_full, p + 1)
                        a.copy(cT[:, :, 2 * p:2 * p + 2, :],
                               PS[:, 4 + p % 2, :].rearrange("p (b k s) -> p k b s", b=2, k=2)).then_inc(ct_taken, 1)
                with act.Fori(0, NB // 4) as i:
                    for u in range(4):
                        b = i * 4 + u
                        act.wait_ge(vt_full, b + (NB * n + 5))
                        a.copy(vT[:, :, ds(b, 1), :].rearrange("p k b s -> p k (b s)"),
                               PS[:, u, 0:D].rearrange("p (k s) -> p k s", k=2)).then_inc(vt_taken, 1)

            def gate_exp(n, r):
                act.wait_ge(ex_in[n], r + 1)
                a.activation(RB[n]["EX"], RB[n]["EX"], ACT.Exp).then_inc(ex_out[n], 1)

            def ffn0():
                def silu(s, c):
                    act.wait_ge(up_full, 3 * s + c + 1)
                    need(act, at_ready, 3 * s + c - 2)
                    r = SCH[c]
                    a.activation(sgT[0:r, c, :], PS[0:r, 2 * ((3 * s + c) % 2), :], ACT.Silu).then_inc(sg_ready, 1)

                for g in range(4):
                    for j in range(4):
                        b = 4 * g + j
                        act.wait_ge(ht_full, b + 1)
                        a.copy(hTa[:, :, b * P:(b + 1) * P],
                               PS[:, 6 + j % 2, 0:D].rearrange("p (k s) -> p k s", k=2)).then_inc(ht_taken, 1)
                    if g < 3:
                        silu(g, 0)
                    gate_exp(0, g)
                    if g == 3:
                        silu(g, 0)
                    silu(g, 1)
                    silu(g, 2)

            def moe(n):
                m = ML[n]
                inter = INTER[n]

                def x_t(t, u, first):
                    act.wait_ge(m["t1_full"], t + 1)
                    if not first:
                        act.wait_ge(m["up_full"], t - 1)
                    a.copy(xTt[u], PS[:, u, 0:D].rearrange("p (k s) -> p k s", k=2)).then_inc(m["xt_ready"], 1)

                def silu(t, u):
                    act.wait_ge(m["up_full"], t + 1)
                    need(act, m["act"], t)
                    a.activation(sg[u][:, 0:inter], PS[:, 2 + u, 0:inter], ACT.Silu).then_inc(m["silu"], 1)

                act.wait_ge(tab_ready[n], 1)
                x_t(0, 0, True)
                silu(0, 0)
                x_t(1, 1, True)
                silu(1, 1)
                x_t(2, 0, False)
                pairs = act.value_load(tab[0:1, 2 * TMAX:2 * TMAX + 1], min_val=1, max_val=TILES[n] // 2 + 1)
                with act.Fori(0, pairs) as i:
                    for u in range(2):
                        t = i * 2 + u
                        silu(t + 2, u)
                        x_t(t + 3, 1 - u, False)
                        act.wait_ge(m["down_full"], t + 2)
                        act.wait_ge(m["ok"], t + 1)
                        a.copy(yt[u], PS[:, 6 + u, 0:D]).then_inc(m["y"], 1)

            def side_copy(b, k, dst, cols, waits=()):
                act.wait_ge(side_full, side(b, k))
                for s, v in waits:
                    need(act, s, v)
                a.copy(dst, PS[:, 7, 0:cols]).then_inc(side_taken, 1)

            def exps(b, i):
                act.wait_ge(nb_ready, b * 4 + (i + 1))
                for r in range(8):
                    par, q = r % 2, r // 2
                    s = SM[i % 2][par][:, q, :]
                    ins = a.activation(s, s, ACT.Exp, bias=nbias[i % 2][:, par, q:q + 1], scale=HD ** -0.5,
                                       accum_out=rs[i % 2][:, par, q:q + 1])
                ins.then_inc(ex_ready, 1)

            def p_t(b, i):
                act.wait_ge(ta_full, turned(b, 2 * i + 1))
                a.copy(PT[0], PS[:, 4, :].rearrange("p (r q) -> p r q", r=4)).then_inc(ta_taken, 1)

            def q_t(b, i):
                c = (i - 1) % 4
                act.wait_ge(ta_full, turned(b, 2 * i + 2))
                a.copy(qT[:, 4 * c:4 * c + 4, :], PS[:, 4, :].rearrange("p (r q) -> p r q", r=4)).then_inc(ta_taken, 1)

            def v_sb(p):
                act.wait_ge(proj_full, p * 6 + 5)
                a.copy(Vs[:, ds(p % 2, 1), :].rearrange("p a d -> p (a d)"), PS[:, 3, :]).then_inc(v_taken, 1)

            def outs(c):
                return OT[:, 4 * c:4 * c + 4, :].rearrange("p r q -> p (r q)")

            mix(0)
            act.wait_ge(x_done, 8)
            ffn0()
            padding(act, 0, 6, E // 2, pad_act)
            moe(0)
            act.wait_ge(moe_done[0], 1)
            mix(1)
            act.wait_ge(x_done, 16)

            def body(b):
                for i in range(4):
                    prev = b if i else b - 1
                    coming = b + 1 if i else b
                    if i == 0:
                        if there(b + 1):
                            side_copy(b, 1, hT.rearrange("p k s -> p (k s)"), D)
                        if there(prev):
                            p_t(b, i)
                        if there(b - 1):
                            side_copy(b, 2, outs(2), 512)
                    if i == 1 and there(b - 1):
                        side_copy(b, 4, outs(3), 512)
                    if i >= 2 and there(b):
                        side_copy(b, 4 + i, outs(i - 2), 512)
                    if i == 1 and there(b - 2):
                        gate_exp(1, b - 2)
                    if i == 3 and there(b + 1):
                        v_sb(b + 1)
                    if i and there(prev):
                        p_t(b, i)
                    if i == 0 and there(b - 2):
                        side_copy(b, 3, RB[1]["LG"].rearrange("p b e -> p (b e)"), E,
                                  [(m_ready[1], b - 2)])
                    if i == 1 and there(b - 2):
                        side_copy(b, 5, RB[1]["RS"].rearrange("p b e -> p (b e)"), E)
                    if there(b):
                        exps(b, i)
                    if i == 3 and there(b - 1):
                        side_copy(b, 8, h2T.rearrange("p k s -> p (k s)"), D)
                    if there(coming):
                        q_t(b, i)
            steps(act, body)
            padding(act, 1, 3, 6, pad_act)
            moe(1)

        @block.tensor
        def _(pe):
            mm, tr = nc.tensor.matmul, nc.tensor.transpose
            pe.sem_inc(vt_full, 4)
            pe.sem_inc(y_full, 4)
            pe.wait_ge(consts, CONSTS)

            def mix(n):
                if n == 0:
                    pe.wait_ge(call_in[0], 16)
                    for p in range(NB // 2):
                        need(pe, ct_taken, p - 1)
                        for q in range(4):
                            ins = tr(PS[:, 4 + p % 2, q * P:(q + 1) * P],
                                     CALL[:, 2 * p + q // 2, (q % 2) * P:(q % 2 + 1) * P], ident[:])
                        ins.then_inc(ct_full, 1)
                def turns(i):
                    for u in range(4):
                        b = i * 4 + u
                        pe.wait_ge(v_ready, b + (NB * n + 1))
                        pe.wait_ge(vt_taken, b + (NB * n + 1))
                        for k in range(2):
                            ins = tr(PS[:, u, k * P:(k + 1) * P], Vb[u][:, k * P:(k + 1) * P], ident[:])
                        ins.then_inc(vt_full, 1)

                def sums(i):
                    for u in range(2):
                        p = i * 2 + u
                        pe.wait_ge(u_ready, p * 2 + (NB * n + 6))
                        pe.wait_ge(g_taken, p + (8 * n + 1))
                        mm(PS[:, 6 + u, :], group_s[:], U[:, ds(p * 2, 2), :].rearrange("p b l -> p (b l)"),
                           start=True, stop=True).then_inc(g_full, 1)

                turns(0)
                pe.wait_ge(gs_ready, n + 1)
                with pe.Fori(1, NB // 4) as i:
                    turns(i)
                    sums(i - 1)
                sums(NB // 4 - 1)
                pe.wait_ge(vt_taken, 4 + NB * (n + 1))
                with pe.Fori(0, MH // 4) as i:
                    for u in range(4):
                        h = i * 4 + u
                        pe.wait_ge(t_in[u], i * 16 + (MH // 4 * 16 * n + 16))
                        for blk in range(2):
                            pe.wait_ge(kv_ready, h * 2 + (32 * n + blk + 1))
                            pe.wait_ge(z_ready, h * 2 + (32 * n + blk + 1))
                            for half in range(2):
                                bank = PS[:, 4 * (u % 2) + 2 * blk + half, :]
                                c = slice(512 * half, 512 * half + 512)
                                if blk:
                                    mm(bank, TZ[u][:, P:D], kv[u % 2][0][:, c], start=True, stop=False)
                                ins = mm(bank, TZ[u][:, 0:P], kv[u % 2][blk][:, c], start=(blk == 0), stop=True)
                            ins.then_inc(y_full, 1)
                pe.wait_ge(z_ready, 4 + 32 * (n + 1))
                pe.wait_ge(dl_ready, 2 + 32 * (n + 1))
                for p in range(8):
                    for q in range(4):
                        ins = tr(PS[:, p, q * P:(q + 1) * P], dT[:, q % 2, 2 * p + q // 2, :], ident[:])
                    ins.then_inc(dt_full, 1)

            def rank(n, nb, bank, cols, full):
                mm(bank[:, 0:cols], tri[:], RB[n]["M"].rearrange("p b e -> p (b e)"), start=True, stop=False)
                mm(bank[:, 0:cols], ones[:], mcum[:, 0:nb, :].rearrange("p b e -> p (b e)"),
                   start=False, stop=True).then_inc(full, 1)

            def ffn0():
                pe.wait_ge(ws_in, 64)
                for g in range(4):
                    for j in range(4):
                        pe.wait_ge(h_ready[0], 4 * g + j + 1)
                        if j == 0:
                            need(pe, lg_taken, g)
                        elif j == 1:
                            need(pe, rk_taken[0], g)
                        else:
                            pe.wait_ge(ht_taken, 4 * g + j - 1)
                        for k in range(2):
                            ins = tr(PS[:, 6 + j % 2, k * P:(k + 1) * P], HR0[g % 2][:, j, k * P:(k + 1) * P],
                                     ident[:])
                        ins.then_inc(ht_full, 1)
                    pe.wait_ge(ht_taken, 4 * g + 4)
                    for j in range(4):
                        b = 4 * g + j
                        for k in range(2):
                            ins = mm(PS[:, 6, j * E:(j + 1) * E], hTa[:, k, b * P:(b + 1) * P], GT0[:, k, :],
                                     start=(k == 0), stop=(k == 1))
                    ins.then_inc(lg_full, 1)
                    if g:
                        down(g - 1)
                    if g < 3:
                        up(g, 0)
                    pe.wait_ge(m_ready[0], g + 1)
                    rank(0, 4, PS[:, 7, :], 64, rk_full)
                    if g < 3:
                        up(g, 1)
                        up(g, 2)
                up(3, 0)
                pe.wait_ge(rk_taken[0], 4)
                count(0)
                up(3, 1)
                tile_rows(0)
                up(3, 2)
                down(3)

            def down(s):
                pe.wait_ge(at_ready, 3 * s + 3)
                for j in range(4):
                    if j % 2 == 0:
                        need(pe, dn_taken, 2 * s - 1 + j // 2)
                    for c in range(3):
                        r = SCH[c]
                        ins = mm(PS[:, 4 + j // 2, (j % 2) * D:(j % 2 + 1) * D],
                                 aTg[0:r, c, j * P:(j + 1) * P], SDN[0:r, c, :], start=(c == 0), stop=(c == 2))
                    if j % 2:
                        ins.then_inc(dn_full, 1)

            def up(s, c):
                need(pe, at_ready, 3 * s + c - 1)
                r = SCH[c]
                for half in range(2):
                    for k in range(2):
                        c0 = half * SI + c * P
                        ins = mm(PS[0:r, 2 * ((3 * s + c) % 2) + half, :], SGU[:, k, c0:c0 + r],
                                 hTa[:, k, 4 * P * s:4 * P * (s + 1)], start=(k == 0), stop=(k == 1))
                ins.then_inc(up_full, 1)

            def count(n):
                mm(PS[:, 7, 0:E], ones[:], mcum[:, 0, :], start=True, stop=True).then_inc(cnt_full[n], 1)

            def tile_rows(n):
                pe.wait_ge(tile_ready[n], 1)
                for q in range(2):
                    ins = tr(PS[0:1, 7, (q + 1) * P:(q + 2) * P], ter[:, q:q + 1], ident[:])
                ins.then_inc(tile_full[n], 1)

            def moe(n):
                m = ML[n]
                inter, kr = INTER[n], KROWS[n]
                up = GU if n == 0 else W13
                down = DN if n == 0 else W2

                def t1(t, loads, u):
                    pe.wait_ge(xin[n][u], loads)
                    need(pe, m["xt_ready"], t - 1)
                    for k in range(2):
                        ins = tr(PS[:, u, k * P:(k + 1) * P], xt[u][:, k * P:(k + 1) * P], ident[:])
                    ins.then_inc(m["t1_full"], 1)

                def ups(t, u, e):
                    pe.wait_ge(m["xt_ready"], t + 1)
                    need(pe, m["act"], t)
                    for k in range(2):
                        ins = mm(PS[:, 2 + u, 0:2 * inter], xTt[u][:, k, :],
                                 up[:, k, ds(e, 1), :].rearrange("p e j -> p (e j)"), start=(k == 0), stop=(k == 1))
                    ins.then_inc(m["up_full"], 1)

                def t2(t, u):
                    pe.wait_ge(m["act"], t + 2)
                    pe.wait_ge(m["at"], t + 1)
                    for k in range(2):
                        ins = tr(PS[0:kr, 4 + u, k * P:(k + 1) * P], am[u][:, k * kr:(k + 1) * kr], ident[:])
                    ins.then_inc(m["t2_full"], 1)

                pe.sem_inc(m["down_full"], 1)
                pe.sem_inc(m["t2_full"], 1)
                pe.wait_ge(tab_ready[n], 1)
                pe.wait_ge(wd_in if n else we_in, 16 * 2 * E)
                t1(0, 16, 0)
                ups(0, 0, pe.value_load(tab[0:1, 0:1], min_val=0, max_val=E - 1))
                t1(1, 16, 1)
                ups(1, 1, pe.value_load(tab[0:1, 1:2], min_val=0, max_val=E - 1))
                t2(0, 0)
                t1(2, 32, 0)
                if n:
                    pe.wait_ge(w2_in, 32)
                pairs = pe.value_load(tab[0:1, 2 * TMAX:2 * TMAX + 1], min_val=1, max_val=TILES[n] // 2 + 1)
                with pe.Fori(0, pairs) as i:
                    e = packed(pe, i)
                    for u in range(2):
                        t = i * 2 + u
                        ups(t + 2, u, e[u + 2])
                        t2(t + 1, 1 - u)
                        t1(t + 3, i * 16 + 32 + 16 * u, 1 - u)
                        pe.wait_ge(m["at"], t + 3)
                        pe.wait_ge(m["ok"], t + 1)
                        for k in range(2):
                            ins = mm(PS[:, 6 + u, 0:D], aTt[u][0:kr, k, :],
                                     down[:, k, ds(e[u], 1), :].rearrange("p e j -> p (e j)"),
                                     start=(k == 0), stop=(k == 1))
                        ins.then_inc(m["down_full"], 1)

            def side_turn(b, k, src, s, v, n):
                pe.wait_ge(s, v)
                need(pe, side_taken, side(b, k - 1))
                for q in range(n):
                    ins = tr(PS[:, 7, q * P:(q + 1) * P], src[:, q * P:(q + 1) * P], ident[:])
                ins.then_inc(side_full, 1)

            def proj(p, c):
                if c == 0:
                    need(pe, rope_taken, p * 5)
                elif c == 1:
                    need(pe, v_taken, p)
                elif c == 4:
                    need(pe, wo_taken, p - 1)
                else:
                    pe.wait_ge(rope_taken, p * 5 + (c if c < 4 else 4))
                w = WK if c == 0 else WV if c == 5 else WQ[:, :, (c - 1) * 512:c * 512]
                for k in range(2):
                    ins = mm(PS[:, 2 if c in (0, 4) else 3, :], hT[:, k, :], w[:, k, :], start=(k == 0), stop=(k == 1))
                ins.then_inc(proj_full, 1)

            def q_t(b, i, p):
                c = (i - 1) % 4
                pe.wait_ge(rp_ready, p * 5 + (c + 2))
                need(pe, ta_taken, turned(b, 2 * i + 1))
                need(pe, td_taken, turned(b, 2 * i + 1))
                for q in range(4):
                    ins = tr(PS[:, 4, q * P:(q + 1) * P], Qr[:, (4 * c + q) * P:(4 * c + q + 1) * P], ident[:])
                ins.then_inc(ta_full, 1)
                for q in range(2):
                    ins = tr(PS[:, 5, q * P:(q + 1) * P], Kd[:, 2 * c + q].rearrange("p a d -> p (a d)"), ident[:])
                ins.then_inc(td_full, 1)

            def score(b, i):
                v = turned(b, 2 * i + 4, -1) if i < 3 else turned(b, 2)
                pe.wait_ge(ta_taken, v)
                pe.wait_ge(td_taken, v)
                need(pe, sm_taken, b * 8 + 2 * i)
                for r in range(8):
                    h = 8 * i + r
                    par, q = r % 2, r // 2
                    rows = slice(par * HD, par * HD + HD)
                    ins = mm(PS[:, par, q * P:(q + 1) * P], qT[rows, h // 2, :], kTd[rows, h // 4, :],
                             start=True, stop=True)
                    if r >= 6:
                        ins.then_inc(s_full, 1)

            def p_t(b, i):
                pe.wait_ge(ex_ready, b * 4 + i)
                need(pe, ta_taken, turned(b, 2 * i))
                need(pe, td_taken, turned(b, 2 * i))
                for par in range(2):
                    for q in range(4):
                        ins = tr(PS[:, 4 + par, q * P:(q + 1) * P], SM[(i - 1) % 2][par][:, q, :], ident[:])
                    ins.then_inc(td_full if par else ta_full, 1)

            def pv(b, i, p):
                pe.wait_ge(ta_taken, turned(b, 2 * i + 1))
                pe.wait_ge(td_taken, turned(b, 2 * i + 1))
                if i == 1:
                    pe.wait_ge(v_taken, b + 1)
                need(pe, o_taken, b * 4 + (i - 1))
                for r in range(8):
                    g = (8 * ((i - 1) % 4) + r) // 4
                    ins = mm(PS[:, 6, r * HD:(r + 1) * HD], PT[r % 2][:, r // 2, :],
                             Vs[:, ds(p % 2, 1), g * HD:(g + 1) * HD].rearrange("p a d -> p (a d)"),
                             start=True, stop=True)
                ins.then_inc(pv_full, 1)

            def w_o(b, half):
                if half == 0:
                    pe.wait_ge(rope_taken, b * 5 + 6 if there(b + 1) else NB * 5)
                pe.wait_ge(side_taken, side(b, 4 if half else 2))
                for t in range(8 * half, 8 * half + 8):
                    ins = mm(PS[:, 2, 0:D], OT[:, t, :], WO[:, t, :], start=(t == 0), stop=(t == 15))
                if half:
                    ins.then_inc(wo_full, 1)

            def logits(b):
                need(pe, side_taken, side(b, 2))
                for k in range(2):
                    ins = mm(PS[:, 7, 0:E], h2T[:, k, :], wg_s[:, k, :], start=(k == 0), stop=(k == 1))
                ins.then_inc(side_full, 1)

            def rank1(b):
                pe.wait_ge(m_ready[1], b - 1)
                need(pe, side_taken, side(b, 4))
                rank(1, 1, PS[:, 7, :], E, side_full)

            mix(0)
            pe.wait_ge(x_done, 8)
            ffn0()
            pe.wait_ge(dn_taken, 8)
            moe(0)
            pe.wait_ge(moe_done[0], 1)
            mix(1)
            pe.wait_ge(x_done, 16)
            pe.wait_ge(wr_in, 48)
            pe.wait_ge(misc_in, 48)

            def body(b):
                for i in range(4):
                    prev = b if i else b - 1
                    coming = b + 1 if i else b
                    if there(b):
                        score(b, i)
                    if i == 0 and there(b + 1):
                        side_turn(b, 1, Hd, h_ready[1], b + 2, 2)
                    if i == 0 and there(prev):
                        p_t(b, i)
                    last = b if i > 1 else b - 1
                    if there(last):
                        side_turn(b, (2, 4, 6, 7)[i], On, o_taken, b * 4 + (i - 1), 4)
                    if i == 0 and there(b + 1):
                        pe.wait_ge(side_taken, side(b, 1))
                        proj(b + 1, 0)
                    if i == 1 and isinstance(b, int) and b == 1:
                        pe.wait_ge(wo_in, 16)
                    if i in (1, 2) and there(b - 1):
                        w_o(b, i - 1)
                    if i == 3 and there(b + 1):
                        proj(b + 1, 5)
                    if i and there(prev):
                        p_t(b, i)
                    if i == 0 and there(b - 2):
                        logits(b)
                    if i == 1 and there(b - 2):
                        rank1(b)
                    if there(b + 1):
                        proj(b + 1, i + 1)
                    if there(prev):
                        pv(b, i, prev)
                    if i == 3 and there(b - 1):
                        side_turn(b, 8, HR1[:, 0, 0:D], row_feat, b, 2)
                    if there(coming):
                        q_t(b, i, coming)
            steps(pe, body)
            pe.wait_ge(side_taken, side(NB + 1, 8))
            pe.wait_ge(rk_taken[1], NB)
            count(1)
            tile_rows(1)
            pe.wait_ge(td_taken, turned(NB + 1, 8))
            pe.wait_ge(wo_taken, NB)
            moe(1)

        @block.vector
        def _(dve):
            v = nc.vector
            ch = Chain(dve, dve_seq)
            dve.sem_inc(g_taken, 2)
            dve.sem_inc(g_res, 2)
            dve.sem_inc(z_ready, 4)
            dve.sem_inc(dl_ready, 2)
            dve.wait_ge(consts, CONSTS)

            def ln_stats(rnd, arrived):
                for q in range(4):
                    dve.wait_ge(arrived[q], 32 if arrived is x_back else 16)
                    if arrived is x_back:
                        xq = X[:, 4 * q:4 * q + 4, :]
                        ch.link(v.tensor_tensor(xq, xq, S1[0][:, 4 * q:4 * q + 4, :], ALU.add))
                    for b in range(4 * q, 4 * q + 4):
                        stats(b)
                    if q == 0:
                        ln_roots(rnd, 0, 4)
                ln_roots(rnd, 4, NB)

            def stats(b):
                v.bn_stats(st6[:, b, :], X[:, b, :]).then_inc(st_done, 1)

            def ln_roots(rnd, lo, hi):
                r = slice(lo, hi)
                d, m2, var, ve = dd[:, r], M2[:, r], VAR[:, r], VE[:, r]
                dve.wait_ge(st_done, NB * rnd + hi)
                ch.link(v.tensor_tensor(s12[:, r, :], st6[:, r, 1:3], st6[:, r, 4:6], ALU.add))
                ch.link(v.tensor_tensor(d, st6[:, r, 1], st6[:, r, 4], ALU.subtract))
                ch.link(v.tensor_scalar(MEAN[:, r], s12[:, r, 0], 0.5, None, ALU.mult))
                ch.link(v.tensor_tensor(d, d, d, ALU.mult))
                ch.link(v.tensor_scalar(m2, s12[:, r, 1], 1.0 / D, None, ALU.mult))
                ch.link(v.scalar_tensor_tensor(out=var, in0=d, scalar=0.25, in1=m2, op0=ALU.mult, op1=ALU.add))
                if rnd < 3:
                    v.tensor_scalar(ve, var, EPS, None, ALU.add).then_inc(ve_ready, 1)
                else:
                    ch.link(v.tensor_scalar(ve, var, EPS, None, ALU.add))
                    ch.link(v.reciprocal(d, ve))
                    ch.link(v.tensor_tensor(d, d, var, ALU.mult))
                    v.tensor_scalar(VE2[:, r], d, EPS, None, ALU.add).then_inc(ve_ready, 1)

            def mix(n, ahead):
                post = cT if n == 0 else vT
                ln_stats(2 * n, x_back if n else x_in)
                if n == 0:
                    dve.wait_ge(misc_in, 48)
                v.tensor_scalar(group_s[:], group[:], skip_s[:, n:n + 1], None, ALU.mult).then_inc(gs_ready, 1)
                def four(i):
                    for u in range(4):
                        b = i * 4 + u
                        dve.wait_ge(vt_full, b + (NB * n + 1))
                        dve.wait_ge(u_ready, b + (NB * n + 1))
                        v.tensor_scalar(Vb[u], X[:, ds(b, 1), :].rearrange("p b l -> p (b l)"), MEAN[:, ds(b, 1)],
                                        RSTD[:, ds(b, 1)], ALU.subtract, ALU.mult).then_inc(v_ready, 1)

                def sums(i):
                    for u in range(2):
                        p = i * 2 + u
                        dve.wait_ge(g_full, p + (8 * n + 1))
                        dve.wait_ge(g_res, p + (8 * n + 1))
                        v.tensor_tensor(gtmp[u], PS[:, 6 + u, :].rearrange("p (b l) -> p b l", b=2),
                                        CALL[:, ds(p * 2, 2), :], ALU.mult).then_inc(g_taken, 1)
                    for u in range(2):
                        p = i * 2 + u
                        dve.wait_ge(g_taken, p + (8 * n + 3))
                        xp = X[:, ds(p * 2, 2), :]
                        v.tensor_tensor(xp, xp, gtmp[u], ALU.add).then_inc(g_res, 1)

                dve.wait_ge(rstd_ready, 4 * n + 1)
                four(0)
                dve.wait_ge(rstd_ready, 4 * n + 2)
                four(1)
                with dve.Fori(2, NB // 4) as i:
                    four(i)
                    sums(i - 2)
                sums(NB // 4 - 2)
                sums(NB // 4 - 1)
                dve.wait_ge(vt_taken, 4 + NB * (n + 1))
                dve.wait_ge(g_full, 8 * (n + 1))
                dve.wait_ge(g_res, 8 * (n + 1) + 2)
                with dve.Fori(0, MH // 2) as i:
                    for u in range(2):
                        h = i * 2 + u
                        for blk in range(2):
                            dve.wait_ge(y_full, h * 2 + (32 * n + blk + 5))
                            dve.wait_ge(dl_ready, h * 2 + (32 * n + blk + 1))
                            a = post[:, blk, :, ds(h * MD, MD)].unsqueeze(3).to_broadcast([P, NB, MD, MD])
                            y = PS[:, 4 * u + 2 * blk:4 * u + 2 * blk + 2, :].rearrange(
                                "p k (b i j) -> p (k b) i j", i=MD, j=MD)
                            v.tensor_tensor(weighted[blk].rearrange("p (b i j) -> p b i j", i=MD, j=MD),
                                            y, a, ALU.mult).then_inc(z_ready, 1)
                        for blk in range(2):
                            dve.wait_ge(z_ready, h * 2 + (32 * n + blk + 5))
                            v.tensor_reduce(dT[:, blk, :, ds(h * MD, MD)],
                                            weighted[blk].rearrange("p (b i j) -> p b j i", i=MD, j=MD),
                                            AX.X, ALU.add).then_inc(dl_ready, 1)
                for p in range(9):
                    if p < 8:
                        dve.wait_ge(dt_full, 8 * n + p + 1)
                        xp = X[:, 2 * p:2 * p + 2, :].rearrange("p b l -> p (b l)")
                        v.tensor_tensor(xp, xp, PS[:, p, :], ALU.add).then_inc(x_done, 1)
                    if p:
                        dve.wait_ge(x_done, 8 * n + p)
                        stats(2 * p - 2)
                        stats(2 * p - 1)
                    if p == 2:
                        ln_roots(2 * n + 1, 0, 4)
                ahead()
                ln_roots(2 * n + 1, 4, NB)

            def picks(n, nb, r):
                R, k = RB[n], TOPK[n]
                for j in range(nb):
                    settle(dve, dve_settled)
                    ch.link(v.max(R["TV"][:, j, :], R["LG"][:, j, :]))
                    settle(dve, dve_settled)
                    ch.link(v.max_index(TI[n][:, j, :], R["TV"][:, j, :], R["LG"][:, j, :]))
                v.tensor_tensor(R["EX"], R["LG"], R["TV"][:, :, 0:1].to_broadcast([P, nb, E]),
                                ALU.subtract).then_inc(ex_in[n], 1)
                ch.link(v.tensor_copy(R["TIF"], TI[n][:, :, 0:k]))
                ch.link(v.tensor_tensor(
                    R["OH"], iota_e[:].unsqueeze(1).unsqueeze(1).to_broadcast([P, nb, k, E]),
                    R["TIF"].unsqueeze(3).to_broadcast([P, nb, k, E]), ALU.is_equal))
                ch.link(v.tensor_reduce(R["M"], R["OH"].rearrange("p b k e -> p b e k"), AX.X, ALU.add))
                for j in range(nb):
                    ins = v.tensor_tensor(mcum[:, j + 1, :], mcum[:, j, :], R["M"][:, j, :], ALU.add)
                    if j < nb - 1:
                        ch.link(ins)
                ins.then_inc(m_ready[n], 1)

            def places(n, nb, bank, r, rows, pos):
                R, k = RB[n], TOPK[n]
                dve.wait_ge(ex_out[n], r + 1)
                ch.link(v.tensor_tensor(R["EM"], R["EX"], R["M"], ALU.mult))
                ch.link(v.tensor_reduce(R["DEN"], R["EX"] if n == 0 else R["EM"], AX.X, ALU.add))
                ch.link(v.reciprocal(R["RD"], R["DEN"]))
                v.tensor_tensor(rows[:, :, D:D + E], R["EM"], R["RD"].unsqueeze(2).to_broadcast([P, nb, E]),
                                ALU.mult).then_inc(row_ready[n], 1)
                if n == 0:
                    dve.wait_ge(rk_full, r + 1)
                ch.link(v.tensor_tensor(R["RK"], bank.rearrange("p (b e) -> p b e", e=E),
                                        row_e[:].unsqueeze(1).to_broadcast([P, nb, E]), ALU.add))
                v.tensor_copy(mcum[:, 0, :], mcum[:, nb, :]).then_inc(rk_taken[n], 1)
                ch.link(v.tensor_tensor(R["PR"], R["OH"], R["RK"].unsqueeze(2).to_broadcast([P, nb, k, E]),
                                        ALU.mult))
                ch.link(v.tensor_reduce(R["PF"], R["PR"], AX.X, ALU.add))
                v.tensor_copy(pos[:], R["PF"]).then_inc(pos_ready[n], 1)

            def rows(g):
                need(dve, scattered0[g % 2], g // 2 * (16 * 8))
                H = HR0[g % 2]
                for j in range(4):
                    b = 4 * g + j
                    v.tensor_copy(H[:, j, D + E:XCOLS].bitcast(I32), token_id[:, b:b + 1])
                    v.tensor_scalar(H[:, j, 0:D], X[:, b, :], MEAN[:, b:b + 1], RSTD[:, b:b + 1],
                                    ALU.subtract, ALU.mult).then_inc(h_ready[0], 1)

            def rows_of_first():
                dve.wait_ge(rstd_ready, 3)
                rows(0)

            def ffn0():
                ch.link(v.memset(mcum[:, 0, :], 0.0))

                def gated(s, c):
                    dve.wait_ge(up_full, 3 * s + c + 1)
                    dve.wait_ge(sg_ready, 3 * s + c + 1)
                    need(dve, dn_full, 2 * s)
                    r = SCH[c]
                    v.tensor_tensor(aTg[0:r, c, :], sgT[0:r, c, :], PS[0:r, 2 * ((3 * s + c) % 2) + 1, :], ALU.mult)\
                        .then_inc(at_ready, 1)

                def sums(s):
                    for q in range(2):
                        dve.wait_ge(dn_full, 2 * s + q + 1)
                        xp = X[:, 4 * s + 2 * q:4 * s + 2 * q + 2, :].rearrange("p b l -> p (b l)")
                        v.tensor_tensor(xp, xp, PS[:, 4 + q, :], ALU.add).then_inc(dn_taken, 1)

                dve.wait_ge(rstd_ready, 4)
                for g in range(4):
                    dve.wait_ge(lg_full, g + 1)
                    v.tensor_copy(RB[0]["LG"], PS[:, 6, 0:64].rearrange("p (b e) -> p b e", e=E))\
                        .then_inc(lg_taken, 1)
                    dve.wait_ge(lg_taken, g + 1)
                    picks(0, 4, g)
                    if g:
                        sums(g - 1)
                    if g < 3:
                        gated(g, 0)
                    places(0, 4, PS[:, 7, 0:64], g, HR0[g % 2], POS0[g % 2])
                    if g < 3:
                        rows(g + 1)
                        gated(g, 1)
                        gated(g, 2)
                ends(0)
                gated(3, 0)
                tiles(0)
                gated(3, 1)
                gated(3, 2)
                sums(3)

            def ends(n):
                dve.wait_ge(cnt_full[n], 1)
                cnt, pad, end, dg = (cnt_s[:, q, :] for q in range(4))
                ch.link(v.tensor_copy(cnt, PS[:, 7, 0:E]))
                c2 = cnt[0:1, :].rearrange("p (i u) -> p i u", u=2)
                v.scalar_tensor_tensor(out=tab[0:1, ENDS:ENDS + E // 2], in0=c2[:, :, 1], scalar=4096.0,
                                       in1=c2[:, :, 0], op0=ALU.mult, op1=ALU.add).then_inc(ends_ready[n], 1)
                ch.link(v.tensor_scalar(cnt_i[:, 0:E], cnt, float(P - 1), None, ALU.add))
                ch.link(v.tensor_scalar(cnt_i[:, E:2 * E], cnt_i[:, 0:E], 7, 7, ALU.arith_shift_right,
                                        ALU.logical_shift_left))
                ch.link(v.tensor_copy(pad, cnt_i[:, E:2 * E]))
                ch.link(v.tensor_tensor(lep, le_e[:], pad.unsqueeze(1).to_broadcast([P, E, E]), ALU.mult))
                ch.link(v.tensor_reduce(end, lep, AX.X, ALU.add))
                ch.link(v.tensor_scalar(dg, pad, -1.0, float(EROWS), ALU.mult, ALU.add))
                ch.link(v.tensor_tensor(tcmp[:, 0, :], tau[:].to_broadcast([P, E]), end, ALU.is_ge))
                ch.link(v.tensor_tensor(tcmp[:, 1, :], tcmp[:, 0, :], dg, ALU.mult))
                ch.link(v.tensor_reduce(ter[:, 0:1], tcmp[:, 0, 0:E - 1], AX.X, ALU.add))
                ch.link(v.tensor_reduce(ter[:, 1:2], tcmp[:, 1, :], AX.X, ALU.add))
                ch.link(v.tensor_tensor(ter[:, 1:2], ter[:, 1:2], tau[:], ALU.add))
                v.tensor_scalar(ter[:, 1:2], ter[:, 1:2], float(DUMMY), None, ALU.min).then_inc(tile_ready[n], 1)
                ch.link(v.tensor_scalar(n_pair[:], end[0:1, E - 1:E], float(P), None, ALU.add))
                ch.link(v.tensor_scalar(tab[0:1, 2 * TMAX:2 * TMAX + 1], n_pair[:], 8, None, ALU.arith_shift_right))

            def tiles(n):
                dve.wait_ge(tile_full[n], 1)
                row = PS[0:1, 7, P:3 * P].rearrange("p (a t) -> p a t", a=2)
                ch.link(v.tensor_copy(tab[0:1, 0:2 * TMAX].rearrange("p (a t) -> p a t", a=2), row[:, :, 0:TMAX]))
                e2 = tab[0:1, 0:TMAX].rearrange("p (i u) -> p i u", u=2)
                n2 = TMAX // 2 - 1
                ch.link(v.scalar_tensor_tensor(out=pk, in0=e2[:, 1:n2 + 1, 1], scalar=float(E), in1=e2[:, 1:n2 + 1, 0],
                                               op0=ALU.mult, op1=ALU.add))
                ch.link(v.scalar_tensor_tensor(out=pk, in0=pk, scalar=float(E), in1=e2[:, 0:n2, 1],
                                               op0=ALU.mult, op1=ALU.add))
                ch.link(v.scalar_tensor_tensor(out=pk, in0=pk, scalar=float(E), in1=e2[:, 0:n2, 0],
                                               op0=ALU.mult, op1=ALU.add))
                v.tensor_copy(tab[0:1, PACKED:PACKED + n2], pk).then_inc(tab_ready[n], 1)

            def moe(n):
                m = ML[n]
                inter, kr = INTER[n], KROWS[n]

                def gates(t, loads, u):
                    dve.wait_ge(xin[n][u], loads)
                    v.tensor_copy(meta[:, ds(t % 4 * META, E + 1)], xt[u][:, D:XCOLS]).then_inc(m["meta"], 1)

                def act_of(t, u, e):
                    dve.wait_ge(m["meta"], t + 1)
                    dve.wait_ge(m["silu"], t + 1)
                    need(dve, m["t2_full"], t)
                    v.scalar_tensor_tensor(out=am[u][:, 0:inter], in0=sg[u][:, 0:inter],
                                           scalar=meta[:, ds(t % 4 * META + e, 1)], in1=PS[:, 2 + u, inter:2 * inter],
                                           op0=ALU.mult, op1=ALU.mult).then_inc(m["act"], 1)

                def a_t(t, u):
                    dve.wait_ge(m["t2_full"], t + 2)
                    need(dve, m["down_full"], t)
                    v.tensor_copy(aTt[u][0:kr], PS[0:kr, 4 + u, 0:D].rearrange("p (k s) -> p k s", k=2))\
                        .then_inc(m["at"], 1)

                dve.sem_inc(m["at"], 2)
                dve.sem_inc(m["act"], 1)
                dve.sem_inc(m["id"], 1)
                dve.wait_ge(tab_ready[n], 1)
                gates(0, 16, 0)
                gates(1, 16, 1)
                act_of(0, 0, dve.value_load(tab[0:1, 0:1], min_val=0, max_val=E - 1))
                act_of(1, 1, dve.value_load(tab[0:1, 1:2], min_val=0, max_val=E - 1))
                a_t(0, 0)
                gates(2, 32, 0)
                pairs = dve.value_load(tab[0:1, 2 * TMAX:2 * TMAX + 1], min_val=1, max_val=TILES[n] // 2 + 1)
                with dve.Fori(0, pairs) as i:
                    e = packed(dve, i)
                    for u in range(2):
                        t = i * 2 + u
                        a_t(t + 1, 1 - u)
                        act_of(t + 2, u, e[u + 2])
                        dve.wait_ge(m["ok"], t + 1)
                        v.tensor_copy(ids[u][:], meta[:, ds(t % 4 * META + E, 1)].bitcast(I32)).then_inc(m["id"], 1)
                        dve.wait_ge(m["id"], t + 1)
                        gates(t + 3, i * 16 + 32 + 16 * u, 1 - u)

            def front(b, turned_h):
                xb = X[:, ds(b, 1), :].rearrange("p b l -> p (b l)")
                xd = XD[:, ds(b % 4, 1), :].rearrange("p b l -> p (b l)")
                dve.wait_ge(rstd_ready, 8 if isinstance(b, int) and b < 4 else 10)
                ch.link(v.tensor_scalar(xd, xb, MEAN[:, ds(b, 1)], RSTD[:, ds(b, 1)], ALU.subtract, ALU.mult))
                need(dve, side_full, turned_h)
                v.scalar_tensor_tensor(out=Hd, in0=xd, scalar=RMS[:, ds(b, 1)], in1=lnw_s, op0=ALU.mult, op1=ALU.mult)\
                    .then_inc(h_ready[1], 1)
                v.tensor_tensor(xb, xb, xd, ALU.add).then_inc(f_res, 1)

            def rope(p, n):
                dve.wait_ge(proj_full, p * 6 + (n + 1 if n < 4 else 6))
                need(dve, rp_ready, p * 5 + (n - 1 if n > 1 else 0))
                bank = PS[:, 2 if n in (0, 4) else 3, :]
                ps = bank.rearrange("p (h a d) -> p h a d", h=8, a=2)
                dst = (Qr[:, (n - 1) * 512:n * 512] if n else KA).rearrange("p (h d) -> p h d", h=8)
                bt = Bt[n % 2].rearrange("p (h a d) -> p h a d", h=8, a=2)
                H2 = HD // 2
                v.tensor_tensor(dst, bank.rearrange("p (h d) -> p h d", h=8),
                                cos_s.unsqueeze(1).to_broadcast([P, 8, HD]), ALU.mult)
                v.tensor_tensor(bt[:, :, 0, :], ps[:, :, 1, :],
                                sin_s[:, 0:H2].unsqueeze(1).to_broadcast([P, 8, H2]), ALU.mult)
                v.tensor_tensor(bt[:, :, 1, :], ps[:, :, 0, :],
                                sin_s[:, H2:HD].unsqueeze(1).to_broadcast([P, 8, H2]), ALU.mult)\
                    .then_inc(rope_taken, 1)

            def k_t(b, i):
                c = (i - 1) % 4
                dve.wait_ge(td_full, turned(b, 2 * i + 2))
                v.tensor_copy(kTd[:, 2 * c:2 * c + 2, :], PS[:, 5, 0:2 * P].rearrange("p (r q) -> p r q", r=2))\
                    .then_inc(td_taken, 1)

            def masked(b, i):
                for par in range(2):
                    dve.wait_ge(s_full, b * 8 + (2 * i + par + 1))
                    settle(dve, dve_settled)
                    for q in range(4):
                        ins = v.tensor_tensor_reduce(SM[i % 2][par][:, q, :], PS[:, par, q * P:(q + 1) * P], maskneg,
                                                     1.0, -3e38, ALU.add, ALU.max, mx[i % 2][:, par, q:q + 1])
                    ins.then_inc(sm_taken, 1)
                dve.wait_ge(sm_taken, b * 8 + (2 * i + 2))
                v.tensor_scalar(nbias[i % 2], mx[i % 2], -(HD ** -0.5), None, ALU.mult).then_inc(nb_ready, 1)

            def p_t(b, i):
                dve.wait_ge(td_full, turned(b, 2 * i + 1))
                v.tensor_copy(PT[1], PS[:, 5, :].rearrange("p (r q) -> p r q", r=4)).then_inc(td_taken, 1)
                j = (i - 1) % 2
                dve.wait_ge(ex_ready, b * 4 + i)
                v.reciprocal(rinv[j], rs[j]).then_inc(ri_ready, 1)

            def o_norm(b, i):
                dve.wait_ge(pv_full, b * 4 + i)
                dve.wait_ge(ri_ready, b * 4 + i)
                o4 = PS[:, 6, :].rearrange("p (q a d) -> p q a d", q=4, a=2)
                d4 = On.rearrange("p (q a d) -> p q a d", q=4, a=2)
                r4 = rinv[(i - 1) % 2].rearrange("p a q -> p q a").unsqueeze(3).to_broadcast([P, 4, 2, HD])
                v.tensor_tensor(d4, o4, r4, ALU.mult).then_inc(o_taken, 1)

            def post(b):
                dve.wait_ge(wo_full, b + 1)
                dve.wait_ge(f_res, b + 1)
                xb = X[:, ds(b, 1), :].rearrange("p b l -> p (b l)")
                xd = XD[:, ds(b % 4, 1), :].rearrange("p b l -> p (b l)")
                v.tensor_tensor(xb, xb, PS[:, 2, 0:D], ALU.add)
                v.tensor_tensor(X2[:], xd, PS[:, 2, 0:D], ALU.add).then_inc(wo_taken, 1)
                dve.wait_ge(wo_taken, b + 1)
                settle(dve, dve_settled)
                ch.link(v.tensor_tensor_reduce(squares[:], X2[:], X2[:], 1.0 / D, 0.0, ALU.mult, ALU.add, rms[:, 0:1]))
                v.tensor_scalar(rms[:, 1:2], rms[:, 0:1], EPS, None, ALU.add).then_inc(rq_ready, 1)

            def row(b):
                dve.wait_ge(rr_ready, b + 1)
                need(dve, scattered1, b * 64)
                v.tensor_copy(HR1[:, 0, D + E:XCOLS].bitcast(I32), token_id[:, ds(b, 1)])
                v.scalar_tensor_tensor(out=HR1[:, 0, 0:D], in0=X2[:], scalar=rms[:, 2:3], in1=fflnw_s,
                                       op0=ALU.mult, op1=ALU.mult).then_inc(row_feat, 1)

            mix(0, rows_of_first)
            ffn0()
            moe(0)
            mix(1, lambda: None)
            ch.link(v.memset(mcum[:, 0, :], 0.0))
            dve.wait_ge(d_in, 64)
            dve.wait_ge(consts, CONSTS + 2)
            front(0, 0)

            def body(b):
                for i in range(4):
                    prev = b if i else b - 1
                    coming = b + 1 if i else b
                    if i == 3 and there(b - 1):
                        post(b - 1)
                    if i == 3 and there(prev):
                        p_t(b, i)
                    if there(b):
                        masked(b, i)
                    if i < 3 and there(prev):
                        p_t(b, i)
                    if i == 0 and there(b + 1):
                        rope(b + 1, 0)
                    if i == 3 and there(b - 1):
                        row(b - 1)
                    if i == 0 and there(b - 2):
                        dve.wait_ge(side_taken, side(b, 3))
                        picks(1, 1, b - 2)
                    if there(prev):
                        o_norm(b, i)
                    if there(b + 1):
                        rope(b + 1, i + 1)
                    if there(coming):
                        k_t(b, i)
                    if i == 1 and there(b - 2):
                        dve.wait_ge(side_taken, side(b, 5))
                        places(1, 1, RB[1]["RS"].rearrange("p b e -> p (b e)"), b - 2, HR1, POS1)
                    if i == 2 and there(b + 2):
                        front(b + 2, side(b, 1))
            steps(dve, body, ch, 13)
            ends(1)
            tiles(1)
            moe(1)
            for q in range(4):
                dve.wait_ge(x_back[q], 64)
                xq = X[:, 4 * q:4 * q + 4, :]
                v.tensor_tensor(xq, xq, S1[1][:, 4 * q:4 * q + 4, :], ALU.add).then_inc(summed, 1)


_NAMES = ["x", "ctx", "conv_k", "skip", "gate_t", "gu", "dn", "sgu", "sdn", "dvec", "lnw", "fflnw",
          "wq", "wk", "wv", "wo", "wg", "w1", "w3", "w2", "cos", "sin"]


def rope_tables():
    half = HD // 2
    inv = (np.float32(1.0) / np.float32(150000.0) ** (np.arange(half, dtype=np.float32) / np.float32(half)))
    ang = np.arange(P, dtype=np.float32)[:, None] * inv.astype(np.float32)
    c, s = np.cos(ang).astype(np.float32), np.sin(ang).astype(np.float32)
    return np.concatenate([c, c], -1), np.concatenate([-s, s], -1)


def kernel(x, fside_S2_0, ctx_2048, L0_xattn_k, L0_ffn_gate_w, L0_ffn_w_gate_up, L0_ffn_w_down,
           L0_ffn_shared_gate_up, L0_ffn_shared_down, L1_xattn_ssm_kernel, L1_xattn_D, L1_ffn_ln_w,
           L1_ffn_ff_ln_w, L1_ffn_wq, L1_ffn_wk, L1_ffn_wv, L1_ffn_wo, L1_ffn_wg, L1_ffn_w1, L1_ffn_w3,
           L1_ffn_w2):
    import concourse.bacc as bacc
    from concourse.bass_utils import run_bass_kernel_spmd

    cos, sin = rope_tables()
    kernels = np.concatenate([np.asarray(L0_xattn_k), np.asarray(L1_xattn_ssm_kernel)])
    kernels = np.concatenate([np.zeros((2 * MH, P), kernels.dtype), kernels], axis=1)
    host = [x, ctx_2048, kernels, fside_S2_0,
            np.asarray(L0_ffn_gate_w).T, L0_ffn_w_gate_up, L0_ffn_w_down, L0_ffn_shared_gate_up,
            L0_ffn_shared_down, L1_xattn_D, L1_ffn_ln_w, L1_ffn_ff_ln_w, L1_ffn_wq, L1_ffn_wk, L1_ffn_wv,
            L1_ffn_wo, L1_ffn_wg, L1_ffn_w1, L1_ffn_w3, L1_ffn_w2, cos, sin]
    nc = bacc.Bacc("TRN2", target_bir_lowering=False, num_devices=1)
    arrays, args = {}, []
    for name, a in zip(_NAMES, host):
        a = np.ascontiguousarray(a)
        arrays[f"in_{name}"] = a
        args.append(nc.dram_tensor(f"in_{name}", a.shape, mybir.dt.from_np(a.dtype), kind="ExternalInput").ap())
    out = nc.dram_tensor("out_0", (NB, P, D), F32, kind="ExternalOutput").ap()
    program(nc, *args, out)
    r = run_bass_kernel_spmd(nc, [arrays], core_ids=[0])
    return r.results[0]["out_0"]
```
